# Optimizing a Trainium2 kernel written in Bass

```python
import numpy as np
import jax
import jax.numpy as jnp

def _softmax(x, axis=-1):
    return jax.nn.softmax(x, axis=axis)
def _gelu(x):
    return jax.nn.gelu(x, approximate=True)
def _silu(x):
    return jax.nn.silu(x)
def _sigmoid(x):
    return jax.nn.sigmoid(x)
def _layernorm(x, axis=-1, eps=1e-5):
    m = jnp.mean(x, axis=axis, keepdims=True)
    v = jnp.var(x, axis=axis, keepdims=True)
    return (x - m) / jnp.sqrt(v + eps)
def _scatter_add(tgt, idx, src, axis=0):
    return tgt.at[idx].add(src)
def _segment_sum(src, seg, n):
    return jax.ops.segment_sum(src, seg, n)

kernel_name = 'mk_conv_preact_d4_conv_nchw128_493007'

def setup_inputs(seed: int = 0):
    np.random.seed(seed)
    _w = jnp.asarray
    def _rec_inputs():
        import jax
        import jax.numpy as jnp
        _gk = jax.random.key(seed)
        x = -7.109e-05 + 0.9999 * jax.random.normal(jax.random.fold_in(_gk, 1), (4, 128, 256, 256), jnp.float32)
        return x
    x = _rec_inputs()
    def _L0_conv_setup():
        import jax, jax.numpy as jnp
        import numpy as np
        B, CIN, COUT, NH, M1, M2, H, W = (8, 128, 128, 1, 32, 32, 256, 256)
        HC = COUT // NH
        key = jax.random.key(seed)
        k1, k2, k3 = jax.random.split(key, 3)
        x = jax.random.normal(k1, (B, CIN, H, W), jnp.float32)
        scales = jnp.asarray(0.01 * 2.0 ** np.arange(NH), jnp.float32)
        weight = jax.random.normal(k2, (NH, HC, HC, M1, M2), jnp.float32) * scales[:, None, None, None, None]
        fc_w = jax.random.normal(k3, (COUT, CIN), jnp.float32) * np.float32(np.sqrt(2.0 / (CIN + COUT)))
        fc_b = jnp.zeros((COUT,), jnp.float32)
        return {'x': x, 'weight': weight, 'fc_w': fc_w, 'fc_b': fc_b}
    _L0_conv_all = _L0_conv_setup()
    _L0_conv_in = {k: v for k, v in _L0_conv_all.items() if k in ('weight', 'fc_w', 'fc_b', )}
    del _L0_conv_all

    def _L1_conv_setup():
        import jax, jax.numpy as jnp
        import numpy as np
        B, C_IN, C_OUT, H, W = (8, 128, 128, 256, 256)
        N_HEADS = 4
        MODES_X, MODES_Y = (64, 64 // 2 + 1)
        HEAD_IN = C_IN // N_HEADS
        HEAD_OUT = C_OUT // N_HEADS
        INIT_STD = (2.0 / (C_IN + C_OUT)) ** 0.5
        key = jax.random.key(seed)
        k1, k2, k3, k4 = jax.random.split(key, 4)
        x = jax.random.normal(k1, (B, C_IN, H, W), dtype=jnp.float32)
        weight_real = INIT_STD * jax.random.normal(k2, (N_HEADS, HEAD_IN, HEAD_OUT, MODES_X, MODES_Y), dtype=jnp.float32)
        weight_imag = INIT_STD * jax.random.normal(k3, (N_HEADS, HEAD_IN, HEAD_OUT, MODES_X, MODES_Y), dtype=jnp.float32)
        bias = INIT_STD * jax.random.normal(k4, (C_OUT, 1, 1), dtype=jnp.float32)
        return {'x': x, 'weight_real': weight_real, 'weight_imag': weight_imag, 'bias': bias}
    _L1_conv_all = _L1_conv_setup()
    _L1_conv_in = {k: v for k, v in _L1_conv_all.items() if k in ('weight_real', 'weight_imag', 'bias', )}
    del _L1_conv_all

    def _L2_conv_setup():
        import jax, jax.numpy as jnp
        import numpy as np
        H, N, LMAX, KCH = (128, 64, 256, 2)

        def _ssm_kernel(A_re, A_im, C_re, C_im, log_dt, L):
            A = A_re + 1j * A_im
            C = C_re + 1j * C_im
            dt = jnp.exp(log_dt)
            dtA = dt[:, None] * A
            K = C * (jnp.exp(dtA) - 1.0) / A
            vand = jnp.exp(dtA[:, :, None] * jnp.arange(L, dtype=dtA.real.dtype))
            return 2.0 * jnp.einsum('chn,hnl->chl', K, vand).real

        def _bidir_pad(k, L_in):
            k0, k1 = (k[:1], k[1:])
            fwd = jnp.pad(k0, ((0, 0), (0, 0), (0, L_in)))
            bwd = jnp.pad(k1[..., ::-1], ((0, 0), (0, 0), (L_in, 0)))
            return fwd + bwd
        key = jax.random.key(seed)
        ks = jax.random.split(key, 8)
        B, L1, L2 = (2, 256, 256)
        u = jax.random.normal(ks[0], (B, H, L1, L2), jnp.float32)
        D = jax.random.normal(ks[1], (1, H), jnp.float32)

        def kparams(k_c, k_ci, k_dt):
            A_re = -0.5 * jnp.ones((H, N), jnp.float32)
            A_im = jnp.pi * jnp.broadcast_to(jnp.arange(N, dtype=jnp.float32), (H, N))
            C_re = jax.random.normal(k_c, (KCH, H, N), jnp.float32) * 0.5 ** 0.5
            C_im = jax.random.normal(k_ci, (KCH, H, N), jnp.float32) * 0.5 ** 0.5
            log_dt = jax.random.uniform(k_dt, (H,), jnp.float32, minval=np.log(0.001), maxval=np.log(0.1))
            return (A_re, A_im, C_re, C_im, log_dt)
        A_re0, A_im0, C_re0, C_im0, log_dt0 = kparams(ks[2], ks[3], ks[4])
        A_re1, A_im1, C_re1, C_im1, log_dt1 = kparams(ks[5], ks[6], ks[7])
        return {'u': u, 'D': D, 'A_re0': A_re0, 'A_im0': A_im0, 'C_re0': C_re0, 'C_im0': C_im0, 'log_dt0': log_dt0, 'A_re1': A_re1, 'A_im1': A_im1, 'C_re1': C_re1, 'C_im1': C_im1, 'log_dt1': log_dt1}
    _L2_conv_all = _L2_conv_setup()
    _L2_conv_in = {k: v for k, v in _L2_conv_all.items() if k in ('D', 'A_re0', 'A_im0', 'C_re0', 'C_im0', 'log_dt0', 'A_re1', 'A_im1', 'C_re1', 'C_im1', 'log_dt1', )}
    del _L2_conv_all

    def _L3_conv_setup():
        import jax, jax.numpy as jnp
        import numpy as np
        DIM = 128
        HEADS = 8
        HDIM = DIM // HEADS
        KS = 4
        START = KS // 2
        EPS = 1e-06

        def _to_seq(t, head=HEADS, d=HDIM):
            b, c, h, w = t.shape
            return t.reshape(b, head, d, h * w).transpose(0, 3, 1, 2)

        def _feature_map(t):
            return jax.nn.elu(t) + 1.0
        key = jax.random.key(seed)
        ks = jax.random.split(key, 7)
        B, H, W = (4, 256, 256)
        x = jax.random.normal(ks[0], (B, DIM, H, W), dtype=jnp.float32)
        s = 0.05
        q_w = jax.random.normal(ks[1], (DIM, DIM), dtype=jnp.float32) * s
        q_b = jax.random.normal(ks[2], (DIM,), dtype=jnp.float32) * s
        kv_w = jax.random.normal(ks[3], (2 * DIM, DIM), dtype=jnp.float32) * s
        kv_b = jax.random.normal(ks[4], (2 * DIM,), dtype=jnp.float32) * s
        proj_w = jax.random.normal(ks[5], (DIM, DIM), dtype=jnp.float32) * s
        proj_b = jax.random.normal(ks[6], (DIM,), dtype=jnp.float32) * s
        return {'x': x, 'q_w': q_w, 'q_b': q_b, 'kv_w': kv_w, 'kv_b': kv_b, 'proj_w': proj_w, 'proj_b': proj_b}
    _L3_conv_all = _L3_conv_setup()
    _L3_conv_in = {k: v for k, v in _L3_conv_all.items() if k in ('q_w', 'q_b', 'kv_w', 'kv_b', 'proj_w', 'proj_b', )}
    del _L3_conv_all

    return {
        "x": x,
        "L0_conv_weight": _L0_conv_in["weight"],
        "L0_conv_fc_w": _L0_conv_in["fc_w"],
        "L0_conv_fc_b": _L0_conv_in["fc_b"],
        "L1_conv_weight_real": _L1_conv_in["weight_real"],
        "L1_conv_weight_imag": _L1_conv_in["weight_imag"],
        "L1_conv_bias": _L1_conv_in["bias"],
        "L2_conv_D": _L2_conv_in["D"],
        "L2_conv_A_re0": _L2_conv_in["A_re0"],
        "L2_conv_A_im0": _L2_conv_in["A_im0"],
        "L2_conv_C_re0": _L2_conv_in["C_re0"],
        "L2_conv_C_im0": _L2_conv_in["C_im0"],
        "L2_conv_log_dt0": _L2_conv_in["log_dt0"],
        "L2_conv_A_re1": _L2_conv_in["A_re1"],
        "L2_conv_A_im1": _L2_conv_in["A_im1"],
        "L2_conv_C_re1": _L2_conv_in["C_re1"],
        "L2_conv_C_im1": _L2_conv_in["C_im1"],
        "L2_conv_log_dt1": _L2_conv_in["log_dt1"],
        "L3_conv_q_w": _L3_conv_in["q_w"],
        "L3_conv_q_b": _L3_conv_in["q_b"],
        "L3_conv_kv_w": _L3_conv_in["kv_w"],
        "L3_conv_kv_b": _L3_conv_in["kv_b"],
        "L3_conv_proj_w": _L3_conv_in["proj_w"],
        "L3_conv_proj_b": _L3_conv_in["proj_b"],
    }

def reference(x, L0_conv_weight, L0_conv_fc_w, L0_conv_fc_b, L1_conv_weight_real, L1_conv_weight_imag, L1_conv_bias, L2_conv_D, L2_conv_A_re0, L2_conv_A_im0, L2_conv_C_re0, L2_conv_C_im0, L2_conv_log_dt0, L2_conv_A_re1, L2_conv_A_im1, L2_conv_C_re1, L2_conv_C_im1, L2_conv_log_dt1, L3_conv_q_w, L3_conv_q_b, L3_conv_kv_w, L3_conv_kv_b, L3_conv_proj_w, L3_conv_proj_b):
    import jax
    import jax.numpy as jnp
    def _L0_conv_ref(x, weight, fc_w, fc_b):
        import jax, jax.numpy as jnp
        import numpy as np
        B, CIN, COUT, NH, M1, M2, H, W = (8, 128, 128, 1, 32, 32, 256, 256)
        HC = COUT // NH
        x_ft = jnp.fft.rfftn(x, axes=(-2, -1))
        Wf = x_ft.shape[-1]
        m1, m2 = (min(M1, H), min(M2, Wf))
        w_c = weight[..., :m1, :m2].astype(x_ft.dtype)
        blk = jnp.einsum('bimn,hiomn->bhomn', x_ft[:, :, :m1, :m2], w_c)
        blk = blk.reshape(x.shape[0], NH * HC, m1, m2)
        out_ft = jnp.zeros((x.shape[0], COUT, H, Wf), x_ft.dtype).at[:, :, :m1, :m2].set(blk)
        xr = jnp.fft.irfftn(out_ft, s=(H, W), axes=(-2, -1))
        return jnp.einsum('bchw,oc->bohw', xr, fc_w) + fc_b[None, :, None, None]

    def _L1_conv_ref(x, weight_real, weight_imag, bias):
        import jax, jax.numpy as jnp
        import numpy as np
        B, C_IN, C_OUT, H, W = (8, 128, 128, 256, 256)
        N_HEADS = 4
        MODES_X, MODES_Y = (64, 64 // 2 + 1)
        HEAD_IN = C_IN // N_HEADS
        HEAD_OUT = C_OUT // N_HEADS
        INIT_STD = (2.0 / (C_IN + C_OUT)) ** 0.5
        Bx, C, Hx, Wx = x.shape
        weight = weight_real + 1j * weight_imag
        n_heads, head_in, head_out, modes_x, modes_y = weight.shape
        x_freq = jnp.fft.rfft2(x, axes=(-2, -1))
        fH, fW = (x_freq.shape[-2], x_freq.shape[-1])
        m_x, m_y = (min(modes_x, fH), min(modes_y, fW))
        x_freq = x_freq.reshape(Bx, n_heads, head_in, fH, fW)
        active = jnp.einsum('bhiXY,hioXY->bhoXY', x_freq[:, :, :, :m_x, :m_y], weight[:, :, :, :m_x, :m_y])
        out_freq = jnp.zeros((Bx, n_heads, head_out, fH, fW), dtype=active.dtype)
        out_freq = out_freq.at[:, :, :, :m_x, :m_y].set(active)
        out_freq = out_freq.reshape(Bx, n_heads * head_out, fH, fW)
        x_out = jnp.fft.irfft2(out_freq, s=(Hx, Wx), axes=(-2, -1))
        return x_out + bias

    def _L2_conv_ref(u, D, A_re0, A_im0, C_re0, C_im0, log_dt0, A_re1, A_im1, C_re1, C_im1, log_dt1):
        import jax, jax.numpy as jnp
        import numpy as np
        H, N, LMAX, KCH = (128, 64, 256, 2)

        def _ssm_kernel(A_re, A_im, C_re, C_im, log_dt, L):
            A = A_re + 1j * A_im
            C = C_re + 1j * C_im
            dt = jnp.exp(log_dt)
            dtA = dt[:, None] * A
            K = C * (jnp.exp(dtA) - 1.0) / A
            vand = jnp.exp(dtA[:, :, None] * jnp.arange(L, dtype=dtA.real.dtype))
            return 2.0 * jnp.einsum('chn,hnl->chl', K, vand).real

        def _bidir_pad(k, L_in):
            k0, k1 = (k[:1], k[1:])
            fwd = jnp.pad(k0, ((0, 0), (0, 0), (0, L_in)))
            bwd = jnp.pad(k1[..., ::-1], ((0, 0), (0, 0), (L_in, 0)))
            return fwd + bwd
        B, _, L1, L2 = u.shape
        Lk1, Lk2 = (min(L1, LMAX), min(L2, LMAX))
        k1 = _bidir_pad(_ssm_kernel(A_re0, A_im0, C_re0, C_im0, log_dt0, Lk1), L1)
        k2 = _bidir_pad(_ssm_kernel(A_re1, A_im1, C_re1, C_im1, log_dt1, Lk2), L2)
        P1, P2 = (L1 + Lk1, L2 + Lk2)
        u_f = jnp.fft.rfftn(u, s=(P1, P2), axes=(-2, -1))
        kf1 = jnp.fft.fft(k1, n=P1, axis=-1)
        kf2 = jnp.fft.rfft(k2, n=P2, axis=-1)
        k_f = jnp.einsum('chm,chn->chmn', kf1, kf2)
        y_f = jnp.einsum('bhmn,chmn->bchmn', u_f, k_f)
        y = jnp.fft.irfftn(y_f, s=(P1, P2), axes=(-2, -1))[..., :L1, :L2]
        y = y + jnp.einsum('bhxy,ch->bchxy', u, D)
        return y.reshape(B, -1, L1, L2)

    def _L3_conv_ref(x, q_w, q_b, kv_w, kv_b, proj_w, proj_b):
        import jax, jax.numpy as jnp
        import numpy as np
        DIM = 128
        HEADS = 8
        HDIM = DIM // HEADS
        KS = 4
        START = KS // 2
        EPS = 1e-06

        def _to_seq(t, head=HEADS, d=HDIM):
            b, c, h, w = t.shape
            return t.reshape(b, head, d, h * w).transpose(0, 3, 1, 2)

        def _feature_map(t):
            return jax.nn.elu(t) + 1.0
        b, c, h, w = x.shape
        q = jnp.einsum('oc,bchw->bohw', q_w, x) + q_b[None, :, None, None]
        xs = x[:, :, START::KS, START::KS]
        kv = jnp.einsum('oc,bchw->bohw', kv_w, xs) + kv_b[None, :, None, None]
        k, v = (kv[:, :DIM], kv[:, DIM:])
        Q = _feature_map(_to_seq(q))
        K = _feature_map(_to_seq(k))
        V = _to_seq(v)
        S = V.shape[1]
        Vn = V / S
        KV = jnp.einsum('nshd,nshv->nhdv', K, Vn)
        Z = 1.0 / (jnp.einsum('nlhd,nhd->nlh', Q, K.sum(axis=1)) + EPS)
        out = jnp.einsum('nlhd,nhdv,nlh->nlhv', Q, KV, Z) * S
        out = out.transpose(0, 2, 3, 1).reshape(b, DIM, h, w)
        out = jnp.einsum('oc,bchw->bohw', proj_w, out) + proj_b[None, :, None, None]
        return out

    def _gn(v, G=32, eps=1e-5):
        B_, C_, H_, W_ = v.shape
        g = v.reshape(B_, G, C_ // G, H_, W_)
        m = jnp.mean(g, axis=(2, 3, 4), keepdims=True)
        s = jnp.var(g, axis=(2, 3, 4), keepdims=True)
        return ((g - m) / jnp.sqrt(s + eps)).reshape(v.shape)

    def _ln_c(v, eps=1e-6):
        m = jnp.mean(v, axis=1, keepdims=True)
        s = jnp.var(v, axis=1, keepdims=True)
        return (v - m) / jnp.sqrt(s + eps)

    def _ln_t(v, eps=1e-5):
        m = jnp.mean(v, axis=-1, keepdims=True)
        s = jnp.var(v, axis=-1, keepdims=True)
        return (v - m) / jnp.sqrt(s + eps)

    def _to_tokens(v):
        B_, C_, H_, W_ = v.shape
        return v.reshape(B_, C_, H_ * W_).transpose(0, 2, 1)
    def _from_tokens(t, like):
        B_, C_, H_, W_ = like.shape
        return t.transpose(0, 2, 1).reshape(B_, C_, H_, W_)

    x = x + _L0_conv_ref(_gn(x), L0_conv_weight, L0_conv_fc_w, L0_conv_fc_b)
    x = x + _L1_conv_ref(_gn(x), L1_conv_weight_real, L1_conv_weight_imag, L1_conv_bias)
    x = x + _L2_conv_ref(_gn(x), L2_conv_D, L2_conv_A_re0, L2_conv_A_im0, L2_conv_C_re0, L2_conv_C_im0, L2_conv_log_dt0, L2_conv_A_re1, L2_conv_A_im1, L2_conv_C_re1, L2_conv_C_im1, L2_conv_log_dt1)
    x = x + _L3_conv_ref(_gn(x), L3_conv_q_w, L3_conv_q_b, L3_conv_kv_w, L3_conv_kv_b, L3_conv_proj_w, L3_conv_proj_b)
    return x


_drawn_inputs = setup_inputs


def setup_inputs(seed=0):
    import zlib

    import numpy as np

    out = dict(_drawn_inputs(seed))
    spreads = {'L0_conv_fc_b': (0.0, 0.1), 'L2_conv_A_re0': (-0.5, 0.2), 'L2_conv_A_re1': (-0.5, 0.2)}
    factors = {'L3_conv_q_w': 8.0, 'L3_conv_q_b': 8.0, 'L3_conv_kv_b': 4.174}
    for name, (base, spread) in spreads.items():
        noise = np.random.default_rng([zlib.crc32(name.encode()), seed]).standard_normal(out[name].shape)
        drawn = base * np.exp(spread * noise) if base else spread * noise
        out[name] = jnp.asarray(drawn.astype(out[name].dtype))
    for name, factor in factors.items():
        out[name] = (out[name] * factor).astype(out[name].dtype)
    return out
```

```python
from contextlib import ExitStack

import numpy as np

import concourse.bass as bass
from concourse import mybir

F32 = mybir.dt.float32
ALU = mybir.AluOpType
ACT = mybir.ActivationFunctionType
AX = mybir.AxisListType

P = 128
B, C, H, W = 4, 128, 256, 256
NPIX = H * W
GROUPS = 32
PER_GROUP = C // GROUPS
GROUP_PIX = PER_GROUP * NPIX
KX, KY = 64, 33
K0 = 32
RI = 2 * KY
HT = H // P
WT = W // P
EPS_GN = 1e-5
N_SSM = 64
STEP = 16
LAGS = 2 * H
HEADS_L3 = 8
SUB, SUB0 = 4, 2
EPS_ATT = 1e-6
QUADS = C // 4
TWO_PI = 2 * np.pi
ROUND = 1.5 * 2.0 ** 23


def constants():
    h = np.arange(H)
    kx, ky = np.arange(KX), np.arange(KY)
    tx = TWO_PI * ((h[:, None] * kx[None, :]) % H) / H
    ty = TWO_PI * ((h[:, None] * ky[None, :]) % W) / W
    dft_x = np.concatenate([np.cos(tx), -np.sin(tx)], 1).reshape(HT, P, 2 * KX).transpose(1, 0, 2)
    from_re = np.concatenate([np.cos(ty), -np.sin(ty)], 1)
    from_im = np.concatenate([np.sin(ty), np.cos(ty)], 1)
    dft_y = np.stack([from_re, from_im], 1).reshape(WT, P, 2, RI).transpose(1, 0, 2, 3)
    inv_y = np.zeros((P, W))
    inv_y[:RI] = np.concatenate([np.cos(ty), -np.sin(ty)], 1).T
    inv_x = np.concatenate([np.cos(tx), -np.sin(tx)], 1).T * (2.0 / NPIX)
    c = np.arange(P)
    same_group = (c[:, None] // PER_GROUP == c[None, :] // PER_GROUP) * 1.0
    same_head = (c[:, None] // (C // HEADS_L3) == c[None, :] // (C // HEADS_L3)) * 1.0
    b = np.arange(STEP)
    fine = np.concatenate([STEP - 1 - b, b])
    coarse = STEP * np.concatenate([STEP - 1 - b, b])
    hermitian = np.ones((KX, 2, KY))
    hermitian[1:, :, 0] = 0.5
    hermitian[0, 1, 0] = 0.0
    rows = lambda a: np.broadcast_to(a.reshape(1, -1), (P, a.size))
    parts = {
        "dft_x": dft_x, "dft_y": dft_y, "inv_y": inv_y, "inv_x": inv_x, "same_group": same_group,
        "same_head": same_head, "ident": np.eye(P), "ones": np.ones((P, P)), "fine": rows(fine),
        "coarse": rows(coarse), "hermitian": rows(hermitian),
    }
    where, at = {}, 0
    for name, a in parts.items():
        n = a.reshape(P, -1).shape[1]
        where[name] = (at, n)
        at += n
    table = np.concatenate([a.reshape(P, -1) for a in parts.values()], 1).astype(np.float32)
    return np.ascontiguousarray(table), where


def chained(eng, sem, start=0):
    count = [start]

    def link(ins):
        count[0] += 1
        ins.then_inc(sem, 1)
        eng.wait_ge(sem, count[0])

    return link


AHEAD = 8
"""In the pipelined parts a counting semaphore starts at AHEAD, so that a wait for "item n minus the
buffers" is never against a value below one."""


def start(eng, *sems):
    for s in sems:
        eng.sem_inc(s, AHEAD)


def done(n):
    return n + (1 + AHEAD)


def reusable(n, buffers):
    assert buffers <= AHEAD
    return n + (1 + AHEAD - buffers)


def side_by_side(eng, turns, per_turn, steps):
    for n in range(-max(lead for lead, _ in steps), 0):
        for lead, step in steps:
            if n + lead >= 0:
                step(0, n + lead)
    with eng.Fori(0, turns - 1) as i:
        for k in range(per_turn):
            for lead, step in steps:
                step(i + (k + lead) // per_turn, (k + lead) % per_turn)
    for k in range(per_turn):
        for lead, step in steps:
            if k + lead < per_turn:
                step(turns - 1, k + lead)


def ssm_kernels(nc, sem, a, rev):
    with ExitStack() as ctx:
        def sb(name, shape):
            return ctx.enter_context(nc.sbuf_tensor(name, shape, F32))

        _, where = constants()
        f0, fn = where["fine"]
        c0, cn = where["coarse"]
        par = sb("ssm_par", [P, 7, P])
        dt_log, a_re, a_im = par[:, 0, :], par[:, 1, :], par[:, 2, :]
        c_re, c_im = par[:, 3:5, :], par[:, 5:7, :]
        fine, coarse = sb("fine", [P, 2 * STEP]), sb("coarse", [P, 2 * STEP])
        tmp = [sb(f"ssm_tmp{j}", [P, P]) for j in range(12)]
        dt, dre, dim, mag, cyc, rnd, cs, sn, er, ei, inv, q_i = tmp
        q_r = sb("ssm_qr", [P, P])
        k_re, k_im, k_t = (sb(n, [P, 2, P]) for n in ("ssm_kre", "ssm_kim", "ssm_kt"))
        big = [P, P, 2 * STEP]
        f_re, f_im, g_re, g_im, b_mag, b_cyc, b_rnd = (sb(f"ssm_big{j}", big) for j in range(7))
        p_re, p_im = sb("ssm_pre", big), sb("ssm_pim", big)
        kk = sb("ssm_kk", [2 * STEP, 2, P, 2 * STEP])
        ps = [ctx.enter_context(nc.psum_tensor(f"ssm_ps{j}", [2 * STEP, STEP, 2 * STEP], F32)) for j in range(4)]
        loaded, dve, act, put = sem("ssm_loaded"), sem("ssm_dve"), sem("ssm_act"), sem("ssm_put")
        ready, summed, kept = sem("ssm_ready"), sem("ssm_summed"), sem("ssm_kept")
        block = ctx.enter_context(nc.Block())
        n_blocks = 2 * P // STEP

        @block.sync
        def _(sp):
            sp.dma_start(fine[:], a["table"][:, f0:f0 + fn]).then_inc(loaded, 16)
            sp.dma_start(coarse[:], a["table"][:, c0:c0 + cn]).then_inc(loaded, 16)
            for axis in range(2):
                s = slice(N_SSM * axis, N_SSM * (axis + 1))
                row = a[f"log_dt{axis}"].rearrange("(o h) -> o h", o=1).broadcast_to([N_SSM, P])
                sp.dma_start(par[s, 0, :], row).then_inc(loaded, 16)
                sp.dma_start(par[s, 1, :], a[f"A_re{axis}"]).then_inc(loaded, 16)
                sp.dma_start(par[s, 2, :], a[f"A_im{axis}"]).then_inc(loaded, 16)
                sp.dma_start(par[s, 3:5, :], a[f"C_re{axis}"]).then_inc(loaded, 16)
                sp.dma_start(par[s, 5:7, :], a[f"C_im{axis}"]).then_inc(loaded, 16)
            sp.wait_ge(kept, n_blocks)
            for axis in range(2):
                for way in range(2):
                    s = slice(STEP * way, STEP * (way + 1))
                    sp.dma_start(rev[axis, :, H * way:H * (way + 1)].rearrange("h (a b) -> a h b", b=STEP),
                                 kk[s, axis, :, s]).then_inc(put, 16)
            sp.wait_ge(put, 16 * 4)

        @block.scalar
        def _(sc):
            def fn(at, out, x, func, scale=1.0):
                if at:
                    sc.wait_ge(dve, at)
                nc.scalar.activation(out, x, func, scale=scale).then_inc(act, 1)

            sc.wait_ge(loaded, 16 * 12)
            fn(0, dt[:], dt_log, ACT.Exp)
            fn(2, mag[:], dre[:], ACT.Exp)
            fn(5, sn[:], cyc[:], ACT.Sin, TWO_PI)
            fn(8, cs[:], rnd[:], ACT.Sin, TWO_PI)
            flat = lambda t: t[:].rearrange("p h j -> p (h j)")
            for at, (re, im) in ((9, (f_re, f_im)), (19, (g_re, g_im))):
                fn(at, flat(b_mag), flat(b_mag), ACT.Exp)
                fn(at + 4, flat(im), flat(b_cyc), ACT.Sin, TWO_PI)
                fn(at + 7, flat(re), flat(b_rnd), ACT.Sin, TWO_PI)
            for n in range(n_blocks):
                sc.wait_ge(summed, n + 1)
                nc.scalar.activation(kk[:, n // (P // STEP), STEP * (n % (P // STEP)):STEP * (n % (P // STEP) + 1), :],
                                     ps[n % 4][:], ACT.Copy, scale=2.0).then_inc(kept, 1)

        @block.vector
        def _(ve):
            link = chained(ve, dve)
            tt, ts = nc.vector.tensor_tensor, nc.vector.tensor_scalar
            ve.wait_ge(loaded, 16 * 12)
            ve.wait_ge(act, 1)
            link(tt(dre[:], dt[:], a_re, ALU.mult))
            link(tt(dim[:], dt[:], a_im, ALU.mult))
            link(ts(cyc[:], dim[:], 1 / TWO_PI, None, ALU.mult))
            link(ts(rnd[:], cyc[:], ROUND, ROUND, ALU.add, ALU.subtract))
            link(tt(cyc[:], cyc[:], rnd[:], ALU.subtract))
            link(ts(cs[:], cyc[:], 0.25, None, ALU.add))
            link(ts(er[:], cs[:], ROUND, ROUND, ALU.add, ALU.subtract))
            link(tt(rnd[:], cs[:], er[:], ALU.subtract))

            def cycles(table, re, im, act_at):
                j = table[:].unsqueeze(1).broadcast_to(big)
                link(tt(b_mag[:], dre[:].unsqueeze(2).broadcast_to(big), j, ALU.mult))
                link(tt(b_cyc[:], dim[:].unsqueeze(2).broadcast_to(big), j, ALU.mult))
                link(ts(b_rnd[:], b_cyc[:], 1 / TWO_PI, None, ALU.mult))
                link(ts(re[:], b_rnd[:], ROUND, ROUND, ALU.add, ALU.subtract))
                link(tt(b_cyc[:], b_rnd[:], re[:], ALU.subtract))
                link(ts(b_rnd[:], b_cyc[:], 0.25, None, ALU.add))
                link(ts(re[:], b_rnd[:], ROUND, ROUND, ALU.add, ALU.subtract))
                link(tt(b_rnd[:], b_rnd[:], re[:], ALU.subtract))
                ve.wait_ge(act, act_at)
                link(tt(re[:], re[:], b_mag[:], ALU.mult))
                link(tt(im[:], im[:], b_mag[:], ALU.mult))

            cycles(fine, f_re, f_im, 7)
            cycles(coarse, g_re, g_im, 10)
            link(tt(er[:], mag[:], cs[:], ALU.mult))
            link(ts(er[:], er[:], 1.0, None, ALU.subtract))
            link(tt(ei[:], mag[:], sn[:], ALU.mult))
            link(tt(inv[:], a_re, a_re, ALU.mult))
            link(tt(rnd[:], a_im, a_im, ALU.mult))
            link(tt(inv[:], inv[:], rnd[:], ALU.add))
            link(nc.vector.reciprocal(inv[:], inv[:]))
            link(tt(q_r[:], er[:], a_re, ALU.mult))
            link(tt(rnd[:], ei[:], a_im, ALU.mult))
            link(tt(q_r[:], q_r[:], rnd[:], ALU.add))
            link(tt(q_r[:], q_r[:], inv[:], ALU.mult))
            link(tt(q_i[:], ei[:], a_re, ALU.mult))
            link(tt(rnd[:], er[:], a_im, ALU.mult))
            link(tt(q_i[:], q_i[:], rnd[:], ALU.subtract))
            link(tt(q_i[:], q_i[:], inv[:], ALU.mult))
            two = [P, 2, P]
            qr2, qi2 = q_r[:].unsqueeze(1).broadcast_to(two), q_i[:].unsqueeze(1).broadcast_to(two)
            link(tt(k_re[:], c_re, qr2, ALU.mult))
            link(tt(k_t[:], c_im, qi2, ALU.mult))
            link(tt(k_re[:], k_re[:], k_t[:], ALU.subtract))
            link(tt(k_im[:], c_re, qi2, ALU.mult))
            link(tt(k_t[:], c_im, qr2, ALU.mult))
            link(tt(k_im[:], k_im[:], k_t[:], ALU.add))
            for way in range(2):
                s = slice(STEP * way, STEP * (way + 1))
                half = [P, P, STEP]
                kr, ki = (t[:, way, :].unsqueeze(2).broadcast_to(half) for t in (k_re, k_im))
                link(tt(p_re[:, :, s], g_re[:, :, s], kr, ALU.mult))
                link(tt(b_rnd[:, :, s], g_im[:, :, s], ki, ALU.mult))
                link(tt(p_re[:, :, s], p_re[:, :, s], b_rnd[:, :, s], ALU.subtract))
                link(tt(p_im[:, :, s], g_re[:, :, s], ki, ALU.mult))
                link(tt(b_rnd[:, :, s], g_im[:, :, s], kr, ALU.mult))
                link(tt(p_im[:, :, s], p_im[:, :, s], b_rnd[:, :, s], ALU.add))
            nc.vector.tensor_scalar(p_im[:], p_im[:], -1.0, None, ALU.mult).then_inc(ready, 1)

        @block.tensor
        def _(pe):
            pe.wait_ge(ready, 1)
            for n in range(n_blocks):
                axis, h0 = n // (P // STEP), STEP * (n % (P // STEP))
                s = slice(N_SSM * axis, N_SSM * (axis + 1))
                if n >= 4:
                    pe.wait_ge(kept, n - 3)
                for j in range(STEP):
                    nc.tensor.matmul(ps[n % 4][:, j, :], p_re[s, h0 + j, :], f_re[s, h0 + j, :], start=True, stop=False)
                    last = nc.tensor.matmul(ps[n % 4][:, j, :], p_im[s, h0 + j, :], f_im[s, h0 + j, :],
                                            start=False, stop=True)
                last.then_inc(summed, 1)


def spectrum(nc, sem, x, spec, squares, a):
    with ExitStack() as ctx:
        def sb(name, shape):
            return ctx.enter_context(nc.sbuf_tensor(name, shape, F32))

        _, where = constants()
        (x0, xn), (y0, yn) = where["dft_x"], where["dft_y"]
        NX = 4
        quads = [sb(f"quad{j}", [P, HT, 4, P]) for j in range(NX)]
        half = sb("half", [P, C, 2 * KX])
        dft_x = sb("dft_x", [P, HT, 2 * KX])
        dft_y = sb("dft_y", [P, WT, 2, RI])
        junk = [sb(f"square_junk{j}", [P, HT * 4 * P]) for j in range(2)]
        sums = sb("square_sums", [P, NX])
        ps1 = [ctx.enter_context(nc.psum_tensor(f"half_ps{j}", [P, 4, 2 * KX], F32)) for j in range(4)]
        ps2 = [ctx.enter_context(nc.psum_tensor(f"spec_ps{j}", [P, 4, RI], F32)) for j in range(4)]
        tables, loaded = sem("dft_tables"), [sem(f"quad_loaded{j}") for j in range(NX)]
        halved, half_kept, squared = sem("halved"), sem("half_kept"), sem("squared")
        modes, modes_kept, sums_kept = sem("modes"), sem("modes_kept"), sem("sums_kept")
        block = ctx.enter_context(nc.Block())
        turns = QUADS // NX
        kgroups = KX // 4

        def quad_of(b, wt, i, j):
            return (b * WT + wt) * QUADS + i * NX + j

        @block.sync
        def _(sp):
            sp.dma_start(dft_x[:], a["table"][:, x0:x0 + xn].rearrange("p (t k) -> p t k", t=HT)).then_inc(tables, 16)
            sp.dma_start(dft_y[:], a["table"][:, y0:y0 + yn].rearrange("p (t i k) -> p t i k", t=WT, i=2))\
                .then_inc(tables, 16)
            with sp.Fori(0, B) as b:
                for wt in range(WT):
                    with sp.Fori(0, turns) as i:
                        for j in range(NX):
                            sp.wait_ge(halved, reusable(quad_of(b, wt, i, j), NX))
                            sp.wait_ge(squared, reusable(quad_of(b, wt, i, j), NX))
                            for t in range(HT):
                                src = x[bass.ds(b, 1), bass.ds(i * (4 * NX) + 4 * j, 4), P * t:P * (t + 1),
                                        P * wt:P * (wt + 1)]
                                sp.dma_start(quads[j][:, t], src.rearrange("o c h w -> h (o c) w"))\
                                    .then_inc(loaded[j], 16)

        @block.tensor
        def _(pe):
            start(pe, halved, modes)
            pe.wait_ge(tables, 32)
            with pe.Fori(0, B) as b:
                for wt in range(WT):
                    with pe.Fori(0, turns) as i:
                        for j in range(NX):
                            pe.wait_ge(loaded[j], ((b * WT + wt) * turns + i) * (16 * HT) + 16 * HT)
                            pe.wait_ge(half_kept, reusable(quad_of(b, wt, i, j), 4))
                            for c in range(4):
                                for t in range(HT):
                                    last = nc.tensor.matmul(ps1[j][:, c, :], quads[j][:, t, c, :], dft_x[:, t, :],
                                                            start=t == 0, stop=t == HT - 1)
                            last.then_inc(halved, 1)
                    pe.wait_ge(half_kept, done(quad_of(b, wt, 0, QUADS - 1)))
                    for g in range(kgroups):
                        pe.wait_ge(modes_kept, reusable((b * WT + wt) * kgroups + g, 4))
                        for k in range(4):
                            for ri in range(2):
                                last = nc.tensor.matmul(ps2[g % 4][:, k, :], half[:, :, KX * ri + 4 * g + k],
                                                        dft_y[:, wt, ri, :], start=ri == 0, stop=ri == 1)
                        last.then_inc(modes, 1)

        @block.scalar
        def _(sc):
            start(sc, half_kept)
            with sc.Fori(0, B) as b:
                for wt in range(WT):
                    sc.wait_ge(modes, reusable((b * WT + wt) * kgroups, 1))
                    with sc.Fori(0, turns) as i:
                        for j in range(NX):
                            sc.wait_ge(halved, done(quad_of(b, wt, i, j)))
                            nc.scalar.activation(half[:, bass.ds(i * (4 * NX) + 4 * j, 4), :], ps1[j][:], ACT.Copy)\
                                .then_inc(half_kept, 1)

        @block.vector
        def _(ve):
            start(ve, squared, modes_kept)
            with ve.Fori(0, B) as b:
                for wt in range(WT):
                    with ve.Fori(0, turns) as i:
                        for j in range(NX):
                            q = quads[j][:].rearrange("p t c w -> p (t c w)")
                            ve.wait_ge(loaded[j], ((b * WT + wt) * turns + i) * (16 * HT) + 16 * HT)
                            ve.wait_ge(squared, reusable(quad_of(b, wt, i, j), 2))
                            nc.vector.tensor_tensor_reduce(junk[j % 2][:], q, q, 1.0, 0.0, ALU.mult, ALU.add,
                                                           sums[:, j:j + 1]).then_inc(squared, 1)
                        ve.wait_ge(squared, done(quad_of(b, wt, i, NX - 1)))
                        nc.vector.tensor_scalar(
                            squares[:, bass.ds(b, 1), wt, bass.ds(i * NX, NX)].rearrange("p o g -> p (o g)"), sums[:],
                            1.0, None, ALU.mult).then_inc(sums_kept, 1)
                        ve.wait_ge(sums_kept, (b * WT + wt) * turns + i + 1)
                    for g in range(kgroups):
                        ve.wait_ge(modes, done((b * WT + wt) * kgroups + g))
                        out = spec[:, bass.ds(b, 1), 4 * g:4 * g + 4, :].rearrange("p o k r -> p (o k) r")
                        if wt == 0:
                            nc.vector.tensor_scalar(out, ps2[g % 4][:], 1.0, None, ALU.mult).then_inc(modes_kept, 1)
                        else:
                            ve.wait_ge(modes_kept, reusable((b * WT + wt) * kgroups + g, 4))
                            nc.vector.tensor_tensor(out, ps2[g % 4][:], out, ALU.add).then_inc(modes_kept, 1)


def norm_moments(nc, sem, name, products, before, after, small, scale=1.0 / NPIX):
    with ExitStack() as ctx:
        ps = ctx.enter_context(nc.psum_tensor(f"{name}_ps", [P, 2, B], F32))
        steps, summed, rooted, var_ready, pair_ready = (sem(f"{name}_{n}") for n in ("steps", "summed", "rooted", "var", "pair"))
        block = ctx.enter_context(nc.Block())

        @block.vector
        def _(ve):
            link = chained(ve, steps)
            tt, ts = nc.vector.tensor_tensor, nc.vector.tensor_scalar
            before(link)
            nc.vector.memset(small["u"], 0.0).then_inc(pair_ready, 1)
            ve.wait_ge(summed, 1)
            link(nc.vector.scalar_tensor_tensor(out=small["q"], in0=ps[:, 0, :], scalar=scale, in1=small["q"],
                                                op0=ALU.mult, op1=ALU.add))
            link(ts(small["mean"], ps[:, 1, :], 1.0 / GROUP_PIX, None, ALU.mult))
            link(tt(small["t"], small["mean"], small["mean"], ALU.mult))
            link(nc.vector.scalar_tensor_tensor(out=small["q"], in0=small["t"], scalar=-float(GROUP_PIX), in1=small["q"],
                                                op0=ALU.mult, op1=ALU.add))
            ts(small["t"], small["q"], 1.0 / GROUP_PIX, EPS_GN, ALU.mult, ALU.add).then_inc(var_ready, 1)
            ve.wait_ge(rooted, 1)
            link(nc.vector.reciprocal(small["inv"], small["u"]))
            after(link)

        @block.scalar
        def _(sc):
            sc.wait_ge(var_ready, 1)
            nc.scalar.activation(small["u"], small["t"], ACT.Sqrt).then_inc(rooted, 1)

        @block.tensor
        def _(pe):
            pe.wait_ge(pair_ready, 1)
            products(ps).then_inc(summed, 1)


def window_energy(nc, sem, name, spec, out):
    with ExitStack() as ctx:
        junk = [ctx.enter_context(nc.sbuf_tensor(f"{name}_junk{j}", [P, KX * RI], F32)) for j in range(2)]
        squared, squared_ve = sem(f"{name}_squared"), sem(f"{name}_squared_ve")
        block = ctx.enter_context(nc.Block())

        @block.scalar
        def _(sc):
            for b in (0, 2):
                nc.scalar.activation(junk[0][:], spec[:, b].rearrange("p k r -> p (k r)"), ACT.Square,
                                     accum_out=out[:, b:b + 1]).then_inc(squared, 1)
                sc.wait_ge(squared, b // 2 + 1)

        @block.vector
        def _(ve):
            for b in (1, 3):
                x = spec[:, b].rearrange("p k r -> p (k r)")
                nc.vector.tensor_tensor_reduce(junk[1][:], x, x, 1.0, 0.0, ALU.mult, ALU.add, out[:, b:b + 1])\
                    .then_inc(squared_ve, 1)
                ve.wait_ge(squared_ve, b // 2 + 1)


def low_part(spec, b):
    return spec[:, b, 0:K0, :].rearrange("p k (r y) -> p k r y", r=2)[:, :, :, 0:K0]


def layer0_products(nc, sem, a, low, fc_w, herm):
    with ExitStack() as ctx:
        ROWS = 4
        w0 = [ctx.enter_context(nc.sbuf_tensor(f"w0_row{j}", [P, K0, P], F32)) for j in range(ROWS)]
        ps = [ctx.enter_context(nc.psum_tensor(f"mix0_ps{j}", [P, B, 2, K0], F32)) for j in range(4)]
        ps_fc = [ctx.enter_context(nc.psum_tensor(f"fc_ps{j}", [P, 8, 2, K0], F32)) for j in range(4)]
        loaded = [sem(f"w0_loaded{j}") for j in range(ROWS)]
        mixed, kept, projected, fc_kept = sem("mix0_mixed"), sem("mix0_kept"), sem("fc_projected"), sem("fc_kept")
        block = ctx.enter_context(nc.Block())
        n_fc = B * K0 // 8

        @block.sync
        def _(sp):
            with sp.Fori(0, K0 // ROWS) as i:
                for j in range(ROWS):
                    sp.wait_ge(mixed, reusable(i * ROWS + j, ROWS))
                    src = a["w0"][bass.ds(i * ROWS + j, 1)].rearrange("m c n o -> c (m n) o")
                    sp.dma_start(w0[j][:], src).then_inc(loaded[j], 16)

        @block.tensor
        def _(pe):
            start(pe, mixed)
            with pe.Fori(0, K0 // ROWS) as i:
                for j in range(ROWS):
                    pe.wait_ge(loaded[j], i * 16 + 16)
                    pe.wait_ge(kept, reusable(i * ROWS + j, 4))
                    for n in range(K0):
                        rhs = low[:, :, bass.ds(i * ROWS + j, 1), :, n].rearrange("p b o r -> p b (o r)")
                        last = nc.tensor.matmul(ps[j][:, :, :, n], w0[j][:, n, :], rhs, start=True, stop=True)
                    last.then_inc(mixed, 1)
            pe.wait_ge(kept, done(K0 - 1))
            for n in range(n_fc):
                if n >= 4:
                    pe.wait_ge(fc_kept, n - 3)
                rhs = low[:, n // 4, 8 * (n % 4):8 * (n % 4) + 8].rearrange("p k r y -> p (k r y)")
                nc.tensor.matmul(ps_fc[n % 4][:].rearrange("p k r y -> p (k r y)"), fc_w[:], rhs, start=True, stop=True)\
                    .then_inc(projected, 1)

        @block.vector
        def _(ve):
            start(ve, kept)
            with ve.Fori(0, K0 // ROWS) as i:
                for j in range(ROWS):
                    ve.wait_ge(mixed, done(i * ROWS + j))
                    out = low[:, :, bass.ds(i * ROWS + j, 1), :, :].rearrange("p b o r y -> p b (o r y)")
                    nc.vector.tensor_scalar(out, ps[j][:].rearrange("p b r y -> p b (r y)"), 1.0, None, ALU.mult)\
                        .then_inc(kept, 1)
            for n in range(n_fc):
                k = slice(8 * (n % 4), 8 * (n % 4) + 8)
                ve.wait_ge(projected, n + 1)
                nc.vector.tensor_tensor(low[:, n // 4, k], ps_fc[n % 4][:], herm[:, k, :, 0:K0], ALU.mult)\
                    .then_inc(fc_kept, 1)


def layer1_products(nc, sem, a, spec, inv, neg_inv, herm, change):
    with ExitStack() as ctx:
        def sb(name, shape):
            return ctx.enter_context(nc.sbuf_tensor(name, shape, F32))

        ROWS, HC = 2, C // 4
        w = [[sb(f"w1_row{j}{r}", [P, P, KY]) for r in "ri"] for j in range(ROWS)]
        scaled = [sb(f"scaled{j}", [P, B, 3, KY]) for j in range(ROWS)]
        added = [sb(f"added{j}", [P, B, RI]) for j in range(ROWS)]
        twice = [sb(f"twice{j}", [P, B, RI]) for j in range(ROWS)]
        ps = [ctx.enter_context(nc.psum_tensor(f"mix1_ps{j}", [P, B, 2, KY], F32)) for j in range(ROWS)]
        loaded = [[sem(f"w1_loaded{j}{r}") for r in "ri"] for j in range(ROWS)]
        zeroed, staged, mixed, steps = sem("w1_zeroed"), sem("mix1_staged"), sem("mix1_mixed"), sem("mix1_steps")
        block = ctx.enter_context(nc.Block())
        STEPS = 5

        @block.gpsimd
        def _(po):
            for j in range(ROWS):
                for r in range(2):
                    nc.gpsimd.memset(w[j][r][:], 0.0).then_inc(zeroed, 1)

        @block.sync
        def _(sp):
            sp.wait_ge(zeroed, 2 * ROWS)
            with sp.Fori(0, KX // ROWS) as i:
                for j in range(ROWS):
                    sp.wait_ge(mixed, reusable(i * ROWS + j, ROWS))
                    for r in range(2):
                        for h in range(4):
                            s = slice(HC * h, HC * (h + 1))
                            src = a["w1_im" if r else "w1_re"][bass.ds(i * ROWS + j, 1), s].rearrange("x i o y -> (x i) o y")
                            sp.dma_start(w[j][r][s, s, :], src).then_inc(loaded[j][r], 16)

        @block.tensor
        def _(pe):
            start(pe, mixed)
            with pe.Fori(0, KX // ROWS) as i:
                for j in range(ROWS):
                    for r in range(2):
                        pe.wait_ge(loaded[j][r], i * 64 + 64)
                    pe.wait_ge(staged, done(i * ROWS + j))
                    for n in range(KY):
                        out = ps[j][:, :, :, n]
                        nc.tensor.matmul(out, w[j][0][:, :, n], scaled[j][:, :, 1:3, n], start=True, stop=False)
                        last = nc.tensor.matmul(out, w[j][1][:, :, n], scaled[j][:, :, 0:2, n], start=False, stop=True)
                    last.then_inc(mixed, 1)

        @block.vector
        def _(ve):
            tt = nc.vector.tensor_tensor
            wide = [P, B, RI]

            def row_of(k):
                return spec[:, :, bass.ds(k, 1), :].rearrange("p b o r -> p b (o r)")

            def stage(k, j):
                ve.wait_ge(mixed, reusable(k, ROWS))
                tt(scaled[j][:, :, 1:3, :].rearrange("p b r y -> p b (r y)"), row_of(k),
                   inv.unsqueeze(2).broadcast_to(wide), ALU.mult)
                tt(scaled[j][:, :, 0, :], row_of(k)[:, :, KY:RI], neg_inv.unsqueeze(2).broadcast_to([P, B, KY]), ALU.mult)\
                    .then_inc(staged, 1)

            def finish(k, j):
                def link(ins, n):
                    ins.then_inc(steps, 1)
                    ve.wait_ge(steps, k * STEPS + n)

                ve.wait_ge(mixed, done(k))
                mask = herm[:, bass.ds(k, 1), :, :].rearrange("p o r y -> p o (r y)").broadcast_to(wide)
                link(tt(added[j][:], ps[j][:].rearrange("p b r y -> p b (r y)"), mask, ALU.mult), 1)
                link(nc.vector.scalar_tensor_tensor(out=twice[j][:], in0=row_of(k), scalar=2.0, in1=added[j][:],
                                                    op0=ALU.mult, op1=ALU.add), 2)
                link(tt(twice[j][:], twice[j][:], added[j][:], ALU.mult), 3)
                link(nc.vector.tensor_reduce(change[:, :, bass.ds(k, 1)], twice[j][:], AX.X, ALU.add), 4)
                link(nc.vector.tensor_scalar(row_of(k), added[j][:], 1.0, None, ALU.mult), 5)

            start(ve, staged)
            for j in range(ROWS):
                stage(j, j)
            with ve.Fori(0, KX // ROWS - 1) as i:
                for j in range(ROWS):
                    finish(i * ROWS + j, j)
                    stage(i * ROWS + j + ROWS, j)
            for j in range(ROWS):
                finish(KX - ROWS + j, j)


def modes_layers(nc, sem, a, spec, squares, small_rows):
    with ExitStack() as ctx:
        def sb(name, shape):
            return ctx.enter_context(nc.sbuf_tensor(name, shape, F32))

        _, where = constants()
        group, ones = sb("same_group", [P, P]), sb("mix_ones", [P, 2])
        herm = sb("hermitian", [P, KX, 2, KY])
        fc_w, bias = sb("fc_w", [P, P]), sb("mode_biases", [P, 3])
        low = sb("low_modes", [P, B, K0, 2, K0])
        change = sb("energy_change", [P, B, KX])
        by_channel = sb("squares_by_channel", [P, B, WT, GROUPS, PER_GROUP])
        names = ("q", "t", "u", "mean", "before", "after", "dc", "added_dc", "bias_dc", "neg_inv", "e0")
        rows = sb("mix_small", [P, len(names), B])
        pair = sb("mix_pair", [P, 2, B])
        small = {n: rows[:, j, :] for j, n in enumerate(names)} | small_rows
        spec_dc = spec[:, :, 0, 0]
        loaded, added0 = sem("mode_tables"), sem("layer0_added")

        def table(name):
            at, n = where[name]
            return a["table"][:, at:at + n]

        with nc.Block() as block:
            @block.sync
            def _(sp):
                sp.dma_start(group[:], table("same_group")).then_inc(loaded, 16)
                sp.dma_start(ones[:], table("ones")[:, 0:2]).then_inc(loaded, 16)
                sp.dma_start(herm[:], table("hermitian").rearrange("p (k r y) -> p k r y", k=KX, r=2)).then_inc(loaded, 16)
                sp.dma_start(fc_w[:], a["fc_wT"]).then_inc(loaded, 16)
                sp.dma_start(bias[:, 0:1], a["fc_b"].rearrange("(c o) -> c o", o=1)).then_inc(loaded, 16)
                sp.dma_start(bias[:, 1:2], a["bias1"].rearrange("c o t -> c (o t)")).then_inc(loaded, 16)
                sp.dma_start(bias[:, 2:3], a["D"].rearrange("o c -> c o")).then_inc(loaded, 16)
                sp.wait_ge(loaded, 16 * 7)

        tt, ts, stt = nc.vector.tensor_tensor, nc.vector.tensor_scalar, nc.vector.scalar_tensor_tensor

        def shift(link):
            link(stt(out=spec_dc, in0=small["mean"], scalar=-float(NPIX), in1=spec_dc, op0=ALU.mult, op1=ALU.add))
            link(tt(small["sum"], small["sum"], small["mean"], ALU.add))

        def products0(ps):
            for b in range(B):
                for t in range(WT):
                    nc.tensor.matmul(ps[:, 0, b:b + 1], by_channel[:, b, t, :, :].rearrange("p g n -> p (g n)"), ones[:, 0:1], start=t == 0, stop=t == WT - 1)
            return nc.tensor.matmul(ps[:, 1, :], group[:], pair[:, 1, :], start=True, stop=True)

        def before0(link):
            for b in range(B):
                link(nc.vector.tensor_copy(by_channel[:, b],
                                           squares[:, b].unsqueeze(3).broadcast_to([P, WT, GROUPS, PER_GROUP])))
            link(nc.vector.memset(small["q"], 0.0))
            link(nc.vector.memset(small["sum"], 0.0))
            link(nc.vector.tensor_copy(pair[:, 1, :], spec_dc))
            link(ts(small["bias_dc"], small["q"], bias[:, 1:2], float(NPIX), ALU.add, ALU.mult))

        def after0(link):
            shift(link)
            for b in range(B):
                link(ts(low[:, b], low_part(spec, b), small["inv"][:, b:b + 1], None, ALU.mult))

        norm_moments(nc, sem, "norm0", products0, before0, after0, small, scale=1.0)
        window_energy(nc, sem, "energy0", spec, small["before"])
        layer0_products(nc, sem, a, low, fc_w, herm)

        with nc.Block() as block:
            @block.vector
            def _(ve):
                link = chained(ve, added0)
                link(tt(small["e0"], spec_dc, spec_dc, ALU.mult))
                link(ts(small["t"], small["q"], 0.0, None, ALU.mult))
                link(ts(small["t"], small["t"], bias[:, 0:1], float(NPIX), ALU.add, ALU.mult))
                link(tt(low[:, :, 0, 0, 0], low[:, :, 0, 0, 0], small["t"], ALU.add))
                for b in range(B):
                    link(tt(low_part(spec, b), low_part(spec, b), low[:, b], ALU.add))
        window_energy(nc, sem, "energy1", spec, small["after"])

        def products(ps):
            return nc.tensor.matmul(ps[:].rearrange("p t b -> p (t b)"), group[:], pair[:].rearrange("p t b -> p (t b)"),
                                    start=True, stop=True)

        def before1(link):
            e, d = pair[:, 0, :], pair[:, 1, :]
            link(tt(e, small["after"], small["before"], ALU.subtract))
            link(stt(out=e, in0=e, scalar=2.0, in1=small["e0"], op0=ALU.mult, op1=ALU.add))
            link(tt(small["t"], spec_dc, spec_dc, ALU.mult))
            link(tt(e, e, small["t"], ALU.subtract))
            link(nc.vector.tensor_copy(d, spec_dc))

        def after1(link):
            shift(link)
            link(ts(small["neg_inv"], small["inv"], -1.0, None, ALU.mult))
            link(nc.vector.tensor_copy(small["dc"], spec_dc))

        norm_moments(nc, sem, "norm1", products, before1, after1, small)
        layer1_products(nc, sem, a, spec, small["inv"], small["neg_inv"], herm, change)

        def before2(link):
            e, d = pair[:, 0, :], pair[:, 1, :]
            hd, t, u = small["added_dc"], small["t"], small["u"]
            link(nc.vector.tensor_copy(hd, spec_dc))
            link(nc.vector.tensor_reduce(e, change[:], AX.X, ALU.add))
            link(stt(out=t, in0=small["dc"], scalar=2.0, in1=hd, op0=ALU.mult, op1=ALU.add))
            link(tt(t, t, hd, ALU.mult))
            link(tt(e, e, t, ALU.subtract))
            link(tt(hd, hd, small["bias_dc"], ALU.add))
            link(stt(out=t, in0=small["dc"], scalar=2.0, in1=hd, op0=ALU.mult, op1=ALU.add))
            link(tt(t, t, hd, ALU.mult))
            link(stt(out=e, in0=e, scalar=2.0, in1=t, op0=ALU.mult, op1=ALU.add))
            link(tt(d, small["dc"], hd, ALU.add))

        def after2(link):
            for b in range(B):
                link(tt(low_part(spec, b), low_part(spec, b), low[:, b], ALU.add))
            link(tt(small["sum"], small["sum"], small["mean"], ALU.add))
            link(tt(spec_dc, spec_dc, small["bias_dc"], ALU.add))
            link(stt(out=spec_dc, in0=small["sum"], scalar=-float(NPIX), in1=spec_dc, op0=ALU.mult, op1=ALU.add))
            link(ts(small["skip"], small["inv"], bias[:, 2:3], 1.0, ALU.mult, ALU.add))
            link(ts(spec_dc, spec_dc, 0.5, None, ALU.mult))

        norm_moments(nc, sem, "norm2", products, before2, after2, small)


def modes_to_rows(nc, sem, a, spec, lhs):
    with ExitStack() as ctx:
        _, where = constants()
        i0, i_n = where["ident"]
        ident = ctx.enter_context(nc.sbuf_tensor("rows_ident", [P, P], F32))
        three = [ctx.enter_context(nc.sbuf_tensor(f"three{j}", [P, KX, 3, KY], F32)) for j in range(2)]
        rows = ctx.enter_context(nc.sbuf_tensor("mode_rows", [P, C, 2, KX], F32))
        ps = [ctx.enter_context(nc.psum_tensor(f"rows_ps{j}", [P, 4, C], F32)) for j in range(8)]
        table, made, turned = sem("ident_loaded"), sem("three_made"), sem("rows_turned")
        kept_ve, kept_sc, stored = sem("rows_kept_ve"), sem("rows_kept_sc"), sem("rows_stored")
        block = ctx.enter_context(nc.Block())
        banks = [(half, k) for half in range(2) for k in range(0, KX, 4)]
        each = len(banks) // 2

        @block.sync
        def _(sp):
            sp.dma_start(ident[:], a["table"][:, i0:i0 + i_n]).then_inc(table, 16)
            for b in range(B):
                sp.wait_ge(kept_ve, each * (b + 1))
                sp.wait_ge(kept_sc, each * (b + 1))
                sp.dma_start(lhs[:, :, b, :], rows[0:RI].rearrange("r c t k -> r c (t k)")).then_inc(stored, 16)
            sp.wait_ge(stored, 16 * B)

        @block.gpsimd
        def _(po):
            for b in range(B):
                if b >= 2:
                    po.wait_ge(turned, len(banks) * (b - 1))
                row = spec[:, b].rearrange("p k (r y) -> p k r y", r=2)
                nc.gpsimd.tensor_copy(three[b % 2][:, :, 0:2, :], row).then_inc(made, 1)
                nc.gpsimd.tensor_scalar(three[b % 2][:, :, 2, :], row[:, :, 0, :], -1.0, None, ALU.mult).then_inc(made, 1)

        @block.tensor
        def _(pe):
            pe.wait_ge(table, 16)
            for b in range(B):
                pe.wait_ge(made, 2 * (b + 1))
                for n, (half, k0) in enumerate(banks):
                    m = len(banks) * b + n
                    if m >= 8:
                        pe.wait_ge(kept_ve if m % 2 == 0 else kept_sc, (m - 8) // 2 + 1)
                    for k in range(4):
                        src = three[b % 2][:, k0 + k, half:half + 2, :].rearrange("p r y -> p (r y)")
                        last = nc.tensor.transpose(ps[m % 8][0:RI, k, :], src, ident[:])
                    last.then_inc(turned, 1)

        def keep(eng, copy, kept, odd):
            for b in range(B):
                if b:
                    eng.wait_ge(stored, 16 * b)
                for n in range(odd, len(banks), 2):
                    m = len(banks) * b + n
                    half, k0 = banks[n]
                    eng.wait_ge(turned, m + 1)
                    copy(rows[0:RI, :, half, k0:k0 + 4].rearrange("r c k -> r k c"), ps[m % 8][0:RI]).then_inc(kept, 1)

        @block.vector
        def _(ve):
            keep(ve, nc.vector.tensor_copy, kept_ve, 0)

        @block.scalar
        def _(sc):
            keep(sc, nc.scalar.copy, kept_sc, 1)


def spread(nc, sem, a, sources, outs):
    with ExitStack() as ctx:
        _, where = constants()
        tables = ctx.enter_context(nc.sbuf_tensor("spread_tables", [P, 2, P], F32))
        n_all = B * len(sources)
        diag = ctx.enter_context(nc.sbuf_tensor("spread_diag", [P, n_all, P], F32))
        ps = [ctx.enter_context(nc.psum_tensor(f"spread_ps{k}", [P, B, C], F32)) for k in range(len(sources))]
        loaded, made, summed, kept = (sem(f"spread_{n}") for n in ("loaded", "made", "summed", "kept"))
        block = ctx.enter_context(nc.Block())

        @block.sync
        def _(sp):
            for j, n in enumerate(("ident", "ones")):
                at, w = where[n]
                sp.dma_start(tables[:, j, :], a["table"][:, at:at + w]).then_inc(loaded, 16)

        @block.vector
        def _(ve):
            ve.wait_ge(loaded, 32)
            for k, s in enumerate(sources):
                for b in range(B):
                    nc.vector.tensor_scalar(diag[:, B * k + b, :], tables[:, 0, :], s[:, b:b + 1], None, ALU.mult)\
                        .then_inc(made, 1)
            for k, out in enumerate(outs):
                ve.wait_ge(summed, k + 1)
                nc.vector.tensor_copy(out, ps[k][:]).then_inc(kept, 1)

        @block.tensor
        def _(pe):
            pe.wait_ge(made, n_all)
            for k in range(len(sources)):
                for b in range(B):
                    last = nc.tensor.matmul(ps[k][:, b, :], tables[:, 1, :], diag[:, B * k + b, :], start=True, stop=True)
                last.then_inc(summed, 1)


def toeplitz_layer(nc, sem, a, x, lhs, rev, x3, inv_all, skip_all, sums):
    with ExitStack() as ctx:
        def sb(name, shape):
            return ctx.enter_context(nc.sbuf_tensor(name, shape, F32))

        def banks(name):
            return [ctx.enter_context(nc.psum_tensor(f"{name}{j}", [P, 2, W], F32)) for j in range(2)]

        _, where = constants()
        (r0, rn), (c0, cn) = where["inv_y"], where["inv_x"]
        inv_y, inv_x = sb("inv_y", [P, W]), sb("inv_x", [P, H])
        SETS, NIMG = 2, 2 * B
        TURNS = C // SETS
        xin = [sb(f"xin{j}", [P, B, HT, W]) for j in range(SETS)]
        xout = [sb(f"xout{j}", [P, B, HT, W]) for j in range(SETS)]
        toep = [sb(f"toeplitz{j}", [P, 2, LAGS - P]) for j in range(SETS)]
        modes = [sb(f"channel_modes{j}", [P, B, 2 * KX]) for j in range(SETS)]
        rows = [sb(f"rows{j}", [P, W]) for j in range(2)]
        v = [sb(f"v{j}", [P, HT, W]) for j in range(4)]
        mid = [sb(f"mid{j}", [P, WT, H]) for j in range(2)]
        junk = [sb(f"conv_junk{j}", [P, HT * W]) for j in range(2)]
        acc = sb("conv_acc", [P, 2, NIMG])
        ps_r, ps_f, ps_m, ps_y = (banks(n) for n in ("rows_ps_", "field_ps", "mid_ps", "y_ps"))
        tables = sem("inv_tables")
        modes_in, x_in, toep_in, stored = (
            [sem(f"{n}{j}") for j in range(SETS)] for n in ("modes_in", "x_in", "toep_in", "x3_stored"))
        xout_free = sem("xout_free")
        rows_made, rows_kept, field_made, v_kept, first, mid_kept, second, x3_kept, squared, sums_kept = (
            sem(n) for n in ("rows_made", "rows_kept", "field_made", "v_kept", "toeplitz1", "mid_kept",
                             "toeplitz2", "x3_kept", "x3_squared", "x3_sums_kept"))
        block = ctx.enter_context(nc.Block())
        hankel = bass.AP(rev.tensor, rev.offset, [[C * LAGS, 2], [LAGS, C], [1, P], [1, LAGS - P]])

        def matrix_rows(j, axis, t):
            lo = P * t
            back = toep[j][:, axis, lo:lo + H]
            return back[:, ::-1]

        def image(i, k):
            return i * NIMG + k

        @block.sync
        def _(sp):
            sp.dma_start(inv_y[:], a["table"][:, r0:r0 + rn]).then_inc(tables, 16)
            sp.dma_start(inv_x[:], a["table"][:, c0:c0 + cn]).then_inc(tables, 16)
            with sp.Fori(0, TURNS) as i:
                for j in range(SETS):
                    ch, last = i * SETS + j, image(i, B * j + B - 1)
                    sp.wait_ge(rows_made, reusable(last, NIMG))
                    sp.dma_start(modes[j][0:RI], lhs[:, bass.ds(ch, 1)].rearrange("r o b k -> r (o b) k"))\
                        .then_inc(modes_in[j], 16)
                    sp.wait_ge(v_kept, reusable(last, NIMG))
                    for b in range(B):
                        src = x[b, bass.ds(ch, 1)].rearrange("o (t p) w -> p (o t) w", p=P)
                        sp.dma_start(xin[j][:, b], src).then_inc(x_in[j], 16)
                    sp.wait_ge(second, reusable(last, NIMG))
                    for axis in range(2):
                        sp.dma_start(toep[j][:, axis, :], hankel[axis, bass.ds(ch, 1)].rearrange("o p j -> p (o j)"))\
                            .then_inc(toep_in[j], 16)

        @block.gpsimd
        def _(po):
            start(po, xout_free)
            with po.Fori(0, TURNS) as i:
                for j in range(SETS):
                    po.wait_ge(x3_kept, done(image(i, B * j + B - 1)))
                    dst = x3[:, bass.ds(i * SETS + j, 1)].rearrange("b o (t p) w -> p b (o t) w", p=P)
                    for b in range(B):
                        po.dma_start(dst[:, b], xout[j][:, b]).then_inc(stored[j], 16)
                    po.wait_ge(stored[j], i * (16 * B) + 16 * B)
                    po.sem_inc(xout_free, 1)

        @block.tensor
        def _(pe):
            start(pe, rows_made, field_made, first, second)
            pe.wait_ge(tables, 32)

            def modes_by_ky(i, k):
                j, b, n = k // B, k % B, image(i, k)
                if b == 0:
                    pe.wait_ge(modes_in[j], i * 16 + 16)
                pe.wait_ge(rows_kept, reusable(n, 2))
                nc.tensor.matmul(ps_r[k % 2][:, 0, :], modes[j][0:RI, b, :], inv_y[0:RI, :], start=True, stop=True)\
                    .then_inc(rows_made, 1)

            def modes_by_kx(i, k):
                n = image(i, k)
                pe.wait_ge(rows_kept, done(n))
                pe.wait_ge(v_kept, reusable(n, 2))
                for t in range(HT):
                    last = nc.tensor.matmul(ps_f[k % 2][:, t, :], inv_x[:, P * t:P * (t + 1)], rows[k % 2][:],
                                            start=True, stop=True)
                last.then_inc(field_made, 1)

            def along_h(i, k):
                j, n = k // B, image(i, k)
                if k % B == 0:
                    pe.wait_ge(toep_in[j], i * 32 + 32)
                pe.wait_ge(v_kept, done(n))
                pe.wait_ge(mid_kept, reusable(n, 2))
                for m in range(WT):
                    for t in range(HT):
                        last = nc.tensor.matmul(ps_m[k % 2][:, m, :], v[k % 4][:, t, P * m:P * (m + 1)],
                                                matrix_rows(j, 0, t), start=t == 0, stop=t == HT - 1)
                last.then_inc(first, 1)

            def along_w(i, k):
                j, n = k // B, image(i, k)
                pe.wait_ge(mid_kept, done(n))
                pe.wait_ge(x3_kept, reusable(n, 2))
                for m in range(HT):
                    for t in range(WT):
                        last = nc.tensor.matmul(ps_y[k % 2][:, m, :], mid[k % 2][:, t, P * m:P * (m + 1)],
                                                matrix_rows(j, 1, t), start=t == 0, stop=t == WT - 1)
                last.then_inc(second, 1)

            side_by_side(pe, TURNS, NIMG, [(3, modes_by_ky), (2, modes_by_kx), (1, along_h), (0, along_w)])

        @block.scalar
        def _(sc):
            start(sc, rows_kept, mid_kept, squared)

            def keep_rows(i, k):
                n = image(i, k)
                sc.wait_ge(rows_made, done(n))
                sc.wait_ge(field_made, reusable(n, 2))
                nc.scalar.copy(rows[k % 2][:], ps_r[k % 2][:, 0, :]).then_inc(rows_kept, 1)

            def keep_mid(i, k):
                n = image(i, k)
                sc.wait_ge(first, done(n))
                sc.wait_ge(second, reusable(n, 2))
                scale = inv_all[:, k % B, bass.ds(i * SETS + k // B, 1)]
                nc.scalar.activation(mid[k % 2][:], ps_m[k % 2][:], ACT.Copy, scale=scale).then_inc(mid_kept, 1)

            def square(i, k):
                n = image(i, k)
                sc.wait_ge(x3_kept, done(n))
                sc.wait_ge(squared, reusable(n, 2))
                sc.wait_ge(sums_kept, reusable(i * SETS + k // B, SETS))
                nc.scalar.activation(junk[k % 2][:], xout[k // B][:, k % B].rearrange("p t w -> p (t w)"), ACT.Square,
                                     accum_out=acc[:, 1, k:k + 1]).then_inc(squared, 1)

            side_by_side(sc, TURNS, NIMG, [(3, keep_rows), (1, keep_mid), (0, square)])

        @block.vector
        def _(ve):
            start(ve, v_kept, x3_kept, sums_kept)

            def add_field(i, k):
                j, b, n = k // B, k % B, image(i, k)
                if b == 0:
                    ve.wait_ge(x_in[j], i * (16 * B) + 16 * B)
                ve.wait_ge(field_made, done(n))
                ve.wait_ge(x3_kept, reusable(n, 4))
                nc.vector.tensor_tensor(v[k % 4][:], ps_f[k % 2][:], xin[j][:, b], ALU.add).then_inc(v_kept, 1)

            def add_up(i, k):
                j, b, n = k // B, k % B, image(i, k)
                if b == 0:
                    ve.wait_ge(xout_free, reusable(i * SETS + j, SETS))
                ve.wait_ge(second, done(n))
                ve.wait_ge(sums_kept, reusable(i * SETS + j, SETS))
                ve.wait_ge(v_kept, done(n))
                nc.vector.scalar_tensor_tensor(out=xout[j][:, b], in0=v[k % 4][:],
                                               scalar=skip_all[:, b, bass.ds(i * SETS + j, 1)], in1=ps_y[k % 2][:],
                                               op0=ALU.mult, op1=ALU.add, accum_out=acc[:, 0, k:k + 1])\
                    .then_inc(x3_kept, 1)
                if b == B - 1:
                    ve.wait_ge(x3_kept, done(n))
                    ve.wait_ge(squared, done(n))
                    nc.vector.tensor_scalar(sums[:, :, :, bass.ds(i * SETS + j, 1)].rearrange("p s b o -> p s (b o)"),
                                            acc[:, :, B * j:B * (j + 1)], 1.0, None, ALU.mult).then_inc(sums_kept, 1)

            side_by_side(ve, TURNS, NIMG, [(2, add_field), (0, add_up)])


def attention_matrices(nc, sem, a, x3, sums, mean_sum, w_q, w_den, w_out, biases):
    with ExitStack() as ctx:
        def sb(name, shape):
            return ctx.enter_context(nc.sbuf_tensor(name, shape, F32))

        _, where = constants()
        masks = sb("att_tables", [P, 2, P])
        weights = sb("att_weights", [P, 4, C])
        vectors = sb("att_vectors", [P, 2])
        kv_row = sb("kv_b_row", [1, 2 * C])
        w_kv, kv_bias = sb("w_kv", [P, B, 2 * C]), sb("kv_bias", [P, B, 2 * C])
        beta_wide = sb("beta_wide", [P, B, P])
        by_group = sb("sums_by_group", [P, 2 * B, GROUPS])
        by_channel = sb("sums_by_channel", [P, 2 * B, GROUPS, PER_GROUP])
        names = ("q", "t", "u", "mean", "inv", "beta")
        rows = sb("att_small", [P, len(names), B])
        small = {n: rows[:, j, :] for j, n in enumerate(names)}
        loaded, summed, kept = (sem(f"att_{n}") for n in ("tables_in", "bias_summed", "bias_kept"))
        ts, tt = nc.vector.tensor_scalar, nc.vector.tensor_tensor
        same_head, ones = masks[:, 0, :], masks[:, 1, :]
        kv_w = weights[:, 1:3, :].rearrange("c t o -> c (t o)")

        with nc.Block() as block:
            @block.sync
            def _(sp):
                for j, n in enumerate(("same_head", "ones")):
                    at, w = where[n]
                    sp.dma_start(masks[:, j, :], a["table"][:, at:at + w]).then_inc(loaded, 16)
                sp.dma_start(weights[:, 0, :], a["q_wT"]).then_inc(loaded, 16)
                sp.dma_start(kv_w, a["kv_wT"]).then_inc(loaded, 16)
                sp.dma_start(weights[:, 3, :], a["proj_wT"]).then_inc(loaded, 16)
                sp.dma_start(vectors[:, 0:1], a["q_b"].rearrange("(c o) -> c o", o=1)).then_inc(loaded, 16)
                sp.dma_start(vectors[:, 1:2], a["proj_b"].rearrange("(c o) -> c o", o=1)).then_inc(loaded, 16)
                sp.dma_start(kv_row[:], a["kv_b"].rearrange("(p o) -> p o", p=1)).then_inc(loaded, 16)
                sp.wait_ge(loaded, 16 * 8)

        def products(ps):
            for s, row in ((1, 0), (0, 1)):
                for b in range(B):
                    last = nc.tensor.matmul(ps[:, row, b:b + 1],
                                            by_channel[:, B * s + b, :, :].rearrange("p g n -> p (g n)"), ones[:, 0:1],
                                            start=True, stop=True)
            return last

        def before(link):
            link(nc.vector.tensor_reduce(by_group[:], sums[:].rearrange("p s b (g n) -> p (s b) g n", n=PER_GROUP),
                                         AX.X, ALU.add))
            link(nc.vector.tensor_copy(by_channel[:], by_group[:].unsqueeze(3).broadcast_to([P, 2 * B, GROUPS, PER_GROUP])))
            link(nc.vector.memset(small["q"], 0.0))

        def after(link):
            link(nc.vector.scalar_tensor_tensor(out=small["beta"], in0=small["mean"], scalar=-1.0, in1=small["inv"],
                                                op0=ALU.mult, op1=ALU.mult))
            link(nc.vector.tensor_copy(beta_wide[:], small["beta"].unsqueeze(2).broadcast_to([P, B, P])))
            for b in range(B):
                link(ts(w_q[:, b, :], weights[:, 0, :], small["inv"][:, b:b + 1], None, ALU.mult))
                link(ts(w_kv[:, b, :], kv_w, small["inv"][:, b:b + 1], None, ALU.mult))
            link(ts(biases[:, 1, :], mean_sum, vectors[:, 1:2], None, ALU.add))

        norm_moments(nc, sem, "norm3", products, before, after, small, scale=1.0)

        with ExitStack() as scope:
            ps_q = scope.enter_context(nc.psum_tensor("q_bias_ps", [P, B], F32))
            ps_kv = [scope.enter_context(nc.psum_tensor(f"kv_bias_ps{j}", [P, 2 * C], F32)) for j in range(2)]
            block = scope.enter_context(nc.Block())

            @block.tensor
            def _(pe):
                nc.tensor.matmul(ps_q[:], weights[:, 0, :], small["beta"], start=True, stop=True).then_inc(summed, 1)
                for b in range(B):
                    if b >= 2:
                        pe.wait_ge(kept, b)
                    nc.tensor.matmul(ps_kv[b % 2][:], beta_wide[:, b, :], kv_w, start=True, stop=False)
                    nc.tensor.matmul(ps_kv[b % 2][:], ones[0:1, :], kv_row[:], start=False, stop=True).then_inc(summed, 1)

            @block.vector
            def _(ve):
                ve.wait_ge(summed, 1)
                ts(biases[:, 0, :], ps_q[:], vectors[:, 0:1], None, ALU.add).then_inc(kept, 1)
                for b in range(B):
                    ve.wait_ge(summed, b + 2)
                    nc.vector.tensor_copy(kv_bias[:, b, :], ps_kv[b % 2][:]).then_inc(kept, 1)

        SIDE = H // SUB
        ROWS, NBUF = 8, 4
        CHUNKS, TILES = SIDE // ROWS, ROWS * SIDE // P
        NT = CHUNKS * TILES
        raw = [sb(f"sample_rows{j}", [P, ROWS, W]) for j in range(NBUF)]
        xs = [sb(f"samples{j}", [P, ROWS * SIDE]) for j in range(NBUF)]
        kv = [sb(f"kv{j}", [P, 2 * C]) for j in range(4)]
        e, r, key = ([sb(f"{n}{j}", [P, C]) for j in range(4)] for n in ("key_exp", "key_relu", "key"))
        kv_masked = sb("kv_masked", [P, C])
        ps_t = [ctx.enter_context(nc.psum_tensor(f"kv_ps{j}", [P, 2 * C], F32)) for j in range(3)]
        ps_kv, ps_k, ps_o = (ctx.enter_context(nc.psum_tensor(n, [P, C], F32)) for n in ("kv_sum_ps", "k_sum_ps", "w_out_ps"))
        rows_in = [sem(f"sample_rows_in{j}") for j in range(NBUF)]
        picked, made, biased, exped, keyed, added, matrices, folded, relued = (
            sem(n) for n in ("samples_picked", "kv_made", "kv_biased", "key_exped", "keys_made", "kv_added",
                             "kv_matrices", "kv_folded", "key_relued"))
        block = ctx.enter_context(nc.Block())
        sampled = x3.rearrange("b c (r s) w -> b c r s w", s=SUB)

        def tile(i, k):
            return i * NT + k

        @block.sync
        def _(sp):
            with sp.Fori(0, B) as i:
                for n in range(CHUNKS):
                    sp.wait_ge(picked, reusable(i * CHUNKS + n, NBUF))
                    src = sampled[bass.ds(i, 1), :, ROWS * n:ROWS * (n + 1), SUB0, :].rearrange("o c r w -> c (o r) w")
                    sp.dma_start(raw[n % NBUF][:], src).then_inc(rows_in[n % NBUF], 16)

        @block.tensor
        def _(pe):
            start(pe, made, made, added, folded)

            def keys_values(i, k):
                n = tile(i, k)
                pe.wait_ge(picked, done(i * CHUNKS + k // TILES))
                pe.wait_ge(biased, reusable(n, 2))
                nc.tensor.matmul(ps_t[k % 2][:], xs[k // TILES % NBUF][:, P * (k % TILES):P * (k % TILES + 1)],
                                 w_kv[:, bass.ds(i, 1), :].rearrange("p o c -> p (o c)"), start=True, stop=True)\
                    .then_inc(made, 1)

            def sum_up(i, k):
                n = tile(i, k)
                pe.wait_ge(keyed, done(n))
                if k == 0:
                    pe.wait_ge(matrices, reusable(i, 1))
                first, last = k == 0, k == NT - 1
                nc.tensor.matmul(ps_kv[:], kv[k % 4][:, C:2 * C], key[k % 4][:], start=first, stop=last)
                nc.tensor.matmul(ps_k[:], key[k % 4][:], ones, start=first, stop=last).then_inc(added, 1)
                if last:
                    pe.wait_ge(matrices, done(i))
                    nc.tensor.matmul(ps_o[:], kv_masked[:], weights[:, 3, :], start=True, stop=True).then_inc(folded, 1)

            side_by_side(pe, B, NT, [(2, keys_values), (0, sum_up)])

        @block.scalar
        def _(sc):
            start(sc, exped, picked)

            def pick(i, k):
                n = k // TILES
                if k % TILES == 0:
                    sc.wait_ge(rows_in[n % NBUF], (i * (CHUNKS // NBUF) + n // NBUF) * 16 + 16)
                    sc.wait_ge(made, done(tile(i, TILES * n + TILES - 1)) + AHEAD - TILES * NBUF)
                    nc.scalar.copy(xs[n % NBUF][:].rearrange("p (r s) -> p r s", r=ROWS),
                                   raw[n % NBUF][:, :, SUB0::SUB]).then_inc(picked, 1)

            def exponentials(i, k):
                n = tile(i, k)
                sc.wait_ge(biased, done(n))
                sc.wait_ge(keyed, reusable(n, 4))
                nc.scalar.activation(e[k % 4][:], kv[k % 4][:, 0:C], ACT.Exp).then_inc(exped, 1)

            side_by_side(sc, B, NT, [(6, pick), (0, exponentials)])

        @block.vector
        def _(ve):
            start(ve, biased, relued, keyed, matrices)

            def add_bias(i, k):
                n = tile(i, k)
                ve.wait_ge(made, done(n) + AHEAD)
                ve.wait_ge(added, reusable(n, 4))
                tt(kv[k % 4][:], ps_t[k % 2][:], kv_bias[:, bass.ds(i, 1), :].rearrange("p o c -> p (o c)"), ALU.add)\
                    .then_inc(biased, 1)
                ve.wait_ge(biased, done(n))
                ve.wait_ge(keyed, reusable(n, 4))
                ts(r[k % 4][:], kv[k % 4][:, 0:C], 0.0, None, ALU.max).then_inc(relued, 1)

            def make_keys(i, k):
                n = tile(i, k)
                ve.wait_ge(exped, done(n))
                ve.wait_ge(relued, done(n))
                nc.vector.scalar_tensor_tensor(out=key[k % 4][:], in0=e[k % 4][:], scalar=1.0, in1=r[k % 4][:],
                                               op0=ALU.min, op1=ALU.add).then_inc(keyed, 1)
                if k == NT - 1:
                    ve.wait_ge(added, done(n))
                    ve.wait_ge(folded, reusable(i, 1))
                    tt(w_den[:, bass.ds(i, 1), :].rearrange("p o c -> p (o c)"), ps_k[:], same_head, ALU.mult)
                    tt(kv_masked[:], ps_kv[:], same_head, ALU.mult).then_inc(matrices, 1)
                    ve.wait_ge(folded, done(i))
                    ts(w_out[:, bass.ds(i, 1), :].rearrange("p o c -> p (o c)"), ps_o[:], 1.0, None, ALU.mult)

            side_by_side(ve, B, NT, [(1, add_bias), (0, make_keys)])


def attend(nc, sem, x3, out, w_q, w_den, w_out, biases):
    with ExitStack() as ctx:
        def sb(name, shape, n):
            return [ctx.enter_context(nc.sbuf_tensor(f"{name}{j}", shape, F32)) for j in range(n)]

        T, SETS, PER = 512, 4, 4
        NT = SETS * PER
        TURNS = NPIX // (T * NT)
        xin, xout = sb("att_in", [P, PER * T], SETS), sb("att_out", [P, PER * T], SETS)
        e, r, q = sb("q_exp", [P, T], 4), sb("q_relu", [P, T], 4), sb("q", [P, T], 4)
        log_den, inv_den, qz = sb("log_den", [P, T], 2), sb("inv_den", [P, T], 2), sb("qz", [P, T], 4)
        eps = sb("att_eps", [P, 1], 1)[0]
        ps_q, ps_d, ps_o = ([ctx.enter_context(nc.psum_tensor(f"{n}{j}", [P, T], F32)) for j in range(2)]
                            for n in ("q_ps", "den_ps", "out_ps"))
        x_in, stored = ([sem(f"{n}{j}") for j in range(SETS)] for n in ("att_x_in", "att_stored"))
        q_made, exped, relued, q_kept, den_made, logged, inverted, scaled, out_made, out_kept, eps_set = (
            sem(f"att_{n}") for n in ("q_made", "q_exped", "q_relued", "q_kept", "den_made", "logged", "inverted", "scaled",
                                      "out_made", "out_kept", "eps_set"))
        block = ctx.enter_context(nc.Block())
        px = PER * T

        def tile(b, i, k):
            return b * (TURNS * NT) + i * NT + k

        @block.sync
        def _(sp):
            for j in range(SETS):
                sp.sem_inc(stored[j], 16)

            def load(b, i, j):
                src = x3[b].rearrange("c h w -> c (h w)")[:, bass.ds(i * (SETS * px) + j * px, px)]
                sp.dma_start(xin[j][:], src).then_inc(x_in[j], 16)

            def store(b, i, j):
                sp.wait_ge(out_kept, done(tile(b, i, PER * j + PER - 1)))
                dst = out[b].rearrange("c h w -> c (h w)")[:, bass.ds(i * (SETS * px) + j * px, px)]
                sp.dma_start(dst, xout[j][:]).then_inc(stored[j], 16)

            for j in range(SETS):
                load(0, 0, j)
            for b in range(B):
                with sp.Fori(0, TURNS - 1) as i:
                    for j in range(SETS):
                        store(b, i, j)
                        load(b, i + 1, j)
                for j in range(SETS):
                    store(b, TURNS - 1, j)
                    if b + 1 < B:
                        load(b + 1, 0, j)
            for j in range(SETS):
                sp.wait_ge(stored[j], 16 + 16 * B * TURNS)

        @block.tensor
        def _(pe):
            start(pe, q_made, den_made, out_made)
            for b in range(B):
                def queries(i, k):
                    if k % PER == 0:
                        pe.wait_ge(x_in[k // PER], (i + b * TURNS) * 16 + 16)
                    pe.wait_ge(relued, reusable(tile(b, i, k), 2))
                    nc.tensor.matmul(ps_q[k % 2][:], w_q[:, b, :], xin[k // PER][:, T * (k % PER):T * (k % PER + 1)],
                                     start=True, stop=True).then_inc(q_made, 1)

                def denominators(i, k):
                    pe.wait_ge(q_kept, done(tile(b, i, k)))
                    pe.wait_ge(logged, reusable(tile(b, i, k), 2))
                    nc.tensor.matmul(ps_d[k % 2][:], w_den[:, b, :], q[k % 4][:], start=True, stop=True)\
                        .then_inc(den_made, 1)

                def outputs(i, k):
                    pe.wait_ge(scaled, done(tile(b, i, k)))
                    pe.wait_ge(out_kept, reusable(tile(b, i, k), 2))
                    nc.tensor.matmul(ps_o[k % 2][:], w_out[:, b, :], qz[k % 4][:], start=True, stop=True)\
                        .then_inc(out_made, 1)

                side_by_side(pe, TURNS, NT, [(6, queries), (4, denominators), (0, outputs)])

        @block.scalar
        def _(sc):
            start(sc, exped, logged, inverted)
            sc.wait_ge(eps_set, 1)
            for b in range(B):
                def exponential(i, k):
                    n = tile(b, i, k)
                    sc.wait_ge(q_made, done(n))
                    sc.wait_ge(q_kept, reusable(n, 4))
                    nc.scalar.activation(e[k % 4][:], ps_q[k % 2][:], ACT.Exp, bias=biases[:, 0, b:b + 1]).then_inc(exped, 1)

                def invert(i, k):
                    n = tile(b, i, k)
                    sc.wait_ge(den_made, done(n))
                    sc.wait_ge(inverted, reusable(n, 2))
                    nc.scalar.activation(log_den[k % 2][:], ps_d[k % 2][:], ACT.Ln, bias=eps[:]).then_inc(logged, 1)
                    sc.wait_ge(logged, done(n))
                    sc.wait_ge(scaled, reusable(n, 2))
                    nc.scalar.activation(inv_den[k % 2][:], log_den[k % 2][:], ACT.Exp, scale=-1.0).then_inc(inverted, 1)

                side_by_side(sc, TURNS, NT, [(6, exponential), (4, invert)])

        @block.gpsimd
        def _(po):
            start(po, scaled)
            nc.gpsimd.memset(eps[:], EPS_ATT).then_inc(eps_set, 1)
            for b in range(B):
                def scale(i, k):
                    n = tile(b, i, k)
                    po.wait_ge(inverted, done(n))
                    po.wait_ge(out_made, reusable(n, 4))
                    nc.gpsimd.tensor_tensor(qz[k % 4][:], q[k % 4][:], inv_den[k % 2][:], ALU.mult).then_inc(scaled, 1)

                side_by_side(po, TURNS, NT, [(2, scale)])

        @block.vector
        def _(ve):
            start(ve, relued, q_kept, out_kept)
            for b in range(B):
                def relu(i, k):
                    n = tile(b, i, k)
                    ve.wait_ge(exped, done(n))
                    ve.wait_ge(q_kept, reusable(n, 4))
                    nc.vector.tensor_scalar(r[k % 4][:], ps_q[k % 2][:], biases[:, 0, b:b + 1], 0.0, ALU.add, ALU.max)\
                        .then_inc(relued, 1)

                def finish_map(i, k):
                    n = tile(b, i, k)
                    ve.wait_ge(relued, done(n))
                    ve.wait_ge(scaled, reusable(n, 4))
                    ve.wait_ge(den_made, reusable(n, 4))
                    nc.vector.scalar_tensor_tensor(out=q[k % 4][:], in0=e[k % 4][:], scalar=1.0, in1=r[k % 4][:],
                                                   op0=ALU.min, op1=ALU.add).then_inc(q_kept, 1)

                def add_up(i, k):
                    n, s = tile(b, i, k), slice(T * (k % PER), T * (k % PER + 1))
                    if k % PER == 0:
                        ve.wait_ge(stored[k // PER], (i + b * TURNS) * 16 + 16)
                    ve.wait_ge(out_made, done(n))
                    nc.vector.scalar_tensor_tensor(out=xout[k // PER][:, s], in0=ps_o[k % 2][:],
                                                   scalar=biases[:, 1, b:b + 1], in1=xin[k // PER][:, s],
                                                   op0=ALU.add, op1=ALU.add).then_inc(out_kept, 1)

                side_by_side(ve, TURNS, NT, [(6, relu), (5, finish_map), (0, add_up)])


def conv_stack(nc, a, out):
    with ExitStack() as top:
        def sem(name):
            return top.enter_context(nc.semaphore(name))

        def sb(name, shape):
            return top.enter_context(nc.sbuf_tensor(name, shape, F32))

        def dram(name, shape):
            return nc.dram_tensor(name, shape, F32, kind="Internal").ap()

        x, x3 = a["x"], dram("x3", [B, C, H, W])
        rev, lhs = dram("reversed_kernels", [2, C, LAGS]), dram("mode_rows_all", [RI, C, B, 2 * KX])
        rows = sb("norm2_rows", [P, 3, B])
        norm2 = {n: rows[:, j, :] for j, n in enumerate(("sum", "inv", "skip"))}
        sums = sb("x3_sums", [P, 2, B, C])

        ssm_kernels(nc, sem, a, rev)
        with nc.sbuf_tensor("modes", [P, B, KX, RI], F32) as spec:
            with nc.sbuf_tensor("x_squares", [P, B, WT, GROUPS], F32) as squares:
                spectrum(nc, sem, x, spec, squares, a)
                modes_layers(nc, sem, a, spec, squares, norm2)
            modes_to_rows(nc, sem, a, spec, lhs)
        with nc.sbuf_tensor("norm2_all", [P, 2, B, C], F32) as every:
            spread(nc, sem, a, [norm2["inv"], norm2["skip"]], [every[:, 0], every[:, 1]])
            toeplitz_layer(nc, sem, a, x, lhs, rev, x3, every[:, 0], every[:, 1], sums)
        w_q, w_den, w_out = sb("w_q", [P, B, C]), sb("w_den", [P, B, C]), sb("w_out", [P, B, C])
        biases = sb("layer3_biases", [P, 2, B])
        attention_matrices(nc, sem, a, x3, sums, norm2["sum"], w_q, w_den, w_out, biases)
        attend(nc, sem, x3, out, w_q, w_den, w_out, biases)


def _laid_out(given):
    def t(name, *axes):
        return np.ascontiguousarray(np.transpose(given[name], axes or None))

    arrays = {
        "x": given["x"], "table": constants()[0],
        "w0": np.ascontiguousarray(np.transpose(given["L0_conv_weight"][0], (2, 0, 3, 1))),
        "fc_wT": t("L0_conv_fc_w"), "fc_b": given["L0_conv_fc_b"],
        "w1_re": t("L1_conv_weight_real", 3, 0, 1, 2, 4).reshape(KX, C, C // 4, KY),
        "w1_im": t("L1_conv_weight_imag", 3, 0, 1, 2, 4).reshape(KX, C, C // 4, KY),
        "bias1": given["L1_conv_bias"], "D": given["L2_conv_D"],
        "q_wT": t("L3_conv_q_w"), "kv_wT": t("L3_conv_kv_w"), "proj_wT": t("L3_conv_proj_w"),
        "q_b": given["L3_conv_q_b"], "kv_b": given["L3_conv_kv_b"], "proj_b": given["L3_conv_proj_b"],
    }
    for axis in range(2):
        arrays[f"log_dt{axis}"] = given[f"L2_conv_log_dt{axis}"]
        for n in ("A_re", "A_im"):
            arrays[f"{n}{axis}"] = t(f"L2_conv_{n}{axis}")
        for n in ("C_re", "C_im"):
            arrays[f"{n}{axis}"] = t(f"L2_conv_{n}{axis}", 2, 0, 1)
    return {n: np.ascontiguousarray(v) for n, v in arrays.items()}


def kernel(**inputs):
    import concourse.bacc as bacc
    from concourse.bass_utils import run_bass_kernel_spmd

    nc = bacc.Bacc("TRN2", target_bir_lowering=False, num_devices=1)
    arrays = _laid_out({n: np.asarray(v) for n, v in inputs.items()})
    a = {n: nc.dram_tensor(f"in_{n}", v.shape, mybir.dt.from_np(v.dtype), kind="ExternalInput").ap()
         for n, v in arrays.items()}
    out = nc.dram_tensor("out", (B, C, H, W), F32, kind="ExternalOutput").ap()
    conv_stack(nc, a, out)
    r = run_bass_kernel_spmd(nc, [{f"in_{n}": v for n, v in arrays.items()}], core_ids=[0])
    return r.results[0]["out"]
```

```python
from contextlib import ExitStack

import numpy as np

import concourse.bass as bass
from concourse import mybir

F32 = mybir.dt.float32
F16 = mybir.dt.float16
ALU = mybir.AluOpType
ACT = mybir.ActivationFunctionType
AX = mybir.AxisListType

P = 128
B, C, H, W = 4, 128, 256, 256
NPIX = H * W
GROUPS = 32
PER_GROUP = C // GROUPS
GROUP_PIX = PER_GROUP * NPIX
KX, KY = 64, 33
K0 = 32
RI = 2 * KY
HT = H // P
WT = W // P
EPS_GN = 1e-5
N_SSM = 64
STEP = 16
LAGS = 2 * H
HEADS_L3 = 8
SUB, SUB0 = 4, 2
EPS_ATT = 1e-6
QUADS = C // 4
TWO_PI = 2 * np.pi
ROUND = 1.5 * 2.0 ** 23


def constants():
    h = np.arange(H)
    kx, ky = np.arange(KX), np.arange(KY)
    tx = TWO_PI * ((h[:, None] * kx[None, :]) % H) / H
    ty = TWO_PI * ((h[:, None] * ky[None, :]) % W) / W
    dft_x = np.concatenate([np.cos(tx), -np.sin(tx)], 1).reshape(HT, P, 2 * KX).transpose(1, 0, 2)
    from_re = np.concatenate([np.cos(ty), -np.sin(ty)], 1)
    from_im = np.concatenate([np.sin(ty), np.cos(ty)], 1)
    dft_y = np.stack([from_re, from_im], 1).reshape(WT, P, 2, RI).transpose(1, 0, 2, 3)
    inv_y = np.zeros((P, W))
    inv_y[:RI] = np.concatenate([np.cos(ty), -np.sin(ty)], 1).T
    inv_x = np.concatenate([np.cos(tx), -np.sin(tx)], 1).T * (2.0 / NPIX)
    c = np.arange(P)
    same_group = (c[:, None] // PER_GROUP == c[None, :] // PER_GROUP) * 1.0
    same_head = (c[:, None] // (C // HEADS_L3) == c[None, :] // (C // HEADS_L3)) * 1.0
    b = np.arange(STEP)
    fine = np.concatenate([STEP - 1 - b, b])
    coarse = STEP * np.concatenate([STEP - 1 - b, b])
    hermitian = np.ones((KX, 2, KY))
    hermitian[1:, :, 0] = 0.5
    hermitian[0, 1, 0] = 0.0
    rows = lambda a: np.broadcast_to(a.reshape(1, -1), (P, a.size))
    parts = {
        "dft_x": dft_x, "dft_y": dft_y, "inv_y": inv_y, "inv_x": inv_x, "same_group": same_group,
        "same_head": same_head, "ident": np.eye(P), "ones": np.ones((P, P)), "fine": rows(fine),
        "coarse": rows(coarse), "hermitian": rows(hermitian),
    }
    where, at = {}, 0
    for name, a in parts.items():
        n = a.reshape(P, -1).shape[1]
        where[name] = (at, n)
        at += n
    table = np.concatenate([a.reshape(P, -1) for a in parts.values()], 1).astype(np.float32)
    return np.ascontiguousarray(table), where


def chained(eng, sem, start=0):
    count = [start]

    def link(ins):
        count[0] += 1
        ins.then_inc(sem, 1)
        eng.wait_ge(sem, count[0])

    return link


TINY = 1e-30
NORM_SCALE = 64.0
KERNEL_SCALE = 2.0 ** 14
"""Where float32 products dominate, an operand known to lie in [-2**15, 2**15] is split into two
float16 parts, high and low, of together 22 bits; high x high + high x low + low x high in float32
sums stands for the float32 product at three passes instead of four. Group norms bound what they
give by sqrt(the group's size) = 512, and a kernel is scaled by its maximum."""

AHEAD = 8
"""In the pipelined parts a counting semaphore starts at AHEAD, so that a wait for "item n minus the
buffers" is never against a value below one."""


def start(eng, *sems):
    for s in sems:
        eng.sem_inc(s, AHEAD)


def done(n):
    return n + (1 + AHEAD)


def reusable(n, buffers):
    assert buffers <= AHEAD
    return n + (1 + AHEAD - buffers)


def side_by_side(eng, turns, per_turn, steps):
    for n in range(-max(lead for lead, _ in steps), 0):
        for lead, step in steps:
            if n + lead >= 0:
                step(0, n + lead)
    with eng.Fori(0, turns - 1) as i:
        for k in range(per_turn):
            for lead, step in steps:
                step(i + (k + lead) // per_turn, (k + lead) % per_turn)
    for k in range(per_turn):
        for lead, step in steps:
            if k + lead < per_turn:
                step(turns - 1, k + lead)


def ssm_kernels(nc, sem, a, rev):
    with ExitStack() as ctx:
        def sb(name, shape):
            return ctx.enter_context(nc.sbuf_tensor(name, shape, F32))

        _, where = constants()
        f0, fn = where["fine"]
        c0, cn = where["coarse"]
        par = sb("ssm_par", [P, 7, P])
        dt_log, a_re, a_im = par[:, 0, :], par[:, 1, :], par[:, 2, :]
        c_re, c_im = par[:, 3:5, :], par[:, 5:7, :]
        fine, coarse = sb("fine", [P, 2 * STEP]), sb("coarse", [P, 2 * STEP])
        tmp = [sb(f"ssm_tmp{j}", [P, P]) for j in range(12)]
        dt, dre, dim, mag, cyc, rnd, cs, sn, er, ei, inv, q_i = tmp
        q_r = sb("ssm_qr", [P, P])
        k_re, k_im, k_t = (sb(n, [P, 2, P]) for n in ("ssm_kre", "ssm_kim", "ssm_kt"))
        big = [P, P, 2 * STEP]
        f_re, f_im, g_re, g_im, b_mag, b_cyc, b_rnd = (sb(f"ssm_big{j}", big) for j in range(7))
        p_re, p_im = sb("ssm_pre", big), sb("ssm_pim", big)
        kk = sb("ssm_kk", [2 * STEP, 2, P, 2 * STEP])
        ps = [ctx.enter_context(nc.psum_tensor(f"ssm_ps{j}", [2 * STEP, STEP, 2 * STEP], F32)) for j in range(4)]
        loaded, dve, act, put = sem("ssm_loaded"), sem("ssm_dve"), sem("ssm_act"), sem("ssm_put")
        ready, summed, kept = sem("ssm_ready"), sem("ssm_summed"), sem("ssm_kept")
        block = ctx.enter_context(nc.Block())
        n_blocks = 2 * P // STEP

        @block.sync
        def _(sp):
            sp.dma_start(fine[:], a["table"][:, f0:f0 + fn]).then_inc(loaded, 16)
            sp.dma_start(coarse[:], a["table"][:, c0:c0 + cn]).then_inc(loaded, 16)
            for axis in range(2):
                s = slice(N_SSM * axis, N_SSM * (axis + 1))
                row = a[f"log_dt{axis}"].rearrange("(o h) -> o h", o=1).broadcast_to([N_SSM, P])
                sp.dma_start(par[s, 0, :], row).then_inc(loaded, 16)
                sp.dma_start(par[s, 1, :], a[f"A_re{axis}"]).then_inc(loaded, 16)
                sp.dma_start(par[s, 2, :], a[f"A_im{axis}"]).then_inc(loaded, 16)
                sp.dma_start(par[s, 3:5, :], a[f"C_re{axis}"]).then_inc(loaded, 16)
                sp.dma_start(par[s, 5:7, :], a[f"C_im{axis}"]).then_inc(loaded, 16)
            sp.wait_ge(kept, n_blocks)
            for axis in range(2):
                for way in range(2):
                    s = slice(STEP * way, STEP * (way + 1))
                    sp.dma_start(rev[axis, :, H * way:H * (way + 1)].rearrange("h (a b) -> a h b", b=STEP),
                                 kk[s, axis, :, s]).then_inc(put, 16)
            sp.wait_ge(put, 16 * 4)

        @block.scalar
        def _(sc):
            def fn(at, out, x, func, scale=1.0):
                if at:
                    sc.wait_ge(dve, at)
                nc.scalar.activation(out, x, func, scale=scale).then_inc(act, 1)

            sc.wait_ge(loaded, 16 * 12)
            fn(0, dt[:], dt_log, ACT.Exp)
            fn(2, mag[:], dre[:], ACT.Exp)
            fn(5, sn[:], cyc[:], ACT.Sin, TWO_PI)
            fn(8, cs[:], rnd[:], ACT.Sin, TWO_PI)
            flat = lambda t: t[:].rearrange("p h j -> p (h j)")
            for at, (re, im) in ((9, (f_re, f_im)), (19, (g_re, g_im))):
                fn(at, flat(b_mag), flat(b_mag), ACT.Exp)
                fn(at + 4, flat(im), flat(b_cyc), ACT.Sin, TWO_PI)
                fn(at + 7, flat(re), flat(b_rnd), ACT.Sin, TWO_PI)
            for n in range(n_blocks):
                sc.wait_ge(summed, n + 1)
                nc.scalar.activation(kk[:, n // (P // STEP), STEP * (n % (P // STEP)):STEP * (n % (P // STEP) + 1), :],
                                     ps[n % 4][:], ACT.Copy, scale=2.0).then_inc(kept, 1)

        @block.vector
        def _(ve):
            link = chained(ve, dve)
            tt, ts = nc.vector.tensor_tensor, nc.vector.tensor_scalar
            ve.wait_ge(loaded, 16 * 12)
            ve.wait_ge(act, 1)
            link(tt(dre[:], dt[:], a_re, ALU.mult))
            link(tt(dim[:], dt[:], a_im, ALU.mult))
            link(ts(cyc[:], dim[:], 1 / TWO_PI, None, ALU.mult))
            link(ts(rnd[:], cyc[:], ROUND, ROUND, ALU.add, ALU.subtract))
            link(tt(cyc[:], cyc[:], rnd[:], ALU.subtract))
            link(ts(cs[:], cyc[:], 0.25, None, ALU.add))
            link(ts(er[:], cs[:], ROUND, ROUND, ALU.add, ALU.subtract))
            link(tt(rnd[:], cs[:], er[:], ALU.subtract))

            def cycles(table, re, im, act_at):
                j = table[:].unsqueeze(1).broadcast_to(big)
                link(tt(b_mag[:], dre[:].unsqueeze(2).broadcast_to(big), j, ALU.mult))
                link(tt(b_cyc[:], dim[:].unsqueeze(2).broadcast_to(big), j, ALU.mult))
                link(ts(b_rnd[:], b_cyc[:], 1 / TWO_PI, None, ALU.mult))
                link(ts(re[:], b_rnd[:], ROUND, ROUND, ALU.add, ALU.subtract))
                link(tt(b_cyc[:], b_rnd[:], re[:], ALU.subtract))
                link(ts(b_rnd[:], b_cyc[:], 0.25, None, ALU.add))
                link(ts(re[:], b_rnd[:], ROUND, ROUND, ALU.add, ALU.subtract))
                link(tt(b_rnd[:], b_rnd[:], re[:], ALU.subtract))
                ve.wait_ge(act, act_at)
                link(tt(re[:], re[:], b_mag[:], ALU.mult))
                link(tt(im[:], im[:], b_mag[:], ALU.mult))

            cycles(fine, f_re, f_im, 7)
            cycles(coarse, g_re, g_im, 10)
            link(tt(er[:], mag[:], cs[:], ALU.mult))
            link(ts(er[:], er[:], 1.0, None, ALU.subtract))
            link(tt(ei[:], mag[:], sn[:], ALU.mult))
            link(tt(inv[:], a_re, a_re, ALU.mult))
            link(tt(rnd[:], a_im, a_im, ALU.mult))
            link(tt(inv[:], inv[:], rnd[:], ALU.add))
            link(nc.vector.reciprocal(inv[:], inv[:]))
            link(tt(q_r[:], er[:], a_re, ALU.mult))
            link(tt(rnd[:], ei[:], a_im, ALU.mult))
            link(tt(q_r[:], q_r[:], rnd[:], ALU.add))
            link(tt(q_r[:], q_r[:], inv[:], ALU.mult))
            link(tt(q_i[:], ei[:], a_re, ALU.mult))
            link(tt(rnd[:], er[:], a_im, ALU.mult))
            link(tt(q_i[:], q_i[:], rnd[:], ALU.subtract))
            link(tt(q_i[:], q_i[:], inv[:], ALU.mult))
            two = [P, 2, P]
            qr2, qi2 = q_r[:].unsqueeze(1).broadcast_to(two), q_i[:].unsqueeze(1).broadcast_to(two)
            link(tt(k_re[:], c_re, qr2, ALU.mult))
            link(tt(k_t[:], c_im, qi2, ALU.mult))
            link(tt(k_re[:], k_re[:], k_t[:], ALU.subtract))
            link(tt(k_im[:], c_re, qi2, ALU.mult))
            link(tt(k_t[:], c_im, qr2, ALU.mult))
            link(tt(k_im[:], k_im[:], k_t[:], ALU.add))
            for way in range(2):
                s = slice(STEP * way, STEP * (way + 1))
                half = [P, P, STEP]
                kr, ki = (t[:, way, :].unsqueeze(2).broadcast_to(half) for t in (k_re, k_im))
                link(tt(p_re[:, :, s], g_re[:, :, s], kr, ALU.mult))
                link(tt(b_rnd[:, :, s], g_im[:, :, s], ki, ALU.mult))
                link(tt(p_re[:, :, s], p_re[:, :, s], b_rnd[:, :, s], ALU.subtract))
                link(tt(p_im[:, :, s], g_re[:, :, s], ki, ALU.mult))
                link(tt(b_rnd[:, :, s], g_im[:, :, s], kr, ALU.mult))
                link(tt(p_im[:, :, s], p_im[:, :, s], b_rnd[:, :, s], ALU.add))
            nc.vector.tensor_scalar(p_im[:], p_im[:], -1.0, None, ALU.mult).then_inc(ready, 1)

        @block.tensor
        def _(pe):
            pe.wait_ge(ready, 1)
            for n in range(n_blocks):
                axis, h0 = n // (P // STEP), STEP * (n % (P // STEP))
                s = slice(N_SSM * axis, N_SSM * (axis + 1))
                if n >= 4:
                    pe.wait_ge(kept, n - 3)
                for j in range(STEP):
                    nc.tensor.matmul(ps[n % 4][:, j, :], p_re[s, h0 + j, :], f_re[s, h0 + j, :], start=True, stop=False)
                    last = nc.tensor.matmul(ps[n % 4][:, j, :], p_im[s, h0 + j, :], f_im[s, h0 + j, :],
                                            start=False, stop=True)
                last.then_inc(summed, 1)


def spectrum(nc, sem, x, spec, squares, a):
    with ExitStack() as ctx:
        def sb(name, shape):
            return ctx.enter_context(nc.sbuf_tensor(name, shape, F32))

        _, where = constants()
        (x0, xn), (y0, yn) = where["dft_x"], where["dft_y"]
        NX = 4
        quads = [sb(f"quad{j}", [P, HT, 4, P]) for j in range(NX)]
        half = sb("half", [P, C, 2 * KX])
        dft_x = sb("dft_x", [P, HT, 2 * KX])
        dft_y = sb("dft_y", [P, WT, 2, RI])
        junk = [sb(f"square_junk{j}", [P, HT * 4 * P]) for j in range(2)]
        sums = sb("square_sums", [P, NX])
        ps1 = [ctx.enter_context(nc.psum_tensor(f"half_ps{j}", [P, 4, 2 * KX], F32)) for j in range(4)]
        ps2 = [ctx.enter_context(nc.psum_tensor(f"spec_ps{j}", [P, 4, RI], F32)) for j in range(4)]
        tables, loaded = sem("dft_tables"), [sem(f"quad_loaded{j}") for j in range(NX)]
        halved, half_kept, squared = sem("halved"), sem("half_kept"), sem("squared")
        modes, modes_kept, sums_kept = sem("modes"), sem("modes_kept"), sem("sums_kept")
        block = ctx.enter_context(nc.Block())
        turns = QUADS // NX
        kgroups = KX // 4

        def quad_of(b, wt, i, j):
            return (b * WT + wt) * QUADS + i * NX + j

        @block.sync
        def _(sp):
            sp.dma_start(dft_x[:], a["table"][:, x0:x0 + xn].rearrange("p (t k) -> p t k", t=HT)).then_inc(tables, 16)
            sp.dma_start(dft_y[:], a["table"][:, y0:y0 + yn].rearrange("p (t i k) -> p t i k", t=WT, i=2))\
                .then_inc(tables, 16)
            with sp.Fori(0, B) as b:
                for wt in range(WT):
                    with sp.Fori(0, turns) as i:
                        for j in range(NX):
                            sp.wait_ge(halved, reusable(quad_of(b, wt, i, j), NX))
                            sp.wait_ge(squared, reusable(quad_of(b, wt, i, j), NX))
                            for t in range(HT):
                                src = x[bass.ds(b, 1), bass.ds(i * (4 * NX) + 4 * j, 4), P * t:P * (t + 1),
                                        P * wt:P * (wt + 1)]
                                sp.dma_start(quads[j][:, t], src.rearrange("o c h w -> h (o c) w"))\
                                    .then_inc(loaded[j], 16)

        @block.tensor
        def _(pe):
            start(pe, halved, modes)
            pe.wait_ge(tables, 32)
            with pe.Fori(0, B) as b:
                for wt in range(WT):
                    with pe.Fori(0, turns) as i:
                        for j in range(NX):
                            pe.wait_ge(loaded[j], ((b * WT + wt) * turns + i) * (16 * HT) + 16 * HT)
                            pe.wait_ge(half_kept, reusable(quad_of(b, wt, i, j), 4))
                            for c in range(4):
                                for t in range(HT):
                                    last = nc.tensor.matmul(ps1[j][:, c, :], quads[j][:, t, c, :], dft_x[:, t, :],
                                                            start=t == 0, stop=t == HT - 1)
                            last.then_inc(halved, 1)
                    pe.wait_ge(half_kept, done(quad_of(b, wt, 0, QUADS - 1)))
                    for g in range(kgroups):
                        pe.wait_ge(modes_kept, reusable((b * WT + wt) * kgroups + g, 4))
                        for k in range(4):
                            for ri in range(2):
                                last = nc.tensor.matmul(ps2[g % 4][:, k, :], half[:, :, KX * ri + 4 * g + k],
                                                        dft_y[:, wt, ri, :], start=ri == 0, stop=ri == 1)
                        last.then_inc(modes, 1)

        @block.scalar
        def _(sc):
            start(sc, half_kept)
            with sc.Fori(0, B) as b:
                for wt in range(WT):
                    sc.wait_ge(modes, reusable((b * WT + wt) * kgroups, 1))
                    with sc.Fori(0, turns) as i:
                        for j in range(NX):
                            sc.wait_ge(halved, done(quad_of(b, wt, i, j)))
                            nc.scalar.activation(half[:, bass.ds(i * (4 * NX) + 4 * j, 4), :], ps1[j][:], ACT.Copy)\
                                .then_inc(half_kept, 1)

        @block.vector
        def _(ve):
            start(ve, squared, modes_kept)
            with ve.Fori(0, B) as b:
                for wt in range(WT):
                    with ve.Fori(0, turns) as i:
                        for j in range(NX):
                            q = quads[j][:].rearrange("p t c w -> p (t c w)")
                            ve.wait_ge(loaded[j], ((b * WT + wt) * turns + i) * (16 * HT) + 16 * HT)
                            ve.wait_ge(squared, reusable(quad_of(b, wt, i, j), 2))
                            nc.vector.tensor_tensor_reduce(junk[j % 2][:], q, q, 1.0, 0.0, ALU.mult, ALU.add,
                                                           sums[:, j:j + 1]).then_inc(squared, 1)
                        ve.wait_ge(squared, done(quad_of(b, wt, i, NX - 1)))
                        nc.vector.tensor_scalar(
                            squares[:, bass.ds(b, 1), wt, bass.ds(i * NX, NX)].rearrange("p o g -> p (o g)"), sums[:],
                            1.0, None, ALU.mult).then_inc(sums_kept, 1)
                        ve.wait_ge(sums_kept, (b * WT + wt) * turns + i + 1)
                    for g in range(kgroups):
                        ve.wait_ge(modes, done((b * WT + wt) * kgroups + g))
                        out = spec[:, bass.ds(b, 1), 4 * g:4 * g + 4, :].rearrange("p o k r -> p (o k) r")
                        if wt == 0:
                            nc.vector.tensor_scalar(out, ps2[g % 4][:], 1.0, None, ALU.mult).then_inc(modes_kept, 1)
                        else:
                            ve.wait_ge(modes_kept, reusable((b * WT + wt) * kgroups + g, 4))
                            nc.vector.tensor_tensor(out, ps2[g % 4][:], out, ALU.add).then_inc(modes_kept, 1)


def norm_moments(nc, sem, name, products, before, after, small, scale=1.0 / NPIX):
    with ExitStack() as ctx:
        ps = ctx.enter_context(nc.psum_tensor(f"{name}_ps", [P, 2, B], F32))
        steps, summed, rooted, var_ready, pair_ready = (sem(f"{name}_{n}") for n in ("steps", "summed", "rooted", "var", "pair"))
        block = ctx.enter_context(nc.Block())

        @block.vector
        def _(ve):
            link = chained(ve, steps)
            tt, ts = nc.vector.tensor_tensor, nc.vector.tensor_scalar
            before(link)
            nc.vector.memset(small["u"], 0.0).then_inc(pair_ready, 1)
            ve.wait_ge(summed, 1)
            link(nc.vector.scalar_tensor_tensor(out=small["q"], in0=ps[:, 0, :], scalar=scale, in1=small["q"],
                                                op0=ALU.mult, op1=ALU.add))
            link(ts(small["mean"], ps[:, 1, :], 1.0 / GROUP_PIX, None, ALU.mult))
            link(tt(small["t"], small["mean"], small["mean"], ALU.mult))
            link(nc.vector.scalar_tensor_tensor(out=small["q"], in0=small["t"], scalar=-float(GROUP_PIX), in1=small["q"],
                                                op0=ALU.mult, op1=ALU.add))
            ts(small["t"], small["q"], 1.0 / GROUP_PIX, EPS_GN, ALU.mult, ALU.add).then_inc(var_ready, 1)
            ve.wait_ge(rooted, 1)
            link(nc.vector.reciprocal(small["inv"], small["u"]))
            after(link)

        @block.scalar
        def _(sc):
            sc.wait_ge(var_ready, 1)
            nc.scalar.activation(small["u"], small["t"], ACT.Sqrt).then_inc(rooted, 1)

        @block.tensor
        def _(pe):
            pe.wait_ge(pair_ready, 1)
            products(ps).then_inc(summed, 1)


def window_energy(nc, sem, name, spec, out):
    with ExitStack() as ctx:
        junk = [ctx.enter_context(nc.sbuf_tensor(f"{name}_junk{j}", [P, KX * RI], F32)) for j in range(2)]
        squared, squared_ve = sem(f"{name}_squared"), sem(f"{name}_squared_ve")
        block = ctx.enter_context(nc.Block())

        @block.scalar
        def _(sc):
            for b in (0, 2):
                nc.scalar.activation(junk[0][:], spec[:, b].rearrange("p k r -> p (k r)"), ACT.Square,
                                     accum_out=out[:, b:b + 1]).then_inc(squared, 1)
                sc.wait_ge(squared, b // 2 + 1)

        @block.vector
        def _(ve):
            for b in (1, 3):
                x = spec[:, b].rearrange("p k r -> p (k r)")
                nc.vector.tensor_tensor_reduce(junk[1][:], x, x, 1.0, 0.0, ALU.mult, ALU.add, out[:, b:b + 1])\
                    .then_inc(squared_ve, 1)
                ve.wait_ge(squared_ve, b // 2 + 1)


def low_part(spec, b):
    return spec[:, b, 0:K0, :].rearrange("p k (r y) -> p k r y", r=2)[:, :, :, 0:K0]


def layer0_products(nc, sem, a, low, fc_w, herm):
    with ExitStack() as ctx:
        ROWS = 4
        w0 = [ctx.enter_context(nc.sbuf_tensor(f"w0_row{j}", [P, K0, P], F32)) for j in range(ROWS)]
        ps = [ctx.enter_context(nc.psum_tensor(f"mix0_ps{j}", [P, B, 2, K0], F32)) for j in range(4)]
        ps_fc = [ctx.enter_context(nc.psum_tensor(f"fc_ps{j}", [P, 8, 2, K0], F32)) for j in range(4)]
        loaded = [sem(f"w0_loaded{j}") for j in range(ROWS)]
        mixed, kept, projected, fc_kept = sem("mix0_mixed"), sem("mix0_kept"), sem("fc_projected"), sem("fc_kept")
        block = ctx.enter_context(nc.Block())
        n_fc = B * K0 // 8

        @block.sync
        def _(sp):
            with sp.Fori(0, K0 // ROWS) as i:
                for j in range(ROWS):
                    sp.wait_ge(mixed, reusable(i * ROWS + j, ROWS))
                    src = a["w0"][bass.ds(i * ROWS + j, 1)].rearrange("m c n o -> c (m n) o")
                    sp.dma_start(w0[j][:], src).then_inc(loaded[j], 16)

        @block.tensor
        def _(pe):
            start(pe, mixed)
            with pe.Fori(0, K0 // ROWS) as i:
                for j in range(ROWS):
                    pe.wait_ge(loaded[j], i * 16 + 16)
                    pe.wait_ge(kept, reusable(i * ROWS + j, 4))
                    for n in range(K0):
                        rhs = low[:, :, bass.ds(i * ROWS + j, 1), :, n].rearrange("p b o r -> p b (o r)")
                        last = nc.tensor.matmul(ps[j][:, :, :, n], w0[j][:, n, :], rhs, start=True, stop=True)
                    last.then_inc(mixed, 1)
            pe.wait_ge(kept, done(K0 - 1))
            for n in range(n_fc):
                if n >= 4:
                    pe.wait_ge(fc_kept, n - 3)
                rhs = low[:, n // 4, 8 * (n % 4):8 * (n % 4) + 8].rearrange("p k r y -> p (k r y)")
                nc.tensor.matmul(ps_fc[n % 4][:].rearrange("p k r y -> p (k r y)"), fc_w[:], rhs, start=True, stop=True)\
                    .then_inc(projected, 1)

        @block.vector
        def _(ve):
            start(ve, kept)
            with ve.Fori(0, K0 // ROWS) as i:
                for j in range(ROWS):
                    ve.wait_ge(mixed, done(i * ROWS + j))
                    out = low[:, :, bass.ds(i * ROWS + j, 1), :, :].rearrange("p b o r y -> p b (o r y)")
                    nc.vector.tensor_scalar(out, ps[j][:].rearrange("p b r y -> p b (r y)"), 1.0, None, ALU.mult)\
                        .then_inc(kept, 1)
            for n in range(n_fc):
                k = slice(8 * (n % 4), 8 * (n % 4) + 8)
                ve.wait_ge(projected, n + 1)
                nc.vector.tensor_tensor(low[:, n // 4, k], ps_fc[n % 4][:], herm[:, k, :, 0:K0], ALU.mult)\
                    .then_inc(fc_kept, 1)


def layer1_products(nc, sem, a, spec, inv, neg_inv, herm, change):
    with ExitStack() as ctx:
        def sb(name, shape):
            return ctx.enter_context(nc.sbuf_tensor(name, shape, F32))

        ROWS, HEADS, HC = 2, 4, C // 4
        PARTS, PER_PART = 3, KY // 3
        w = [[sb(f"w1_row{j}{r}", [P, KY, HC]) for r in "ri"] for j in range(ROWS)]
        scaled = [sb(f"scaled{j}", [P, KY, 3, HEADS, B]) for j in range(ROWS)]
        turned = [sb(f"turned{j}", [HC, KY, 2, HEADS, B]) for j in range(ROWS)]
        added = [sb(f"added{j}", [P, B, 2, KY]) for j in range(ROWS)]
        twice = [sb(f"twice{j}", [P, B, RI]) for j in range(ROWS)]
        ps = [[ctx.enter_context(nc.psum_tensor(f"mix1_ps{j}{t}", [HC, PER_PART, HC], F32)) for t in range(PARTS)]
              for j in range(ROWS)]
        loaded = [[sem(f"w1_loaded{j}{r}") for r in "ri"] for j in range(ROWS)]
        zeroed, staged, mixed, steps, back, headed, copied = (
            sem(n) for n in ("scaled_zeroed", "mix1_staged", "mix1_mixed", "mix1_steps", "mix1_turned", "mix1_headed",
                             "mix1_copied"))
        block = ctx.enter_context(nc.Block())
        STEPS = 4

        def row_of(k):
            return spec[:, :, bass.ds(k, 1), :].rearrange("p b o r -> p b (o r)")

        def head(h):
            return slice(HC * h, HC * (h + 1))

        @block.sync
        def _(sp):
            with sp.Fori(0, KX // ROWS) as i:
                for j in range(ROWS):
                    sp.wait_ge(mixed, reusable(i * ROWS + j, ROWS))
                    for r in range(2):
                        src = a["w1_im" if r else "w1_re"][bass.ds(i * ROWS + j, 1)].rearrange("x c y o -> c (x y) o")
                        sp.dma_start(w[j][r][:], src).then_inc(loaded[j][r], 16)

        @block.gpsimd
        def _(po):
            for j in range(ROWS):
                nc.gpsimd.memset(scaled[j][:], 0.0).then_inc(zeroed, 1)
            po.wait_ge(zeroed, ROWS)
            start(po, staged)
            with po.Fori(0, KX // ROWS) as i:
                for j in range(ROWS):
                    po.wait_ge(mixed, reusable(i * ROWS + j, ROWS))
                    for h in range(HEADS):
                        s = head(h)
                        row = row_of(i * ROWS + j)[s]
                        nc.gpsimd.tensor_tensor(
                            scaled[j][s, :, 1:3, h, :].rearrange("p y r b -> p b r y"),
                            row.rearrange("p b (r y) -> p b r y", r=2),
                            inv[s].unsqueeze(2).unsqueeze(3).broadcast_to([HC, B, 2, KY]), ALU.mult)
                        last = nc.gpsimd.tensor_tensor(
                            scaled[j][s, :, 0, h, :].rearrange("p y b -> p b y"), row[:, :, KY:RI],
                            neg_inv[s].unsqueeze(2).broadcast_to([HC, B, KY]), ALU.mult)
                    last.then_inc(staged, 1)

        @block.tensor
        def _(pe):
            start(pe, mixed)
            with pe.Fori(0, KX // ROWS) as i:
                for j in range(ROWS):
                    for r in range(2):
                        pe.wait_ge(loaded[j][r], i * 16 + 16)
                    pe.wait_ge(staged, done(i * ROWS + j))
                    pe.wait_ge(back, reusable(i * ROWS + j, ROWS))
                    for n in range(KY):
                        out = ps[j][n // PER_PART][:, n % PER_PART, :]
                        by_ri = scaled[j][:, n].rearrange("p t h b -> p (t h b)")
                        nc.tensor.matmul(out, by_ri[:, 16:48], w[j][0][:, n, :], start=True, stop=False)
                        last = nc.tensor.matmul(out, by_ri[:, 0:32], w[j][1][:, n, :], start=False, stop=True)
                    last.then_inc(mixed, 1)

        @block.scalar
        def _(sc):
            start(sc, headed, copied)
            with sc.Fori(0, KX // ROWS) as i:
                for j in range(ROWS):
                    k = i * ROWS + j
                    sc.wait_ge(back, done(k))
                    sc.wait_ge(copied, reusable(k, ROWS))
                    for h in range(HEADS):
                        last = nc.scalar.copy(added[j][head(h)].rearrange("p b r y -> p r b y"),
                                              turned[j][:, :, :, h, :].rearrange("p y r b -> p r b y"))
                    last.then_inc(headed, 1)
                    sc.wait_ge(steps, k * STEPS + STEPS)
                    nc.scalar.copy(row_of(k), added[j][:].rearrange("p b r y -> p b (r y)")).then_inc(copied, 1)

        @block.vector
        def _(ve):
            tt = nc.vector.tensor_tensor
            start(ve, back)

            def turn_back(k, j):
                ve.wait_ge(mixed, done(k))
                ve.wait_ge(headed, reusable(k, ROWS))
                for t in range(PARTS):
                    out = turned[j][:, PER_PART * t:PER_PART * (t + 1)].rearrange("p y r h b -> p (y r h b)")
                    last = nc.vector.transpose(out, ps[j][t][:].rearrange("p y o -> p (y o)"))
                last.then_inc(back, 1)

            def sums(k, j):
                def link(ins, n):
                    ins.then_inc(steps, 1)
                    ve.wait_ge(steps, k * STEPS + n)

                ve.wait_ge(headed, done(k))
                flat = added[j][:].rearrange("p b r y -> p b (r y)")
                mask = herm[:, bass.ds(k, 1), :, :].rearrange("p o r y -> p o (r y)").broadcast_to([P, B, RI])
                link(tt(flat, flat, mask, ALU.mult), 1)
                link(nc.vector.scalar_tensor_tensor(out=twice[j][:], in0=row_of(k), scalar=2.0, in1=flat,
                                                    op0=ALU.mult, op1=ALU.add), 2)
                link(tt(twice[j][:], twice[j][:], flat, ALU.mult), 3)
                link(nc.vector.tensor_reduce(change[:, :, bass.ds(k, 1)], twice[j][:], AX.X, ALU.add), 4)

            turn_back(0, 0)
            with ve.Fori(0, KX // ROWS - 1) as i:
                for j in range(ROWS):
                    turn_back(i * ROWS + j + 1, (j + 1) % ROWS)
                    sums(i * ROWS + j, j)
            turn_back(KX - 1, 1)
            sums(KX - 2, 0)
            sums(KX - 1, 1)


def modes_layers(nc, sem, a, spec, squares, small_rows):
    with ExitStack() as ctx:
        def sb(name, shape):
            return ctx.enter_context(nc.sbuf_tensor(name, shape, F32))

        _, where = constants()
        group, ones = sb("same_group", [P, P]), sb("mix_ones", [P, 2])
        herm = sb("hermitian", [P, KX, 2, KY])
        fc_w, bias = sb("fc_w", [P, P]), sb("mode_biases", [P, 3])
        low = sb("low_modes", [P, B, K0, 2, K0])
        change = sb("energy_change", [P, B, KX])
        by_channel = sb("squares_by_channel", [P, B, WT, GROUPS, PER_GROUP])
        names = ("q", "t", "u", "mean", "before", "after", "dc", "added_dc", "bias_dc", "neg_inv", "e0")
        rows = sb("mix_small", [P, len(names), B])
        pair = sb("mix_pair", [P, 2, B])
        small = {n: rows[:, j, :] for j, n in enumerate(names)} | small_rows
        spec_dc = spec[:, :, 0, 0]
        loaded, added0 = sem("mode_tables"), sem("layer0_added")

        def table(name):
            at, n = where[name]
            return a["table"][:, at:at + n]

        with nc.Block() as block:
            @block.sync
            def _(sp):
                sp.dma_start(group[:], table("same_group")).then_inc(loaded, 16)
                sp.dma_start(ones[:], table("ones")[:, 0:2]).then_inc(loaded, 16)
                sp.dma_start(herm[:], table("hermitian").rearrange("p (k r y) -> p k r y", k=KX, r=2)).then_inc(loaded, 16)
                sp.dma_start(fc_w[:], a["fc_wT"]).then_inc(loaded, 16)
                sp.dma_start(bias[:, 0:1], a["fc_b"].rearrange("(c o) -> c o", o=1)).then_inc(loaded, 16)
                sp.dma_start(bias[:, 1:2], a["bias1"].rearrange("c o t -> c (o t)")).then_inc(loaded, 16)
                sp.dma_start(bias[:, 2:3], a["D"].rearrange("o c -> c o")).then_inc(loaded, 16)
                sp.wait_ge(loaded, 16 * 7)

        tt, ts, stt = nc.vector.tensor_tensor, nc.vector.tensor_scalar, nc.vector.scalar_tensor_tensor

        def shift(link):
            link(stt(out=spec_dc, in0=small["mean"], scalar=-float(NPIX), in1=spec_dc, op0=ALU.mult, op1=ALU.add))
            link(tt(small["sum"], small["sum"], small["mean"], ALU.add))

        def products0(ps):
            for b in range(B):
                for t in range(WT):
                    nc.tensor.matmul(ps[:, 0, b:b + 1], by_channel[:, b, t, :, :].rearrange("p g n -> p (g n)"), ones[:, 0:1], start=t == 0, stop=t == WT - 1)
            return nc.tensor.matmul(ps[:, 1, :], group[:], pair[:, 1, :], start=True, stop=True)

        def before0(link):
            for b in range(B):
                link(nc.vector.tensor_copy(by_channel[:, b],
                                           squares[:, b].unsqueeze(3).broadcast_to([P, WT, GROUPS, PER_GROUP])))
            link(nc.vector.memset(small["q"], 0.0))
            link(nc.vector.memset(small["sum"], 0.0))
            link(nc.vector.tensor_copy(pair[:, 1, :], spec_dc))
            link(ts(small["bias_dc"], small["q"], bias[:, 1:2], float(NPIX), ALU.add, ALU.mult))

        def after0(link):
            shift(link)
            for b in range(B):
                link(ts(low[:, b], low_part(spec, b), small["inv"][:, b:b + 1], None, ALU.mult))

        norm_moments(nc, sem, "norm0", products0, before0, after0, small, scale=1.0)
        window_energy(nc, sem, "energy0", spec, small["before"])
        layer0_products(nc, sem, a, low, fc_w, herm)

        with nc.Block() as block:
            @block.vector
            def _(ve):
                link = chained(ve, added0)
                link(tt(small["e0"], spec_dc, spec_dc, ALU.mult))
                link(ts(small["t"], small["q"], 0.0, None, ALU.mult))
                link(ts(small["t"], small["t"], bias[:, 0:1], float(NPIX), ALU.add, ALU.mult))
                link(tt(low[:, :, 0, 0, 0], low[:, :, 0, 0, 0], small["t"], ALU.add))
                for b in range(B):
                    link(tt(low_part(spec, b), low_part(spec, b), low[:, b], ALU.add))
        window_energy(nc, sem, "energy1", spec, small["after"])

        def products(ps):
            return nc.tensor.matmul(ps[:].rearrange("p t b -> p (t b)"), group[:], pair[:].rearrange("p t b -> p (t b)"),
                                    start=True, stop=True)

        def before1(link):
            e, d = pair[:, 0, :], pair[:, 1, :]
            link(tt(e, small["after"], small["before"], ALU.subtract))
            link(stt(out=e, in0=e, scalar=2.0, in1=small["e0"], op0=ALU.mult, op1=ALU.add))
            link(tt(small["t"], spec_dc, spec_dc, ALU.mult))
            link(tt(e, e, small["t"], ALU.subtract))
            link(nc.vector.tensor_copy(d, spec_dc))

        def after1(link):
            shift(link)
            link(ts(small["neg_inv"], small["inv"], -1.0, None, ALU.mult))
            link(nc.vector.tensor_copy(small["dc"], spec_dc))

        norm_moments(nc, sem, "norm1", products, before1, after1, small)
        layer1_products(nc, sem, a, spec, small["inv"], small["neg_inv"], herm, change)

        def before2(link):
            e, d = pair[:, 0, :], pair[:, 1, :]
            hd, t, u = small["added_dc"], small["t"], small["u"]
            link(nc.vector.tensor_copy(hd, spec_dc))
            link(nc.vector.tensor_reduce(e, change[:], AX.X, ALU.add))
            link(stt(out=t, in0=small["dc"], scalar=2.0, in1=hd, op0=ALU.mult, op1=ALU.add))
            link(tt(t, t, hd, ALU.mult))
            link(tt(e, e, t, ALU.subtract))
            link(tt(hd, hd, small["bias_dc"], ALU.add))
            link(stt(out=t, in0=small["dc"], scalar=2.0, in1=hd, op0=ALU.mult, op1=ALU.add))
            link(tt(t, t, hd, ALU.mult))
            link(stt(out=e, in0=e, scalar=2.0, in1=t, op0=ALU.mult, op1=ALU.add))
            link(tt(d, small["dc"], hd, ALU.add))

        def after2(link):
            for b in range(B):
                link(tt(low_part(spec, b), low_part(spec, b), low[:, b], ALU.add))
            link(tt(small["sum"], small["sum"], small["mean"], ALU.add))
            link(tt(spec_dc, spec_dc, small["bias_dc"], ALU.add))
            link(stt(out=spec_dc, in0=small["sum"], scalar=-float(NPIX), in1=spec_dc, op0=ALU.mult, op1=ALU.add))
            link(ts(small["skip"], small["inv"], bias[:, 2:3], 1.0, ALU.mult, ALU.add))
            link(ts(small["inv"], small["inv"], NORM_SCALE, None, ALU.mult))
            link(ts(spec_dc, spec_dc, 0.5, None, ALU.mult))

        norm_moments(nc, sem, "norm2", products, before2, after2, small)


def split_kernels(nc, sem, rev, parts, gains):
    with ExitStack() as ctx:
        def sb(name, shape, dt=F32):
            return ctx.enter_context(nc.sbuf_tensor(name, shape, dt))

        kernels, size = sb("kernels", [P, 2, LAGS]), sb("kernel_size", [P, 2, LAGS])
        two = sb("kernel_halves", [P, 2, 2, LAGS], F16)
        top, total, inv_top = sb("kernel_top", [P, 2]), sb("kernel_total", [P, 2]), sb("kernel_inv_top", [P, 2])
        loaded, steps, sized, put = sem("kernels_in"), sem("kernel_steps"), sem("kernels_sized"), sem("kernel_parts_out")
        block = ctx.enter_context(nc.Block())

        @block.sync
        def _(sp):
            sp.dma_start(kernels[:], rev.rearrange("a h m -> h a m")).then_inc(loaded, 16)
            sp.wait_ge(steps, 13)
            sp.dma_start(parts.rearrange("h p m -> h (p m)"), two[:].rearrange("h a p m -> h (a p m)")).then_inc(put, 16)
            sp.wait_ge(put, 16)

        @block.scalar
        def _(sc):
            sc.wait_ge(loaded, 16)
            nc.scalar.activation(size[:], kernels[:], ACT.Abs).then_inc(sized, 1)

        @block.vector
        def _(ve):
            link = chained(ve, steps)
            ts, stt = nc.vector.tensor_scalar, nc.vector.scalar_tensor_tensor
            ve.wait_ge(sized, 1)
            link(nc.vector.tensor_reduce(top[:], size[:], AX.X, ALU.max))
            link(nc.vector.tensor_reduce(total[:], size[:], AX.X, ALU.add))
            link(ts(top[:], top[:], TINY, None, ALU.max))
            link(ts(total[:], total[:], TINY, None, ALU.max))
            link(nc.vector.reciprocal(inv_top[:], top[:]))
            for axis in range(2):
                r = kernels[:, axis, :]
                link(ts(r, r, inv_top[:, axis:axis + 1], KERNEL_SCALE, ALU.mult, ALU.mult))
                link(nc.vector.tensor_copy(two[:, axis, 0, :], r))
                link(nc.vector.tensor_tensor(two[:, axis, 1, :], r, two[:, axis, 0, :], ALU.subtract))
            link(nc.vector.memset(gains, 0.0))
            link(stt(out=gains[:, 1:2], in0=total[:, 0:1], scalar=1 / (NORM_SCALE * KERNEL_SCALE),
                     in1=top[:, 1:2], op0=ALU.mult, op1=ALU.mult))
            link(nc.vector.reciprocal(total[:, 0:1], total[:, 0:1]))
            link(stt(out=gains[:, 0:1], in0=total[:, 0:1], scalar=1 / KERNEL_SCALE, in1=top[:, 0:1], op0=ALU.mult, op1=ALU.mult))


def modes_to_rows(nc, sem, a, spec, lhs):
    with ExitStack() as ctx:
        _, where = constants()
        i0, i_n = where["ident"]
        ident = ctx.enter_context(nc.sbuf_tensor("rows_ident", [P, P], F32))
        three = [ctx.enter_context(nc.sbuf_tensor(f"three{j}", [P, KX, 3, KY], F32)) for j in range(2)]
        rows = ctx.enter_context(nc.sbuf_tensor("mode_rows", [P, C, 2, KX], F32))
        ps = [ctx.enter_context(nc.psum_tensor(f"rows_ps{j}", [P, 4, C], F32)) for j in range(8)]
        table, made, turned = sem("ident_loaded"), sem("three_made"), sem("rows_turned")
        kept_ve, kept_sc, stored = sem("rows_kept_ve"), sem("rows_kept_sc"), sem("rows_stored")
        block = ctx.enter_context(nc.Block())
        banks = [(half, k) for half in range(2) for k in range(0, KX, 4)]
        each = len(banks) // 2

        @block.sync
        def _(sp):
            sp.dma_start(ident[:], a["table"][:, i0:i0 + i_n]).then_inc(table, 16)
            for b in range(B):
                sp.wait_ge(kept_ve, each * (b + 1))
                sp.wait_ge(kept_sc, each * (b + 1))
                sp.dma_start(lhs[:, :, b, :], rows[0:RI].rearrange("r c t k -> r c (t k)")).then_inc(stored, 16)
            sp.wait_ge(stored, 16 * B)

        @block.gpsimd
        def _(po):
            for b in range(B):
                if b >= 2:
                    po.wait_ge(turned, len(banks) * (b - 1))
                row = spec[:, b].rearrange("p k (r y) -> p k r y", r=2)
                nc.gpsimd.tensor_copy(three[b % 2][:, :, 0:2, :], row).then_inc(made, 1)
                nc.gpsimd.tensor_scalar(three[b % 2][:, :, 2, :], row[:, :, 0, :], -1.0, None, ALU.mult).then_inc(made, 1)

        @block.tensor
        def _(pe):
            pe.wait_ge(table, 16)
            for b in range(B):
                pe.wait_ge(made, 2 * (b + 1))
                for n, (half, k0) in enumerate(banks):
                    m = len(banks) * b + n
                    if m >= 8:
                        pe.wait_ge(kept_ve if m % 2 == 0 else kept_sc, (m - 8) // 2 + 1)
                    for k in range(4):
                        src = three[b % 2][:, k0 + k, half:half + 2, :].rearrange("p r y -> p (r y)")
                        last = nc.tensor.transpose(ps[m % 8][0:RI, k, :], src, ident[:])
                    last.then_inc(turned, 1)

        def keep(eng, copy, kept, odd):
            for b in range(B):
                if b:
                    eng.wait_ge(stored, 16 * b)
                for n in range(odd, len(banks), 2):
                    m = len(banks) * b + n
                    half, k0 = banks[n]
                    eng.wait_ge(turned, m + 1)
                    copy(rows[0:RI, :, half, k0:k0 + 4].rearrange("r c k -> r k c"), ps[m % 8][0:RI]).then_inc(kept, 1)

        @block.vector
        def _(ve):
            keep(ve, nc.vector.tensor_copy, kept_ve, 0)

        @block.scalar
        def _(sc):
            keep(sc, nc.scalar.copy, kept_sc, 1)


def spread(nc, sem, a, sources, outs):
    with ExitStack() as ctx:
        _, where = constants()
        tables = ctx.enter_context(nc.sbuf_tensor("spread_tables", [P, 2, P], F32))
        n_all = B * len(sources)
        diag = ctx.enter_context(nc.sbuf_tensor("spread_diag", [P, n_all, P], F32))
        ps = [ctx.enter_context(nc.psum_tensor(f"spread_ps{k}", [P, B, C], F32)) for k in range(len(sources))]
        loaded, made, summed, kept = (sem(f"spread_{n}") for n in ("loaded", "made", "summed", "kept"))
        block = ctx.enter_context(nc.Block())

        @block.sync
        def _(sp):
            for j, n in enumerate(("ident", "ones")):
                at, w = where[n]
                sp.dma_start(tables[:, j, :], a["table"][:, at:at + w]).then_inc(loaded, 16)

        @block.vector
        def _(ve):
            ve.wait_ge(loaded, 32)
            for k, s in enumerate(sources):
                for b in range(B):
                    nc.vector.tensor_scalar(diag[:, B * k + b, :], tables[:, 0, :], s[:, b:b + 1], None, ALU.mult)\
                        .then_inc(made, 1)
            for k, out in enumerate(outs):
                ve.wait_ge(summed, k + 1)
                nc.vector.tensor_copy(out, ps[k][:]).then_inc(kept, 1)

        @block.tensor
        def _(pe):
            pe.wait_ge(made, n_all)
            for k in range(len(sources)):
                for b in range(B):
                    last = nc.tensor.matmul(ps[k][:, b, :], tables[:, 1, :], diag[:, B * k + b, :], start=True, stop=True)
                last.then_inc(summed, 1)


def toeplitz_layer(nc, sem, a, x, lhs, kernel_parts, x3, every, sums):
    with ExitStack() as ctx:
        def sb(name, shape, dt=F32):
            return ctx.enter_context(nc.sbuf_tensor(name, shape, dt))

        def banks(name):
            return [ctx.enter_context(nc.psum_tensor(f"{name}{j}", [P, 2, W], F32)) for j in range(2)]

        _, where = constants()
        (r0, rn), (c0, cn) = where["inv_y"], where["inv_x"]
        inv_y, inv_x = sb("inv_y", [P, W]), sb("inv_x", [P, H])
        SETS, NIMG = 2, 2 * B
        TURNS = C // SETS
        xin = [sb(f"xin{j}", [P, B, HT, W]) for j in range(SETS)]
        xout = [sb(f"xout{j}", [P, B, HT, W]) for j in range(SETS)]
        toep = [sb(f"toeplitz{j}", [P, 4, LAGS - P], F16) for j in range(SETS)]
        modes = [sb(f"channel_modes{j}", [P, B, 2 * KX]) for j in range(SETS)]
        rows = [sb(f"rows{j}", [P, W]) for j in range(2)]
        v = [sb(f"v{j}", [P, HT, W]) for j in range(4)]
        v_skip = [sb(f"v_skip{j}", [P, HT, W]) for j in range(2)]
        u = [sb(f"u{j}", [P, 2, HT, W], F16) for j in range(2)]
        mid = [sb(f"mid{j}", [P, 2, WT, H], F16) for j in range(2)]
        scalars = [sb(f"channel_scalars{j}", [P, 3 * B]) for j in range(SETS)]
        INV, SKIP, GAIN = 0, B, 2 * B
        junk = [sb(f"conv_junk{j}", [P, HT * W]) for j in range(2)]
        acc = sb("conv_acc", [P, 2, NIMG])
        ps_r, ps_f, ps_m, ps_y = (banks(n) for n in ("rows_ps_", "field_ps", "mid_ps", "y_ps"))
        tables = sem("inv_tables")
        modes_in, x_in, toep_in, stored = (
            [sem(f"{n}{j}") for j in range(SETS)] for n in ("modes_in", "x_in", "toep_in", "x3_stored"))
        scalars_in, skipped, u_high, u_kept, mid_high = (
            sem(n) for n in ("channel_scalars", "v_skipped", "u_high", "u_kept", "mid_high"))
        rows_made, rows_kept, field_made, v_kept, first, mid_kept, second, x3_kept, squared, sums_kept = (
            sem(n) for n in ("rows_made", "rows_kept", "field_made", "v_kept", "toeplitz1", "mid_kept",
                             "toeplitz2", "x3_kept", "x3_squared", "x3_sums_kept"))
        block = ctx.enter_context(nc.Block())
        hankel = bass.AP(kernel_parts.tensor, kernel_parts.offset, [[4 * LAGS, C], [1, P], [LAGS, 4], [1, LAGS - P]])
        PRODUCTS = ((0, 0), (0, 1), (1, 0))

        def matrix_rows(j, axis, part, t):
            return toep[j][:, 2 * axis + part, P * t:P * t + H][:, ::-1]

        def image(i, k):
            return i * NIMG + k

        @block.sync
        def _(sp):
            sp.dma_start(inv_y[:], a["table"][:, r0:r0 + rn]).then_inc(tables, 16)
            sp.dma_start(inv_x[:], a["table"][:, c0:c0 + cn]).then_inc(tables, 16)
            def load_modes(i, j):
                sp.dma_start(modes[j][0:RI], lhs[:, bass.ds(i * SETS + j, 1)].rearrange("r o b k -> r (o b) k"))\
                    .then_inc(modes_in[j], 16)

            def load_x(i, j):
                for b in range(B):
                    src = x[b, bass.ds(i * SETS + j, 1)].rearrange("o (t p) w -> p (o t) w", p=P)
                    sp.dma_start(xin[j][:, b], src).then_inc(x_in[j], 16)

            def load_kernels(i, j):
                sp.dma_start(toep[j][:], hankel[bass.ds(i * SETS + j, 1)].rearrange("o p k j -> p (o k) j"))\
                    .then_inc(toep_in[j], 16)

            def store(i, j):
                sp.wait_ge(x3_kept, done(image(i, B * j + B - 1)))
                for b in range(B):
                    dst = x3[b, bass.ds(i * SETS + j, 1)].rearrange("o (t p) w -> p (o t) w", p=P)
                    sp.dma_start(dst, xout[j][:, b]).then_inc(stored[j], 16)

            for j in range(SETS):
                sp.sem_inc(stored[j], 16 * B)
                load_modes(0, j)
                load_x(0, j)
                load_kernels(0, j)
            with sp.Fori(0, TURNS - 1) as i:
                for j in range(SETS):
                    last = image(i, B * j + B - 1)
                    sp.wait_ge(rows_made, done(last))
                    load_modes(i + 1, j)
                    sp.wait_ge(v_kept, done(last))
                    load_x(i + 1, j)
                    sp.wait_ge(second, done(last))
                    load_kernels(i + 1, j)
                    store(i, j)
            for j in range(SETS):
                store(TURNS - 1, j)
            for j in range(SETS):
                sp.wait_ge(stored[j], 16 * B * (TURNS + 1))

        @block.gpsimd
        def _(po):
            start(po, skipped)

            def skip(i, k):
                n = image(i, k)
                po.wait_ge(u_kept, done(n))
                po.wait_ge(x3_kept, reusable(n, 2))
                at = SKIP + k % B
                by = scalars[k // B][:, at:at + 1].to_broadcast([P, HT * W])
                nc.gpsimd.tensor_tensor(v_skip[k % 2][:].rearrange("p t w -> p (t w)"),
                                        v[k % 4][:].rearrange("p t w -> p (t w)"), by, ALU.mult).then_inc(skipped, 1)

            side_by_side(po, TURNS, NIMG, [(1, skip)])

        @block.tensor
        def _(pe):
            start(pe, rows_made, field_made, first, second)
            pe.wait_ge(tables, 32)

            def modes_by_ky(i, k):
                j, b, n = k // B, k % B, image(i, k)
                if b == 0:
                    pe.wait_ge(modes_in[j], i * 16 + 16)
                pe.wait_ge(rows_kept, reusable(n, 2))
                nc.tensor.matmul(ps_r[k % 2][:, 0, :], modes[j][0:RI, b, :], inv_y[0:RI, :], start=True, stop=True)\
                    .then_inc(rows_made, 1)

            def modes_by_kx(i, k):
                n = image(i, k)
                pe.wait_ge(rows_kept, done(n))
                pe.wait_ge(v_kept, reusable(n, 2))
                for t in range(HT):
                    last = nc.tensor.matmul(ps_f[k % 2][:, t, :], inv_x[:, P * t:P * (t + 1)], rows[k % 2][:],
                                            start=True, stop=True)
                last.then_inc(field_made, 1)

            def along_h(i, k):
                j, n = k // B, image(i, k)
                if k % B == 0:
                    pe.wait_ge(toep_in[j], i * 16 + 16)
                pe.wait_ge(u_kept, done(n))
                pe.wait_ge(mid_kept, reusable(n, 2))
                for m in range(WT):
                    for t in range(HT):
                        for f, g in PRODUCTS:
                            last = nc.tensor.matmul(ps_m[k % 2][:, m, :], u[k % 2][:, f, t, P * m:P * (m + 1)],
                                                    matrix_rows(j, 0, g, t), start=t == 0 and (f, g) == (0, 0),
                                                    stop=t == HT - 1 and f == 1)
                last.then_inc(first, 1)

            def along_w(i, k):
                j, n = k // B, image(i, k)
                pe.wait_ge(mid_kept, done(n))
                pe.wait_ge(x3_kept, reusable(n, 2))
                for m in range(HT):
                    for t in range(WT):
                        for f, g in PRODUCTS:
                            last = nc.tensor.matmul(ps_y[k % 2][:, m, :], mid[k % 2][:, f, t, P * m:P * (m + 1)],
                                                    matrix_rows(j, 1, g, t), start=t == 0 and (f, g) == (0, 0),
                                                    stop=t == WT - 1 and f == 1)
                last.then_inc(second, 1)

            side_by_side(pe, TURNS, NIMG, [(4, modes_by_ky), (3, modes_by_kx), (1, along_h), (0, along_w)])

        @block.scalar
        def _(sc):
            start(sc, rows_kept, u_high, mid_high, squared)

            def keep_rows(i, k):
                n = image(i, k)
                sc.wait_ge(rows_made, done(n))
                sc.wait_ge(field_made, reusable(n, 2))
                nc.scalar.copy(rows[k % 2][:], ps_r[k % 2][:, 0, :]).then_inc(rows_kept, 1)

            def split_v(i, k):
                n = image(i, k)
                if k % B == 0:
                    sc.wait_ge(scalars_in, done(i * SETS + k // B))
                sc.wait_ge(v_kept, done(n))
                sc.wait_ge(first, reusable(n, 2))
                scale = scalars[k // B][:, INV + k % B:INV + k % B + 1]
                nc.scalar.activation(u[k % 2][:, 0], v[k % 4][:], ACT.Copy, scale=scale).then_inc(u_high, 1)

            def keep_mid(i, k):
                n = image(i, k)
                sc.wait_ge(first, done(n))
                sc.wait_ge(second, reusable(n, 2))
                scale = scalars[k // B][:, GAIN:GAIN + 1]
                nc.scalar.activation(mid[k % 2][:, 0], ps_m[k % 2][:], ACT.Copy, scale=scale).then_inc(mid_high, 1)

            def square(i, k):
                n = image(i, k)
                sc.wait_ge(x3_kept, done(n))
                sc.wait_ge(squared, reusable(n, 2))
                sc.wait_ge(sums_kept, reusable(i * SETS + k // B, SETS))
                nc.scalar.activation(junk[k % 2][:], xout[k // B][:, k % B].rearrange("p t w -> p (t w)"), ACT.Square,
                                     accum_out=acc[:, 1, k:k + 1]).then_inc(squared, 1)

            side_by_side(sc, TURNS, NIMG, [(4, keep_rows), (3, split_v), (1, keep_mid), (0, square)])

        @block.vector
        def _(ve):
            start(ve, scalars_in, v_kept, u_kept, mid_kept, x3_kept, sums_kept)

            def add_field(i, k):
                j, b, n = k // B, k % B, image(i, k)
                if b == 0:
                    ve.wait_ge(x3_kept, reusable(n, NIMG - (B - 1)))
                    nc.vector.tensor_scalar(scalars[j][:], every[:, :, :, bass.ds(i * SETS + j, 1)]
                                            .rearrange("p s b o -> p (s b o)"), 1.0, None, ALU.mult)\
                        .then_inc(scalars_in, 1)
                    ve.wait_ge(x_in[j], i * (16 * B) + 16 * B)
                ve.wait_ge(field_made, done(n))
                ve.wait_ge(skipped, reusable(n, 4))
                nc.vector.tensor_tensor(v[k % 4][:], ps_f[k % 2][:], xin[j][:, b], ALU.add).then_inc(v_kept, 1)

            def low_of_v(i, k):
                n = image(i, k)
                ve.wait_ge(u_high, done(n))
                scale = scalars[k // B][:, INV + k % B:INV + k % B + 1]
                nc.vector.scalar_tensor_tensor(out=u[k % 2][:, 1], in0=v[k % 4][:], scalar=scale, in1=u[k % 2][:, 0],
                                               op0=ALU.mult, op1=ALU.subtract).then_inc(u_kept, 1)

            def low_of_mid(i, k):
                n = image(i, k)
                ve.wait_ge(mid_high, done(n))
                scale = scalars[k // B][:, GAIN:GAIN + 1]
                nc.vector.scalar_tensor_tensor(out=mid[k % 2][:, 1], in0=ps_m[k % 2][:], scalar=scale,
                                               in1=mid[k % 2][:, 0], op0=ALU.mult, op1=ALU.subtract).then_inc(mid_kept, 1)

            def add_up(i, k):
                j, b, n = k // B, k % B, image(i, k)
                if b == 0:
                    ve.wait_ge(stored[j], i * (16 * B) + 16 * B)
                ve.wait_ge(second, done(n))
                ve.wait_ge(sums_kept, reusable(i * SETS + j, SETS))
                ve.wait_ge(skipped, done(n))
                nc.vector.scalar_tensor_tensor(out=xout[j][:, b], in0=ps_y[k % 2][:],
                                               scalar=scalars[j][:, GAIN + 1:GAIN + 2], in1=v_skip[k % 2][:],
                                               op0=ALU.mult, op1=ALU.add, accum_out=acc[:, 0, k:k + 1])\
                    .then_inc(x3_kept, 1)
                if b == B - 1:
                    ve.wait_ge(x3_kept, done(n))
                    ve.wait_ge(squared, done(n))
                    nc.vector.tensor_scalar(sums[:, :, :, bass.ds(i * SETS + j, 1)].rearrange("p s b o -> p s (b o)"),
                                            acc[:, :, B * j:B * (j + 1)], 1.0, None, ALU.mult).then_inc(sums_kept, 1)

            side_by_side(ve, TURNS, NIMG, [(3, add_field), (2, low_of_v), (1, low_of_mid), (0, add_up)])


def attention_matrices(nc, sem, a, x3, sums, mean_sum, w_q, w_den, w_out, biases):
    with ExitStack() as ctx:
        def sb(name, shape):
            return ctx.enter_context(nc.sbuf_tensor(name, shape, F32))

        _, where = constants()
        masks = sb("att_tables", [P, 2, P])
        weights = sb("att_weights", [P, 4, C])
        vectors = sb("att_vectors", [P, 2])
        kv_row = sb("kv_b_row", [1, 2 * C])
        w_kv, kv_bias = sb("w_kv", [P, B, 2 * C]), sb("kv_bias", [P, B, 2 * C])
        beta_wide = sb("beta_wide", [P, B, P])
        by_group = sb("sums_by_group", [P, 2 * B, GROUPS])
        by_channel = sb("sums_by_channel", [P, 2 * B, GROUPS, PER_GROUP])
        names = ("q", "t", "u", "mean", "inv", "beta")
        rows = sb("att_small", [P, len(names), B])
        small = {n: rows[:, j, :] for j, n in enumerate(names)}
        loaded, summed, kept = (sem(f"att_{n}") for n in ("tables_in", "bias_summed", "bias_kept"))
        ts, tt = nc.vector.tensor_scalar, nc.vector.tensor_tensor
        same_head, ones = masks[:, 0, :], masks[:, 1, :]
        kv_w = weights[:, 1:3, :].rearrange("c t o -> c (t o)")

        with nc.Block() as block:
            @block.sync
            def _(sp):
                for j, n in enumerate(("same_head", "ones")):
                    at, w = where[n]
                    sp.dma_start(masks[:, j, :], a["table"][:, at:at + w]).then_inc(loaded, 16)
                sp.dma_start(weights[:, 0, :], a["q_wT"]).then_inc(loaded, 16)
                sp.dma_start(kv_w, a["kv_wT"]).then_inc(loaded, 16)
                sp.dma_start(weights[:, 3, :], a["proj_wT"]).then_inc(loaded, 16)
                sp.dma_start(vectors[:, 0:1], a["q_b"].rearrange("(c o) -> c o", o=1)).then_inc(loaded, 16)
                sp.dma_start(vectors[:, 1:2], a["proj_b"].rearrange("(c o) -> c o", o=1)).then_inc(loaded, 16)
                sp.dma_start(kv_row[:], a["kv_b"].rearrange("(p o) -> p o", p=1)).then_inc(loaded, 16)
                sp.wait_ge(loaded, 16 * 8)

        def products(ps):
            for s, row in ((1, 0), (0, 1)):
                for b in range(B):
                    last = nc.tensor.matmul(ps[:, row, b:b + 1],
                                            by_channel[:, B * s + b, :, :].rearrange("p g n -> p (g n)"), ones[:, 0:1],
                                            start=True, stop=True)
            return last

        def before(link):
            link(nc.vector.tensor_reduce(by_group[:], sums[:].rearrange("p s b (g n) -> p (s b) g n", n=PER_GROUP),
                                         AX.X, ALU.add))
            link(nc.vector.tensor_copy(by_channel[:], by_group[:].unsqueeze(3).broadcast_to([P, 2 * B, GROUPS, PER_GROUP])))
            link(nc.vector.memset(small["q"], 0.0))

        def after(link):
            link(nc.vector.scalar_tensor_tensor(out=small["beta"], in0=small["mean"], scalar=-1.0, in1=small["inv"],
                                                op0=ALU.mult, op1=ALU.mult))
            link(nc.vector.tensor_copy(beta_wide[:], small["beta"].unsqueeze(2).broadcast_to([P, B, P])))
            for b in range(B):
                link(ts(w_q[:, b, :], weights[:, 0, :], small["inv"][:, b:b + 1], None, ALU.mult))
                link(ts(w_kv[:, b, :], kv_w, small["inv"][:, b:b + 1], None, ALU.mult))
            link(ts(biases[:, 1, :], mean_sum, vectors[:, 1:2], None, ALU.add))

        norm_moments(nc, sem, "norm3", products, before, after, small, scale=1.0)

        with ExitStack() as scope:
            ps_q = scope.enter_context(nc.psum_tensor("q_bias_ps", [P, B], F32))
            ps_kv = [scope.enter_context(nc.psum_tensor(f"kv_bias_ps{j}", [P, 2 * C], F32)) for j in range(2)]
            block = scope.enter_context(nc.Block())

            @block.tensor
            def _(pe):
                nc.tensor.matmul(ps_q[:], weights[:, 0, :], small["beta"], start=True, stop=True).then_inc(summed, 1)
                for b in range(B):
                    if b >= 2:
                        pe.wait_ge(kept, b)
                    nc.tensor.matmul(ps_kv[b % 2][:], beta_wide[:, b, :], kv_w, start=True, stop=False)
                    nc.tensor.matmul(ps_kv[b % 2][:], ones[0:1, :], kv_row[:], start=False, stop=True).then_inc(summed, 1)

            @block.vector
            def _(ve):
                ve.wait_ge(summed, 1)
                ts(biases[:, 0, :], ps_q[:], vectors[:, 0:1], None, ALU.add).then_inc(kept, 1)
                for b in range(B):
                    ve.wait_ge(summed, b + 2)
                    nc.vector.tensor_copy(kv_bias[:, b, :], ps_kv[b % 2][:]).then_inc(kept, 1)

        SIDE = H // SUB
        ROWS, NBUF = 8, 4
        CHUNKS, TILES = SIDE // ROWS, ROWS * SIDE // P
        NT = CHUNKS * TILES
        raw = [sb(f"sample_rows{j}", [P, ROWS, W]) for j in range(NBUF)]
        xs = [sb(f"samples{j}", [P, ROWS * SIDE]) for j in range(NBUF)]
        kv = [sb(f"kv{j}", [P, 2 * C]) for j in range(4)]
        e, r, key = ([sb(f"{n}{j}", [P, C]) for j in range(4)] for n in ("key_exp", "key_relu", "key"))
        kv_masked = sb("kv_masked", [P, C])
        ps_t = [ctx.enter_context(nc.psum_tensor(f"kv_ps{j}", [P, 2 * C], F32)) for j in range(3)]
        ps_kv, ps_k, ps_o = (ctx.enter_context(nc.psum_tensor(n, [P, C], F32)) for n in ("kv_sum_ps", "k_sum_ps", "w_out_ps"))
        rows_in = [sem(f"sample_rows_in{j}") for j in range(NBUF)]
        picked, made, biased, exped, keyed, added, matrices, folded, relued = (
            sem(n) for n in ("samples_picked", "kv_made", "kv_biased", "key_exped", "keys_made", "kv_added",
                             "kv_matrices", "kv_folded", "key_relued"))
        block = ctx.enter_context(nc.Block())
        sampled = x3.rearrange("b c (r s) w -> b c r s w", s=SUB)

        def tile(i, k):
            return i * NT + k

        @block.sync
        def _(sp):
            with sp.Fori(0, B) as i:
                for n in range(CHUNKS):
                    sp.wait_ge(picked, reusable(i * CHUNKS + n, NBUF))
                    src = sampled[bass.ds(i, 1), :, ROWS * n:ROWS * (n + 1), SUB0, :].rearrange("o c r w -> c (o r) w")
                    sp.dma_start(raw[n % NBUF][:], src).then_inc(rows_in[n % NBUF], 16)

        @block.tensor
        def _(pe):
            start(pe, made, made, added, folded)

            def keys_values(i, k):
                n = tile(i, k)
                pe.wait_ge(picked, done(i * CHUNKS + k // TILES))
                pe.wait_ge(biased, reusable(n, 2))
                nc.tensor.matmul(ps_t[k % 2][:], xs[k // TILES % NBUF][:, P * (k % TILES):P * (k % TILES + 1)],
                                 w_kv[:, bass.ds(i, 1), :].rearrange("p o c -> p (o c)"), start=True, stop=True)\
                    .then_inc(made, 1)

            def sum_up(i, k):
                n = tile(i, k)
                pe.wait_ge(keyed, done(n))
                if k == 0:
                    pe.wait_ge(matrices, reusable(i, 1))
                first, last = k == 0, k == NT - 1
                nc.tensor.matmul(ps_kv[:], kv[k % 4][:, C:2 * C], key[k % 4][:], start=first, stop=last)
                nc.tensor.matmul(ps_k[:], key[k % 4][:], ones, start=first, stop=last).then_inc(added, 1)
                if last:
                    pe.wait_ge(matrices, done(i))
                    nc.tensor.matmul(ps_o[:], kv_masked[:], weights[:, 3, :], start=True, stop=True).then_inc(folded, 1)

            side_by_side(pe, B, NT, [(2, keys_values), (0, sum_up)])

        @block.scalar
        def _(sc):
            start(sc, exped, picked)

            def pick(i, k):
                n = k // TILES
                if k % TILES == 0:
                    sc.wait_ge(rows_in[n % NBUF], (i * (CHUNKS // NBUF) + n // NBUF) * 16 + 16)
                    sc.wait_ge(made, done(tile(i, TILES * n + TILES - 1)) + AHEAD - TILES * NBUF)
                    nc.scalar.copy(xs[n % NBUF][:].rearrange("p (r s) -> p r s", r=ROWS),
                                   raw[n % NBUF][:, :, SUB0::SUB]).then_inc(picked, 1)

            def exponentials(i, k):
                n = tile(i, k)
                sc.wait_ge(biased, done(n))
                sc.wait_ge(keyed, reusable(n, 4))
                nc.scalar.activation(e[k % 4][:], kv[k % 4][:, 0:C], ACT.Exp).then_inc(exped, 1)

            side_by_side(sc, B, NT, [(6, pick), (0, exponentials)])

        @block.vector
        def _(ve):
            start(ve, biased, relued, keyed, matrices)

            def add_bias(i, k):
                n = tile(i, k)
                ve.wait_ge(made, done(n) + AHEAD)
                ve.wait_ge(added, reusable(n, 4))
                tt(kv[k % 4][:], ps_t[k % 2][:], kv_bias[:, bass.ds(i, 1), :].rearrange("p o c -> p (o c)"), ALU.add)\
                    .then_inc(biased, 1)
                ve.wait_ge(biased, done(n))
                ve.wait_ge(keyed, reusable(n, 4))
                ts(r[k % 4][:], kv[k % 4][:, 0:C], 0.0, None, ALU.max).then_inc(relued, 1)

            def make_keys(i, k):
                n = tile(i, k)
                ve.wait_ge(exped, done(n))
                ve.wait_ge(relued, done(n))
                nc.vector.scalar_tensor_tensor(out=key[k % 4][:], in0=e[k % 4][:], scalar=1.0, in1=r[k % 4][:],
                                               op0=ALU.min, op1=ALU.add).then_inc(keyed, 1)
                if k == NT - 1:
                    ve.wait_ge(added, done(n))
                    ve.wait_ge(folded, reusable(i, 1))
                    tt(w_den[:, bass.ds(i, 1), :].rearrange("p o c -> p (o c)"), ps_k[:], same_head, ALU.mult)
                    tt(kv_masked[:], ps_kv[:], same_head, ALU.mult).then_inc(matrices, 1)
                    ve.wait_ge(folded, done(i))
                    ts(w_out[:, bass.ds(i, 1), :].rearrange("p o c -> p (o c)"), ps_o[:], 1.0, None, ALU.mult)

            side_by_side(ve, B, NT, [(1, add_bias), (0, make_keys)])


def attend(nc, sem, x3, out, w_q, w_den, w_out, biases):
    with ExitStack() as ctx:
        def sb(name, shape, n):
            return [ctx.enter_context(nc.sbuf_tensor(f"{name}{j}", shape, F32)) for j in range(n)]

        T, SETS, PER = 512, 4, 4
        NT = SETS * PER
        TURNS = NPIX // (T * NT)
        xin, xout = sb("att_in", [P, PER * T], SETS), sb("att_out", [P, PER * T], SETS)
        e, r, q = sb("q_exp", [P, T], 4), sb("q_relu", [P, T], 4), sb("q", [P, T], 4)
        log_den, inv_den, qz = sb("log_den", [P, T], 2), sb("inv_den", [P, T], 2), sb("qz", [P, T], 4)
        eps = sb("att_eps", [P, 1], 1)[0]
        ps_q, ps_d, ps_o = ([ctx.enter_context(nc.psum_tensor(f"{n}{j}", [P, T], F32)) for j in range(2)]
                            for n in ("q_ps", "den_ps", "out_ps"))
        x_in, stored = ([sem(f"{n}{j}") for j in range(SETS)] for n in ("att_x_in", "att_stored"))
        q_made, exped, relued, q_kept, den_made, logged, inverted, scaled, out_made, out_kept, eps_set = (
            sem(f"att_{n}") for n in ("q_made", "q_exped", "q_relued", "q_kept", "den_made", "logged", "inverted", "scaled",
                                      "out_made", "out_kept", "eps_set"))
        block = ctx.enter_context(nc.Block())
        px = PER * T

        def tile(b, i, k):
            return b * (TURNS * NT) + i * NT + k

        @block.sync
        def _(sp):
            for j in range(SETS):
                sp.sem_inc(stored[j], 16)

            def load(b, i, j):
                src = x3[b].rearrange("c h w -> c (h w)")[:, bass.ds(i * (SETS * px) + j * px, px)]
                sp.dma_start(xin[j][:], src).then_inc(x_in[j], 16)

            def store(b, i, j):
                sp.wait_ge(out_kept, done(tile(b, i, PER * j + PER - 1)))
                dst = out[b].rearrange("c h w -> c (h w)")[:, bass.ds(i * (SETS * px) + j * px, px)]
                sp.dma_start(dst, xout[j][:]).then_inc(stored[j], 16)

            for j in range(SETS):
                load(0, 0, j)
            for b in range(B):
                with sp.Fori(0, TURNS - 1) as i:
                    for j in range(SETS):
                        store(b, i, j)
                        load(b, i + 1, j)
                for j in range(SETS):
                    store(b, TURNS - 1, j)
                    if b + 1 < B:
                        load(b + 1, 0, j)
            for j in range(SETS):
                sp.wait_ge(stored[j], 16 + 16 * B * TURNS)

        @block.tensor
        def _(pe):
            start(pe, q_made, den_made, out_made)
            for b in range(B):
                def queries(i, k):
                    if k % PER == 0:
                        pe.wait_ge(x_in[k // PER], (i + b * TURNS) * 16 + 16)
                    pe.wait_ge(relued, reusable(tile(b, i, k), 2))
                    nc.tensor.matmul(ps_q[k % 2][:], w_q[:, b, :], xin[k // PER][:, T * (k % PER):T * (k % PER + 1)],
                                     start=True, stop=True).then_inc(q_made, 1)

                def denominators(i, k):
                    pe.wait_ge(q_kept, done(tile(b, i, k)))
                    pe.wait_ge(logged, reusable(tile(b, i, k), 2))
                    nc.tensor.matmul(ps_d[k % 2][:], w_den[:, b, :], q[k % 4][:], start=True, stop=True)\
                        .then_inc(den_made, 1)

                def outputs(i, k):
                    pe.wait_ge(scaled, done(tile(b, i, k)))
                    pe.wait_ge(out_kept, reusable(tile(b, i, k), 2))
                    nc.tensor.matmul(ps_o[k % 2][:], w_out[:, b, :], qz[k % 4][:], start=True, stop=True)\
                        .then_inc(out_made, 1)

                side_by_side(pe, TURNS, NT, [(6, queries), (4, denominators), (0, outputs)])

        @block.scalar
        def _(sc):
            sc.preload_act_table_set("natural_log_exp_and_others")
            start(sc, exped, logged, inverted)
            sc.wait_ge(eps_set, 1)
            for b in range(B):
                def exponential(i, k):
                    n = tile(b, i, k)
                    sc.wait_ge(q_made, done(n))
                    sc.wait_ge(q_kept, reusable(n, 4))
                    nc.scalar.activation(e[k % 4][:], ps_q[k % 2][:], ACT.Exp, bias=biases[:, 0, b:b + 1]).then_inc(exped, 1)

                def invert(i, k):
                    n = tile(b, i, k)
                    sc.wait_ge(den_made, done(n))
                    sc.wait_ge(inverted, reusable(n, 2))
                    nc.scalar.activation(log_den[k % 2][:], ps_d[k % 2][:], ACT.Ln, bias=eps[:]).then_inc(logged, 1)
                    sc.wait_ge(logged, done(n))
                    sc.wait_ge(scaled, reusable(n, 2))
                    nc.scalar.activation(inv_den[k % 2][:], log_den[k % 2][:], ACT.Exp, scale=-1.0).then_inc(inverted, 1)

                side_by_side(sc, TURNS, NT, [(6, exponential), (4, invert)])

        @block.gpsimd
        def _(po):
            start(po, scaled)
            nc.gpsimd.memset(eps[:], EPS_ATT).then_inc(eps_set, 1)
            for b in range(B):
                def scale(i, k):
                    n = tile(b, i, k)
                    po.wait_ge(inverted, done(n))
                    po.wait_ge(out_made, reusable(n, 4))
                    nc.gpsimd.tensor_tensor(qz[k % 4][:], q[k % 4][:], inv_den[k % 2][:], ALU.mult).then_inc(scaled, 1)

                side_by_side(po, TURNS, NT, [(2, scale)])

        @block.vector
        def _(ve):
            start(ve, relued, q_kept, out_kept)
            for b in range(B):
                def relu(i, k):
                    n = tile(b, i, k)
                    ve.wait_ge(exped, done(n))
                    ve.wait_ge(q_kept, reusable(n, 4))
                    nc.vector.tensor_scalar(r[k % 4][:], ps_q[k % 2][:], biases[:, 0, b:b + 1], 0.0, ALU.add, ALU.max)\
                        .then_inc(relued, 1)

                def finish_map(i, k):
                    n = tile(b, i, k)
                    ve.wait_ge(relued, done(n))
                    ve.wait_ge(scaled, reusable(n, 4))
                    ve.wait_ge(den_made, reusable(n, 4))
                    nc.vector.scalar_tensor_tensor(out=q[k % 4][:], in0=e[k % 4][:], scalar=1.0, in1=r[k % 4][:],
                                                   op0=ALU.min, op1=ALU.add).then_inc(q_kept, 1)

                def add_up(i, k):
                    n, s = tile(b, i, k), slice(T * (k % PER), T * (k % PER + 1))
                    if k % PER == 0:
                        ve.wait_ge(stored[k // PER], (i + b * TURNS) * 16 + 16)
                    ve.wait_ge(out_made, done(n))
                    nc.vector.scalar_tensor_tensor(out=xout[k // PER][:, s], in0=ps_o[k % 2][:],
                                                   scalar=biases[:, 1, b:b + 1], in1=xin[k // PER][:, s],
                                                   op0=ALU.add, op1=ALU.add).then_inc(out_kept, 1)

                side_by_side(ve, TURNS, NT, [(6, relu), (5, finish_map), (0, add_up)])


def conv_stack(nc, a, out):
    with ExitStack() as top:
        def sem(name):
            return top.enter_context(nc.semaphore(name))

        def sb(name, shape):
            return top.enter_context(nc.sbuf_tensor(name, shape, F32))

        def dram(name, shape):
            return nc.dram_tensor(name, shape, F32, kind="Internal").ap()

        x, x3 = a["x"], dram("x3", [B, C, H, W])
        rev, lhs = dram("reversed_kernels", [2, C, LAGS]), dram("mode_rows_all", [RI, C, B, 2 * KX])
        kernel_parts = nc.dram_tensor("kernel_parts", [C, 4, LAGS], F16, kind="Internal").ap()
        gains = sb("kernel_gains", [P, B])
        rows = sb("norm2_rows", [P, 3, B])
        norm2 = {n: rows[:, j, :] for j, n in enumerate(("sum", "inv", "skip"))}
        sums = sb("x3_sums", [P, 2, B, C])

        ssm_kernels(nc, sem, a, rev)
        split_kernels(nc, sem, rev, kernel_parts, gains[:])
        with nc.sbuf_tensor("modes", [P, B, KX, RI], F32) as spec:
            with nc.sbuf_tensor("x_squares", [P, B, WT, GROUPS], F32) as squares:
                spectrum(nc, sem, x, spec, squares, a)
                modes_layers(nc, sem, a, spec, squares, norm2)
            modes_to_rows(nc, sem, a, spec, lhs)
        with nc.sbuf_tensor("norm2_all", [P, 3, B, C], F32) as every:
            spread(nc, sem, a, [norm2["inv"], norm2["skip"], gains[:]], [every[:, j] for j in range(3)])
            toeplitz_layer(nc, sem, a, x, lhs, kernel_parts, x3, every, sums)
        w_q, w_den, w_out = sb("w_q", [P, B, C]), sb("w_den", [P, B, C]), sb("w_out", [P, B, C])
        biases = sb("layer3_biases", [P, 2, B])
        attention_matrices(nc, sem, a, x3, sums, norm2["sum"], w_q, w_den, w_out, biases)
        attend(nc, sem, x3, out, w_q, w_den, w_out, biases)


def _laid_out(given):
    def t(name, *axes):
        return np.ascontiguousarray(np.transpose(given[name], axes or None))

    arrays = {
        "x": given["x"], "table": constants()[0],
        "w0": np.ascontiguousarray(np.transpose(given["L0_conv_weight"][0], (2, 0, 3, 1))),
        "fc_wT": t("L0_conv_fc_w"), "fc_b": given["L0_conv_fc_b"],
        "w1_re": t("L1_conv_weight_real", 3, 0, 1, 4, 2).reshape(KX, C, KY, C // 4),
        "w1_im": t("L1_conv_weight_imag", 3, 0, 1, 4, 2).reshape(KX, C, KY, C // 4),
        "bias1": given["L1_conv_bias"], "D": given["L2_conv_D"],
        "q_wT": t("L3_conv_q_w"), "kv_wT": t("L3_conv_kv_w"), "proj_wT": t("L3_conv_proj_w"),
        "q_b": given["L3_conv_q_b"], "kv_b": given["L3_conv_kv_b"], "proj_b": given["L3_conv_proj_b"],
    }
    for axis in range(2):
        arrays[f"log_dt{axis}"] = given[f"L2_conv_log_dt{axis}"]
        for n in ("A_re", "A_im"):
            arrays[f"{n}{axis}"] = t(f"L2_conv_{n}{axis}")
        for n in ("C_re", "C_im"):
            arrays[f"{n}{axis}"] = t(f"L2_conv_{n}{axis}", 2, 0, 1)
    return {n: np.ascontiguousarray(v) for n, v in arrays.items()}


def kernel(**inputs):
    import concourse.bacc as bacc
    from concourse.bass_utils import run_bass_kernel_spmd

    nc = bacc.Bacc("TRN2", target_bir_lowering=False, num_devices=1)
    arrays = _laid_out({n: np.asarray(v) for n, v in inputs.items()})
    a = {n: nc.dram_tensor(f"in_{n}", v.shape, mybir.dt.from_np(v.dtype), kind="ExternalInput").ap()
         for n, v in arrays.items()}
    out = nc.dram_tensor("out", (B, C, H, W), F32, kind="ExternalOutput").ap()
    conv_stack(nc, a, out)
    r = run_bass_kernel_spmd(nc, [{f"in_{n}": v for n, v in arrays.items()}], core_ids=[0])
    return r.results[0]["out"]
```

```python
from contextlib import ExitStack

import numpy as np

import concourse.bass as bass
from concourse import mybir

F32 = mybir.dt.float32
F16 = mybir.dt.float16
ALU = mybir.AluOpType
ACT = mybir.ActivationFunctionType
AX = mybir.AxisListType

P = 128
B, C, H, W = 4, 128, 256, 256
NPIX = H * W
GROUPS = 32
PER_GROUP = C // GROUPS
GROUP_PIX = PER_GROUP * NPIX
KX, KY = 64, 33
K0 = 32
RI = 2 * KY
HT = H // P
WT = W // P
EPS_GN = 1e-5
N_SSM = 64
STEP = 16
LAGS = 2 * H
HEADS_L3 = 8
SUB, SUB0 = 4, 2
EPS_ATT = 1e-6
QUADS = C // 4
TWO_PI = 2 * np.pi
ROUND = 1.5 * 2.0 ** 23

TINY = 1e-30
NORM_SCALE = 64.0
KERNEL_SCALE = 2.0 ** 14
FIELD_SCALE = 2.0 ** 15
TABLE_SCALE = 2.0 ** 10
"""Where float32 products dominate, an operand known to lie in [-2**15, 2**15] is split into two
float16 parts, high and low, of together 22 bits; high x high + high x low + low x high in float32
sums stands for the float32 product at three passes instead of four. Group norms bound what they
give by sqrt(the group's size) = 512, a kernel is scaled by its maximum, and modes by their sum of
magnitudes."""
PRODUCTS = ((0, 0), (0, 1), (1, 0))


def constants():
    h = np.arange(H)
    kx, ky = np.arange(KX), np.arange(KY)
    tx = TWO_PI * ((h[:, None] * kx[None, :]) % H) / H
    ty = TWO_PI * ((h[:, None] * ky[None, :]) % W) / W
    dft_x = np.concatenate([np.cos(tx), -np.sin(tx)], 1).reshape(HT, P, 2 * KX).transpose(1, 0, 2)
    from_re = np.concatenate([np.cos(ty), -np.sin(ty)], 1)
    from_im = np.concatenate([np.sin(ty), np.cos(ty)], 1)
    dft_y = np.stack([from_re, from_im], 1).reshape(WT, P, 2, RI).transpose(1, 0, 2, 3)
    c = np.arange(P)
    same_group = (c[:, None] // PER_GROUP == c[None, :] // PER_GROUP) * 1.0
    same_head = (c[:, None] // (C // HEADS_L3) == c[None, :] // (C // HEADS_L3)) * 1.0
    powers = np.arange(STEP)
    hermitian = np.ones((KX, 2, KY))
    hermitian[1:, :, 0] = 0.5
    hermitian[0, 1, 0] = 0.0
    rows = lambda a: np.broadcast_to(a.reshape(1, -1), (P, a.size))
    parts = {
        "dft_x": dft_x, "dft_y": dft_y, "same_group": same_group,
        "same_head": same_head, "ident": np.eye(P), "ones": np.ones((P, P)), "fine": rows(powers),
        "coarse": rows(STEP * powers), "hermitian": rows(hermitian),
    }
    where, at = {}, 0
    for name, a in parts.items():
        n = a.reshape(P, -1).shape[1]
        where[name] = (at, n)
        at += n
    table = np.concatenate([a.reshape(P, -1) for a in parts.values()], 1).astype(np.float32)
    return np.ascontiguousarray(table), where


def inverse_tables():
    ty = TWO_PI * np.outer(np.arange(KY), np.arange(W)) / W
    tx = TWO_PI * np.outer(np.arange(KX), np.arange(H)) / H
    by_ky = np.zeros((P, 2 * W))
    by_ky[:RI] = np.block([[np.cos(ty), np.sin(ty)], [-np.sin(ty), np.cos(ty)]])
    by_kx = np.concatenate([np.cos(tx), -np.sin(tx)], 0)
    both = TABLE_SCALE * np.concatenate([by_ky, by_kx], 1)
    high = both.astype(np.float16)
    return np.ascontiguousarray(np.stack([high, (both - high).astype(np.float16)], 1))


def chained(eng, sem, start=0):
    count = [start]

    def link(ins):
        count[0] += 1
        ins.then_inc(sem, 1)
        eng.wait_ge(sem, count[0])

    return link


AHEAD = 8
"""In the pipelined parts a counting semaphore starts at AHEAD, so that a wait for "item n minus the
buffers" is never against a value below one."""


def start(eng, *sems):
    for s in sems:
        eng.sem_inc(s, AHEAD)


def done(n):
    return n + (1 + AHEAD)


def reusable(n, buffers):
    assert buffers <= AHEAD
    return n + (1 + AHEAD - buffers)


def side_by_side(eng, turns, per_turn, steps):
    for n in range(-max(lead for lead, _ in steps), 0):
        for lead, step in steps:
            if n + lead >= 0:
                step(0, n + lead)
    with eng.Fori(0, turns - 1) as i:
        for k in range(per_turn):
            for lead, step in steps:
                step(i + (k + lead) // per_turn, (k + lead) % per_turn)
    for k in range(per_turn):
        for lead, step in steps:
            if k + lead < per_turn:
                step(turns - 1, k + lead)


def ssm_kernels(nc, sem, a, rev):
    with ExitStack() as ctx:
        def sb(name, shape):
            return ctx.enter_context(nc.sbuf_tensor(name, shape, F32))

        _, where = constants()
        f0, fn = where["fine"]
        c0, cn = where["coarse"]
        par = sb("ssm_par", [P, 7, P])
        dt_log, a_re, a_im = par[:, 0, :], par[:, 1, :], par[:, 2, :]
        c_re, c_im = par[:, 3:5, :], par[:, 5:7, :]
        fine, coarse = sb("fine", [P, STEP]), sb("coarse", [P, STEP])
        tmp = [sb(f"ssm_tmp{j}", [P, P]) for j in range(12)]
        dt, dre, dim, mag, cyc, rnd, cs, sn, er, ei, inv, q_i = tmp
        q_r = sb("ssm_qr", [P, P])
        k_re, k_im, k_t = (sb(n, [P, 2, P]) for n in ("ssm_kre", "ssm_kim", "ssm_kt"))
        k_neg = sb("ssm_kneg", [P, 2, P])
        wide, full = [P, P, STEP], [P, P, 2 * STEP]
        mags, cycs, rnds, rests = (
            [sb(f"ssm_{n}s{j}", wide) for j in range(2)] for n in ("mag", "cyc", "rnd", "rest"))
        sins, coss = cycs, rnds
        f_re, f_im, p_re, p_im = (sb(f"ssm_{n}", full) for n in ("fre", "fim", "pre", "pim"))
        kk = sb("ssm_kk", [2 * STEP, 2, P, 2 * STEP])
        ps = [ctx.enter_context(nc.psum_tensor(f"ssm_ps{j}", [2 * STEP, STEP, 2 * STEP], F32)) for j in range(4)]
        loaded, dve, pool, act, put = (sem(f"ssm_{n}") for n in ("loaded", "dve", "pool", "act", "put"))
        ready, summed, kept = [sem(f"ssm_ready{j}") for j in range(2)], sem("ssm_summed"), sem("ssm_kept")
        block = ctx.enter_context(nc.Block())
        n_blocks = 2 * P // STEP
        HALF = P // 2
        blocks = [(axis, h) for first in range(0, P, HALF) for axis in range(2)
                  for h in range(first, first + HALF, STEP)]

        @block.sync
        def _(sp):
            sp.dma_start(fine[:], a["table"][:, f0:f0 + fn]).then_inc(loaded, 16)
            sp.dma_start(coarse[:], a["table"][:, c0:c0 + cn]).then_inc(loaded, 16)
            for axis in range(2):
                s = slice(N_SSM * axis, N_SSM * (axis + 1))
                row = a[f"log_dt{axis}"].rearrange("(o h) -> o h", o=1).broadcast_to([N_SSM, P])
                sp.dma_start(par[s, 0, :], row).then_inc(loaded, 16)
                sp.dma_start(par[s, 1, :], a[f"A_re{axis}"]).then_inc(loaded, 16)
                sp.dma_start(par[s, 2, :], a[f"A_im{axis}"]).then_inc(loaded, 16)
                sp.dma_start(par[s, 3:5, :], a[f"C_re{axis}"]).then_inc(loaded, 16)
                sp.dma_start(par[s, 5:7, :], a[f"C_im{axis}"]).then_inc(loaded, 16)
            sp.wait_ge(kept, n_blocks)
            for axis in range(2):
                for way in range(2):
                    s = slice(STEP * way, STEP * (way + 1))
                    sp.dma_start(rev[axis, :, H * way:H * (way + 1)].rearrange("h (a b) -> a h b", b=STEP),
                                 kk[s, axis, :, s]).then_inc(put, 16)
            sp.wait_ge(put, 16 * 4)

        SMALL, TABLES, K_STEPS = 9, 14, 22
        SN_DONE, F_DONE, G_DONE = 6, 8, 10

        @block.scalar
        def _(sc):
            def fn(ready, at, out, x, func, scale=1.0):
                sc.wait_ge(ready, at)
                nc.scalar.activation(out, x, func, scale=scale).then_inc(act, 1)

            flat = lambda t: t[:].rearrange("p h j -> p (h j)")
            fn(loaded, 16 * 12, dt[:], dt_log, ACT.Exp)
            fn(dve, 2, mag[:], dre[:], ACT.Exp)
            fn(dve, SMALL + 1, flat(mags[0]), flat(mags[0]), ACT.Exp)
            fn(pool, 1, flat(mags[1]), flat(mags[1]), ACT.Exp)
            fn(dve, 7, sn[:], cyc[:], ACT.Sin, TWO_PI)
            fn(dve, 9, cs[:], rnd[:], ACT.Sin, TWO_PI)
            for n, base in ((0, SMALL + 2), (1, SMALL + 8)):
                fn(dve, base + 4, flat(sins[n]), flat(cycs[n]), ACT.Sin, TWO_PI)
                fn(dve, base + 6, flat(coss[n]), flat(rnds[n]), ACT.Sin, TWO_PI)
            for n, (axis, h0) in enumerate(blocks):
                sc.wait_ge(summed, n + 1)
                nc.scalar.activation(kk[:, axis, h0:h0 + STEP, :], ps[n % 4][:], ACT.Copy, scale=2.0).then_inc(kept, 1)

        def arguments(eng, link, n, table):
            j = table[:].unsqueeze(1).broadcast_to(wide)
            link(eng.tensor_tensor(mags[n][:], dre[:].unsqueeze(2).broadcast_to(wide), j, ALU.mult))
            link(eng.tensor_tensor(cycs[n][:], dim[:].unsqueeze(2).broadcast_to(wide), j, ALU.mult))

        def cycles(link, c, r, t):
            tt, ts = nc.vector.tensor_tensor, nc.vector.tensor_scalar
            link(ts(r, c, 1 / TWO_PI, None, ALU.mult))
            link(ts(t, r, ROUND, ROUND, ALU.add, ALU.subtract))
            link(tt(c, r, t, ALU.subtract))
            link(ts(r, c, 0.25, None, ALU.add))
            link(ts(t, r, ROUND, ROUND, ALU.add, ALU.subtract))
            link(tt(r, r, t, ALU.subtract))

        def weigh(eng, link, n, way, g_re, g_im):
            tt = eng.tensor_tensor
            s = slice(STEP * way, STEP * (way + 1))
            for half in range(2):
                h = slice(HALF * half, HALF * (half + 1))
                kr, ki, kn = (t[:, way, h].unsqueeze(2).broadcast_to([P, HALF, STEP]) for t in (k_re, k_im, k_neg))
                gr, gi, re, im, t = g_re[:, h], g_im[:, h], p_re[:, h, s], p_im[:, h, s], rests[n][:, h]
                link(tt(re, gr, kr, ALU.mult))
                link(tt(t, gi, ki, ALU.mult))
                link(tt(re, re, t, ALU.subtract))
                link(tt(im, gr, kn, ALU.mult))
                link(tt(t, gi, kr, ALU.mult))
                tt(im, im, t, ALU.subtract).then_inc(ready[n], 1)

        @block.gpsimd
        def _(po):
            link = chained(po, pool)
            po.wait_ge(dve, 2)
            arguments(nc.gpsimd, link, 1, coarse)
            po.wait_ge(act, G_DONE)
            link(nc.gpsimd.tensor_tensor(coss[1][:], coss[1][:], mags[1][:], ALU.mult))
            link(nc.gpsimd.tensor_tensor(sins[1][:], sins[1][:], mags[1][:], ALU.mult))
            po.wait_ge(dve, SMALL + TABLES + K_STEPS)
            weigh(nc.gpsimd, link, 1, 1, coss[1], sins[1])

        @block.vector
        def _(ve):
            link = chained(ve, dve)
            tt, ts = nc.vector.tensor_tensor, nc.vector.tensor_scalar
            ve.wait_ge(loaded, 16 * 12)
            ve.wait_ge(act, 1)
            link(tt(dre[:], dt[:], a_re, ALU.mult))
            link(tt(dim[:], dt[:], a_im, ALU.mult))
            link(nc.vector.tensor_copy(cyc[:], dim[:]))
            cycles(link, cyc[:], rnd[:], er[:])
            arguments(nc.vector, link, 0, fine)
            cycles(link, cycs[0][:], rnds[0][:], rests[0][:])
            ve.wait_ge(pool, 2)
            cycles(link, cycs[1][:], rnds[1][:], rests[1][:])
            ve.wait_ge(act, SN_DONE)
            link(tt(er[:], mag[:], cs[:], ALU.mult))
            link(ts(er[:], er[:], 1.0, None, ALU.subtract))
            link(tt(ei[:], mag[:], sn[:], ALU.mult))
            link(tt(inv[:], a_re, a_re, ALU.mult))
            link(tt(rnd[:], a_im, a_im, ALU.mult))
            link(tt(inv[:], inv[:], rnd[:], ALU.add))
            link(nc.vector.reciprocal(inv[:], inv[:]))
            link(tt(q_r[:], er[:], a_re, ALU.mult))
            link(tt(rnd[:], ei[:], a_im, ALU.mult))
            link(tt(q_r[:], q_r[:], rnd[:], ALU.add))
            link(tt(q_r[:], q_r[:], inv[:], ALU.mult))
            link(tt(q_i[:], ei[:], a_re, ALU.mult))
            link(tt(rnd[:], er[:], a_im, ALU.mult))
            link(tt(q_i[:], q_i[:], rnd[:], ALU.subtract))
            link(tt(q_i[:], q_i[:], inv[:], ALU.mult))
            two = [P, 2, P]
            qr2, qi2 = q_r[:].unsqueeze(1).broadcast_to(two), q_i[:].unsqueeze(1).broadcast_to(two)
            link(tt(k_re[:], c_re, qr2, ALU.mult))
            link(tt(k_t[:], c_im, qi2, ALU.mult))
            link(tt(k_re[:], k_re[:], k_t[:], ALU.subtract))
            link(tt(k_im[:], c_re, qi2, ALU.mult))
            link(tt(k_t[:], c_im, qr2, ALU.mult))
            link(tt(k_im[:], k_im[:], k_t[:], ALU.add))
            link(ts(k_neg[:], k_im[:], -1.0, None, ALU.mult))
            ve.wait_ge(act, F_DONE)
            for out, x in ((f_re, coss[0]), (f_im, sins[0])):
                link(tt(out[:, :, 0:STEP], x[:, :, ::-1], mags[0][:, :, ::-1], ALU.mult))
                link(tt(out[:, :, STEP:], x[:], mags[0][:], ALU.mult))
            ve.wait_ge(pool, 4)
            weigh(nc.vector, link, 0, 0, coss[1][:, :, ::-1], sins[1][:, :, ::-1])

        @block.tensor
        def _(pe):
            for n, (axis, h0) in enumerate(blocks):
                s = slice(N_SSM * axis, N_SSM * (axis + 1))
                if n % (len(blocks) // 2) == 0:
                    for r in ready:
                        pe.wait_ge(r, n // (len(blocks) // 2) + 1)
                if n >= 4:
                    pe.wait_ge(kept, n - 3)
                for j in range(STEP):
                    nc.tensor.matmul(ps[n % 4][:, j, :], p_re[s, h0 + j, :], f_re[s, h0 + j, :], start=True, stop=False)
                    last = nc.tensor.matmul(ps[n % 4][:, j, :], p_im[s, h0 + j, :], f_im[s, h0 + j, :],
                                            start=False, stop=True)
                last.then_inc(summed, 1)


def spectrum(nc, sem, x, spec, squares, a):
    with ExitStack() as ctx:
        def sb(name, shape):
            return ctx.enter_context(nc.sbuf_tensor(name, shape, F32))

        _, where = constants()
        (x0, xn), (y0, yn) = where["dft_x"], where["dft_y"]
        NX = 4
        quads = [sb(f"quad{j}", [P, HT, 4, P]) for j in range(NX)]
        half = sb("half", [P, C, 2 * KX])
        dft_x = sb("dft_x", [P, HT, 2 * KX])
        dft_y = sb("dft_y", [P, WT, 2, RI])
        junk = [sb(f"square_junk{j}", [P, HT * 4 * P]) for j in range(2)]
        sums = sb("square_sums", [P, NX])
        ps1 = [ctx.enter_context(nc.psum_tensor(f"half_ps{j}", [P, 4, 2 * KX], F32)) for j in range(4)]
        ps2 = [ctx.enter_context(nc.psum_tensor(f"spec_ps{j}", [P, 4, RI], F32)) for j in range(4)]
        tables, loaded = sem("dft_tables"), [sem(f"quad_loaded{j}") for j in range(NX)]
        halved, half_kept, squared = sem("halved"), sem("half_kept"), sem("squared")
        modes, modes_kept, sums_kept = sem("modes"), sem("modes_kept"), sem("sums_kept")
        block = ctx.enter_context(nc.Block())
        turns = QUADS // NX
        kgroups = KX // 4

        def quad_of(b, wt, i, j):
            return (b * WT + wt) * QUADS + i * NX + j

        @block.sync
        def _(sp):
            sp.dma_start(dft_x[:], a["table"][:, x0:x0 + xn].rearrange("p (t k) -> p t k", t=HT)).then_inc(tables, 16)
            sp.dma_start(dft_y[:], a["table"][:, y0:y0 + yn].rearrange("p (t i k) -> p t i k", t=WT, i=2))\
                .then_inc(tables, 16)
            with sp.Fori(0, B) as b:
                for wt in range(WT):
                    with sp.Fori(0, turns) as i:
                        for j in range(NX):
                            sp.wait_ge(halved, reusable(quad_of(b, wt, i, j), NX))
                            sp.wait_ge(squared, reusable(quad_of(b, wt, i, j), NX))
                            for t in range(HT):
                                src = x[bass.ds(b, 1), bass.ds(i * (4 * NX) + 4 * j, 4), P * t:P * (t + 1),
                                        P * wt:P * (wt + 1)]
                                sp.dma_start(quads[j][:, t], src.rearrange("o c h w -> h (o c) w"))\
                                    .then_inc(loaded[j], 16)

        @block.tensor
        def _(pe):
            start(pe, halved, modes)
            pe.wait_ge(tables, 32)
            with pe.Fori(0, B) as b:
                for wt in range(WT):
                    with pe.Fori(0, turns) as i:
                        for j in range(NX):
                            pe.wait_ge(loaded[j], ((b * WT + wt) * turns + i) * (16 * HT) + 16 * HT)
                            pe.wait_ge(half_kept, reusable(quad_of(b, wt, i, j), 4))
                            for c in range(4):
                                for t in range(HT):
                                    last = nc.tensor.matmul(ps1[j][:, c, :], quads[j][:, t, c, :], dft_x[:, t, :],
                                                            start=t == 0, stop=t == HT - 1)
                            last.then_inc(halved, 1)
                    pe.wait_ge(half_kept, done(quad_of(b, wt, 0, QUADS - 1)))
                    for g in range(kgroups):
                        pe.wait_ge(modes_kept, reusable((b * WT + wt) * kgroups + g, 4))
                        for k in range(4):
                            for ri in range(2):
                                last = nc.tensor.matmul(ps2[g % 4][:, k, :], half[:, :, KX * ri + 4 * g + k],
                                                        dft_y[:, wt, ri, :], start=ri == 0, stop=ri == 1)
                        last.then_inc(modes, 1)

        @block.scalar
        def _(sc):
            start(sc, half_kept)
            with sc.Fori(0, B) as b:
                for wt in range(WT):
                    sc.wait_ge(modes, reusable((b * WT + wt) * kgroups, 1))
                    with sc.Fori(0, turns) as i:
                        for j in range(NX):
                            sc.wait_ge(halved, done(quad_of(b, wt, i, j)))
                            nc.scalar.activation(half[:, bass.ds(i * (4 * NX) + 4 * j, 4), :], ps1[j][:], ACT.Copy)\
                                .then_inc(half_kept, 1)

        @block.vector
        def _(ve):
            start(ve, squared, modes_kept)
            with ve.Fori(0, B) as b:
                for wt in range(WT):
                    with ve.Fori(0, turns) as i:
                        for j in range(NX):
                            q = quads[j][:].rearrange("p t c w -> p (t c w)")
                            ve.wait_ge(loaded[j], ((b * WT + wt) * turns + i) * (16 * HT) + 16 * HT)
                            ve.wait_ge(squared, reusable(quad_of(b, wt, i, j), 2))
                            nc.vector.tensor_tensor_reduce(junk[j % 2][:], q, q, 1.0, 0.0, ALU.mult, ALU.add,
                                                           sums[:, j:j + 1]).then_inc(squared, 1)
                        ve.wait_ge(squared, done(quad_of(b, wt, i, NX - 1)))
                        nc.vector.tensor_scalar(
                            squares[:, bass.ds(b, 1), wt, bass.ds(i * NX, NX)].rearrange("p o g -> p (o g)"), sums[:],
                            1.0, None, ALU.mult).then_inc(sums_kept, 1)
                        ve.wait_ge(sums_kept, (b * WT + wt) * turns + i + 1)
                    for g in range(kgroups):
                        ve.wait_ge(modes, done((b * WT + wt) * kgroups + g))
                        out = spec[:, bass.ds(b, 1), 4 * g:4 * g + 4, :].rearrange("p o k r -> p (o k) r")
                        if wt == 0:
                            nc.vector.tensor_scalar(out, ps2[g % 4][:], 1.0, None, ALU.mult).then_inc(modes_kept, 1)
                        else:
                            ve.wait_ge(modes_kept, reusable((b * WT + wt) * kgroups + g, 4))
                            nc.vector.tensor_tensor(out, ps2[g % 4][:], out, ALU.add).then_inc(modes_kept, 1)


def norm_moments(nc, sem, name, products, before, after, small, scale=1.0 / NPIX):
    with ExitStack() as ctx:
        ps = ctx.enter_context(nc.psum_tensor(f"{name}_ps", [P, 2, B], F32))
        steps, summed, rooted, var_ready, pair_ready = (sem(f"{name}_{n}") for n in ("steps", "summed", "rooted", "var", "pair"))
        block = ctx.enter_context(nc.Block())

        @block.vector
        def _(ve):
            link = chained(ve, steps)
            tt, ts = nc.vector.tensor_tensor, nc.vector.tensor_scalar
            before(link)
            nc.vector.memset(small["u"], 0.0).then_inc(pair_ready, 1)
            ve.wait_ge(summed, 1)
            link(nc.vector.scalar_tensor_tensor(out=small["q"], in0=ps[:, 0, :], scalar=scale, in1=small["q"],
                                                op0=ALU.mult, op1=ALU.add))
            link(ts(small["mean"], ps[:, 1, :], 1.0 / GROUP_PIX, None, ALU.mult))
            link(tt(small["t"], small["mean"], small["mean"], ALU.mult))
            link(nc.vector.scalar_tensor_tensor(out=small["q"], in0=small["t"], scalar=-float(GROUP_PIX), in1=small["q"],
                                                op0=ALU.mult, op1=ALU.add))
            ts(small["t"], small["q"], 1.0 / GROUP_PIX, EPS_GN, ALU.mult, ALU.add).then_inc(var_ready, 1)
            ve.wait_ge(rooted, 1)
            link(nc.vector.reciprocal(small["inv"], small["u"]))
            after(link)

        @block.scalar
        def _(sc):
            sc.wait_ge(var_ready, 1)
            nc.scalar.activation(small["u"], small["t"], ACT.Sqrt).then_inc(rooted, 1)

        @block.tensor
        def _(pe):
            pe.wait_ge(pair_ready, 1)
            products(ps).then_inc(summed, 1)


def low_part(spec, b):
    return spec[:, b, 0:K0, :].rearrange("p k (r y) -> p k r y", r=2)[:, :, :, 0:K0]


def layer0_products(nc, sem, a, spec, inv, low, fc_w, herm, change):
    with ExitStack() as ctx:
        def sb(name, shape):
            return ctx.enter_context(nc.sbuf_tensor(name, shape, F32))

        ROWS, LOADS, PACK, G, Q = 2, 4, 4, K0 // 4, 32
        w0 = [sb(f"w0_row{j}", [P, PACK, G, P]) for j in range(LOADS)]
        packed = [sb(f"packed{j}", [P, PACK, G, Q]) for j in range(ROWS)]
        turned = [sb(f"turned0_{j}", [Q, G, P // Q, PACK, B, 2]) for j in range(ROWS)]
        twice = sb("layer0_twice", [P, B, 2, K0])
        ps = [[ctx.enter_context(nc.psum_tensor(f"mix0_ps{j}{t}", [Q, G // 2, P], F32)) for t in range(2)]
              for j in range(ROWS)]
        ps_fc = [ctx.enter_context(nc.psum_tensor(f"fc_ps{j}", [P, B, 2, K0], F32)) for j in range(ROWS)]
        loaded = [sem(f"w0_loaded{j}") for j in range(LOADS)]
        zeroed, staged, mixed, back, kept, projected, steps = (
            sem(f"mix0_{n}") for n in ("zeroed", "staged", "mixed", "turned", "kept", "projected", "steps"))
        block = ctx.enter_context(nc.Block())
        STEPS = 6

        def row_of(t, k):
            return t[:, :, bass.ds(k, 1)].rearrange("p b o r y -> p b (o r) y")

        spec_ri = spec.rearrange("p b k (r y) -> p b k r y", r=2)

        @block.sync
        def _(sp):
            with sp.Fori(0, K0 // LOADS) as i:
                for j in range(LOADS):
                    sp.wait_ge(mixed, reusable(i * LOADS + j, LOADS))
                    src = a["w0"][bass.ds(i * LOADS + j, 1)].rearrange("m c n o -> c (m n) o")
                    sp.dma_start(w0[j][:].rearrange("p j g o -> p (j g) o"), src).then_inc(loaded[j], 16)

        @block.gpsimd
        def _(po):
            for j in range(ROWS):
                nc.gpsimd.memset(packed[j][:], 0.0).then_inc(zeroed, 1)
            po.wait_ge(zeroed, ROWS)
            start(po, staged)
            with po.Fori(0, K0 // ROWS) as i:
                for j in range(ROWS):
                    po.wait_ge(mixed, reusable(i * ROWS + j, ROWS))
                    row = row_of(spec_ri, i * ROWS + j)
                    for n in range(PACK):
                        last = nc.gpsimd.tensor_tensor(
                            packed[j][:, n, :, 8 * n:8 * (n + 1)].rearrange("p g (b r) -> p b r g", r=2),
                            row[:, :, :, G * n:G * (n + 1)], inv.unsqueeze(2).unsqueeze(3).broadcast_to([P, B, 2, G]),
                            ALU.mult)
                    last.then_inc(staged, 1)

        @block.tensor
        def _(pe):
            start(pe, mixed, projected)

            def mix(n, j):
                buf = j % ROWS
                pe.wait_ge(staged, done(n))
                pe.wait_ge(back, reusable(n, ROWS))
                for g in range(G):
                    out = ps[buf][g // (G // 2)][:, g % (G // 2), :]
                    for m in range(PACK):
                        last = nc.tensor.matmul(out, packed[buf][:, m, g, :], w0[j][:, m, g, :], start=m == 0,
                                                stop=m == PACK - 1)
                last.then_inc(mixed, 1)

            def project(n, j):
                pe.wait_ge(kept, done(n))
                pe.wait_ge(steps, n * STEPS + (AHEAD - (ROWS - 1) * STEPS))
                rhs = low[:, :, bass.ds(n, 1)].rearrange("p b o r y -> p b (o r y)")
                nc.tensor.matmul(ps_fc[j % ROWS][:].rearrange("p b r y -> p b (r y)"), fc_w[:], rhs, start=True, stop=True)\
                    .then_inc(projected, 1)

            pe.wait_ge(loaded[0], 16)
            mix(0, 0)
            with pe.Fori(0, K0 // LOADS - 1) as i:
                for j in range(LOADS):
                    ahead = (j + 1) % LOADS
                    pe.wait_ge(loaded[ahead], i * 16 + (16 if ahead else 32))
                    mix(i * LOADS + j + 1, ahead)
                    project(i * LOADS + j, j)
            for n in range(K0 - LOADS, K0):
                if n + 1 < K0:
                    pe.wait_ge(loaded[(n + 1) % LOADS], 16 * (K0 // LOADS))
                    mix(n + 1, (n + 1) % LOADS)
                project(n, n % LOADS)

        @block.scalar
        def _(sc):
            start(sc, kept)
            with sc.Fori(0, K0 // ROWS) as i:
                for j in range(ROWS):
                    k = i * ROWS + j
                    sc.wait_ge(back, done(k))
                    for q in range(P // Q):
                        s = slice(Q * q, Q * (q + 1))
                        for r in range(2):
                            out = low[s, :, bass.ds(k, 1), r, :].rearrange("p b o (m g) -> p b (o m) g", g=G)
                            last = nc.scalar.copy(out, turned[j][:, :, q, :, :, r].rearrange("p g m b -> p b m g"))
                    last.then_inc(kept, 1)

        @block.vector
        def _(ve):
            tt = nc.vector.tensor_tensor
            start(ve, back, steps)

            def turn_back(k, j):
                ve.wait_ge(mixed, done(k))
                ve.wait_ge(kept, reusable(k, ROWS))
                for t in range(2):
                    half = turned[j][:, G // 2 * t:G // 2 * (t + 1)].rearrange("p g q m b r -> p (g q m b r)")
                    last = nc.vector.transpose(half, ps[j][t][:].rearrange("p g o -> p (g o)"))
                last.then_inc(back, 1)

            def add(k, j):
                def link(ins, n):
                    ins.then_inc(steps, 1)
                    ve.wait_ge(steps, k * STEPS + (AHEAD + n))

                ve.wait_ge(projected, done(k))
                x, h, t = row_of(spec_ri, k)[:, :, :, 0:K0], row_of(low, k), twice[:]
                mask = herm[:, bass.ds(k, 1), :, 0:K0].broadcast_to([P, B, 2, K0])
                link(tt(h, ps_fc[j][:], mask, ALU.mult), 1)
                link(tt(t, x, h, ALU.add), 2)
                link(tt(t, x, t, ALU.add), 3)
                link(tt(t, t, h, ALU.mult), 4)
                link(nc.vector.tensor_reduce(change[:, :, bass.ds(k, 1)], t.rearrange("p b r y -> p b (r y)"), AX.X,
                                             ALU.add), 5)
                link(tt(x, x, h, ALU.add), 6)

            turn_back(0, 0)
            with ve.Fori(0, K0 // ROWS - 1) as i:
                for j in range(ROWS):
                    turn_back(i * ROWS + j + 1, (j + 1) % ROWS)
                    add(i * ROWS + j, j)
            turn_back(K0 - 1, 1)
            add(K0 - 2, 0)
            add(K0 - 1, 1)


def layer1_products(nc, sem, a, spec, inv, neg_inv, herm, change):
    with ExitStack() as ctx:
        def sb(name, shape):
            return ctx.enter_context(nc.sbuf_tensor(name, shape, F32))

        ROWS, HEADS, HC = 2, 4, C // 4
        PARTS, PER_PART = 3, KY // 3
        w = [[sb(f"w1_row{j}{r}", [P, KY, HC]) for r in "ri"] for j in range(ROWS)]
        scaled = [sb(f"scaled{j}", [P, KY, 3, HEADS, B]) for j in range(ROWS)]
        turned = [sb(f"turned{j}", [HC, KY, 2, HEADS, B]) for j in range(ROWS)]
        added = [sb(f"added{j}", [P, B, 2, KY]) for j in range(ROWS)]
        twice = [sb(f"twice{j}", [P, B, RI]) for j in range(ROWS)]
        ps = [[ctx.enter_context(nc.psum_tensor(f"mix1_ps{j}{t}", [HC, PER_PART, HC], F32)) for t in range(PARTS)]
              for j in range(ROWS)]
        loaded = [[sem(f"w1_loaded{j}{r}") for r in "ri"] for j in range(ROWS)]
        zeroed, staged, mixed, steps, back, headed, copied = (
            sem(n) for n in ("scaled_zeroed", "mix1_staged", "mix1_mixed", "mix1_steps", "mix1_turned", "mix1_headed",
                             "mix1_copied"))
        block = ctx.enter_context(nc.Block())
        STEPS = 4

        def row_of(k):
            return spec[:, :, bass.ds(k, 1), :].rearrange("p b o r -> p b (o r)")

        def head(h):
            return slice(HC * h, HC * (h + 1))

        @block.sync
        def _(sp):
            with sp.Fori(0, KX // ROWS) as i:
                for j in range(ROWS):
                    sp.wait_ge(mixed, reusable(i * ROWS + j, ROWS))
                    for r in range(2):
                        src = a["w1_im" if r else "w1_re"][bass.ds(i * ROWS + j, 1)].rearrange("x c y o -> c (x y) o")
                        sp.dma_start(w[j][r][:], src).then_inc(loaded[j][r], 16)

        @block.gpsimd
        def _(po):
            for j in range(ROWS):
                nc.gpsimd.memset(scaled[j][:], 0.0).then_inc(zeroed, 1)
            po.wait_ge(zeroed, ROWS)
            start(po, staged)
            with po.Fori(0, KX // ROWS) as i:
                for j in range(ROWS):
                    po.wait_ge(mixed, reusable(i * ROWS + j, ROWS))
                    for h in range(HEADS):
                        s = head(h)
                        row = row_of(i * ROWS + j)[s]
                        nc.gpsimd.tensor_tensor(
                            scaled[j][s, :, 1:3, h, :].rearrange("p y r b -> p b r y"),
                            row.rearrange("p b (r y) -> p b r y", r=2),
                            inv[s].unsqueeze(2).unsqueeze(3).broadcast_to([HC, B, 2, KY]), ALU.mult)
                        last = nc.gpsimd.tensor_tensor(
                            scaled[j][s, :, 0, h, :].rearrange("p y b -> p b y"), row[:, :, KY:RI],
                            neg_inv[s].unsqueeze(2).broadcast_to([HC, B, KY]), ALU.mult)
                    last.then_inc(staged, 1)

        @block.tensor
        def _(pe):
            start(pe, mixed)
            with pe.Fori(0, KX // ROWS) as i:
                for j in range(ROWS):
                    for r in range(2):
                        pe.wait_ge(loaded[j][r], i * 16 + 16)
                    pe.wait_ge(staged, done(i * ROWS + j))
                    pe.wait_ge(back, reusable(i * ROWS + j, ROWS))
                    for n in range(KY):
                        out = ps[j][n // PER_PART][:, n % PER_PART, :]
                        by_ri = scaled[j][:, n].rearrange("p t h b -> p (t h b)")
                        nc.tensor.matmul(out, by_ri[:, 16:48], w[j][0][:, n, :], start=True, stop=False)
                        last = nc.tensor.matmul(out, by_ri[:, 0:32], w[j][1][:, n, :], start=False, stop=True)
                    last.then_inc(mixed, 1)

        @block.scalar
        def _(sc):
            start(sc, headed, copied)
            with sc.Fori(0, KX // ROWS) as i:
                for j in range(ROWS):
                    k = i * ROWS + j
                    sc.wait_ge(back, done(k))
                    sc.wait_ge(copied, reusable(k, ROWS))
                    for h in range(HEADS):
                        last = nc.scalar.copy(added[j][head(h)].rearrange("p b r y -> p r b y"),
                                              turned[j][:, :, :, h, :].rearrange("p y r b -> p r b y"))
                    last.then_inc(headed, 1)
                    sc.wait_ge(steps, k * STEPS + STEPS)
                    nc.scalar.copy(row_of(k), added[j][:].rearrange("p b r y -> p b (r y)")).then_inc(copied, 1)

        @block.vector
        def _(ve):
            tt = nc.vector.tensor_tensor
            start(ve, back)

            def turn_back(k, j):
                ve.wait_ge(mixed, done(k))
                ve.wait_ge(headed, reusable(k, ROWS))
                for t in range(PARTS):
                    out = turned[j][:, PER_PART * t:PER_PART * (t + 1)].rearrange("p y r h b -> p (y r h b)")
                    last = nc.vector.transpose(out, ps[j][t][:].rearrange("p y o -> p (y o)"))
                last.then_inc(back, 1)

            def sums(k, j):
                def link(ins, n):
                    ins.then_inc(steps, 1)
                    ve.wait_ge(steps, k * STEPS + n)

                ve.wait_ge(headed, done(k))
                flat = added[j][:].rearrange("p b r y -> p b (r y)")
                mask = herm[:, bass.ds(k, 1), :, :].rearrange("p o r y -> p o (r y)").broadcast_to([P, B, RI])
                link(tt(flat, flat, mask, ALU.mult), 1)
                link(nc.vector.scalar_tensor_tensor(out=twice[j][:], in0=row_of(k), scalar=2.0, in1=flat,
                                                    op0=ALU.mult, op1=ALU.add), 2)
                link(tt(twice[j][:], twice[j][:], flat, ALU.mult), 3)
                link(nc.vector.tensor_reduce(change[:, :, bass.ds(k, 1)], twice[j][:], AX.X, ALU.add), 4)

            turn_back(0, 0)
            with ve.Fori(0, KX // ROWS - 1) as i:
                for j in range(ROWS):
                    turn_back(i * ROWS + j + 1, (j + 1) % ROWS)
                    sums(i * ROWS + j, j)
            turn_back(KX - 1, 1)
            sums(KX - 2, 0)
            sums(KX - 1, 1)


def modes_layers(nc, sem, a, spec, squares, small_rows):
    with ExitStack() as ctx:
        def sb(name, shape):
            return ctx.enter_context(nc.sbuf_tensor(name, shape, F32))

        _, where = constants()
        group, ones = sb("same_group", [P, P]), sb("mix_ones", [P, 2])
        herm = sb("hermitian", [P, KX, 2, KY])
        fc_w, bias = sb("fc_w", [P, P]), sb("mode_biases", [P, 3])
        low = sb("low_modes", [P, B, K0, 2, K0])
        change = sb("energy_change", [P, B, KX])
        by_channel = sb("squares_by_channel", [P, B, WT, GROUPS, PER_GROUP])
        names = ("q", "t", "u", "mean", "dc", "added_dc", "fc_dc", "bias_dc", "neg_inv")
        rows = sb("mix_small", [P, len(names), B])
        pair = sb("mix_pair", [P, 2, B])
        small = {n: rows[:, j, :] for j, n in enumerate(names)} | small_rows
        spec_dc = spec[:, :, 0, 0]
        loaded = sem("mode_tables")

        def table(name):
            at, n = where[name]
            return a["table"][:, at:at + n]

        with nc.Block() as block:
            @block.sync
            def _(sp):
                sp.dma_start(group[:], table("same_group")).then_inc(loaded, 16)
                sp.dma_start(ones[:], table("ones")[:, 0:2]).then_inc(loaded, 16)
                sp.dma_start(herm[:], table("hermitian").rearrange("p (k r y) -> p k r y", k=KX, r=2)).then_inc(loaded, 16)
                sp.dma_start(fc_w[:], a["fc_wT"]).then_inc(loaded, 16)
                sp.dma_start(bias[:, 0:1], a["fc_b"].rearrange("(c o) -> c o", o=1)).then_inc(loaded, 16)
                sp.dma_start(bias[:, 1:2], a["bias1"].rearrange("c o t -> c (o t)")).then_inc(loaded, 16)
                sp.dma_start(bias[:, 2:3], a["D"].rearrange("o c -> c o")).then_inc(loaded, 16)
                sp.wait_ge(loaded, 16 * 7)

        tt, ts, stt = nc.vector.tensor_tensor, nc.vector.tensor_scalar, nc.vector.scalar_tensor_tensor

        def products(ps):
            return nc.tensor.matmul(ps[:].rearrange("p t b -> p (t b)"), group[:], pair[:].rearrange("p t b -> p (t b)"),
                                    start=True, stop=True)

        def gather(link, bias_dc, added_dc, rows):
            e, d = pair[:, 0, :], pair[:, 1, :]
            hd, t = small["added_dc"], small["t"]
            link(nc.vector.tensor_copy(hd, added_dc))
            link(nc.vector.tensor_reduce(e, change[:, :, 0:rows], AX.X, ALU.add))
            link(stt(out=t, in0=small["dc"], scalar=2.0, in1=hd, op0=ALU.mult, op1=ALU.add))
            link(tt(t, t, hd, ALU.mult))
            link(tt(e, e, t, ALU.subtract))
            link(tt(hd, hd, bias_dc, ALU.add))
            link(stt(out=t, in0=small["dc"], scalar=2.0, in1=hd, op0=ALU.mult, op1=ALU.add))
            link(tt(t, t, hd, ALU.mult))
            link(stt(out=e, in0=e, scalar=2.0, in1=t, op0=ALU.mult, op1=ALU.add))
            link(tt(d, small["dc"], hd, ALU.add))

        def shift(link):
            link(stt(out=spec_dc, in0=small["mean"], scalar=-float(NPIX), in1=spec_dc, op0=ALU.mult, op1=ALU.add))
            link(nc.vector.tensor_copy(small["dc"], spec_dc))
            link(tt(small["sum"], small["sum"], small["mean"], ALU.add))

        def products0(ps):
            for b in range(B):
                for t in range(WT):
                    nc.tensor.matmul(ps[:, 0, b:b + 1], by_channel[:, b, t, :, :].rearrange("p g n -> p (g n)"),
                                     ones[:, 0:1], start=t == 0, stop=t == WT - 1)
            return nc.tensor.matmul(ps[:, 1, :], group[:], pair[:, 1, :], start=True, stop=True)

        def before0(link):
            for b in range(B):
                link(nc.vector.tensor_copy(by_channel[:, b],
                                           squares[:, b].unsqueeze(3).broadcast_to([P, WT, GROUPS, PER_GROUP])))
            link(nc.vector.memset(small["q"], 0.0))
            link(nc.vector.memset(small["sum"], 0.0))
            link(nc.vector.tensor_copy(pair[:, 1, :], spec_dc))
            link(ts(small["fc_dc"], small["q"], bias[:, 0:1], float(NPIX), ALU.add, ALU.mult))
            link(ts(small["bias_dc"], small["q"], bias[:, 1:2], float(NPIX), ALU.add, ALU.mult))

        def after0(link):
            shift(link)

        norm_moments(nc, sem, "norm0", products0, before0, after0, small, scale=1.0)
        layer0_products(nc, sem, a, spec, small["inv"], low, fc_w, herm, change)

        def before1(link):
            low_dc = low[:, :, 0, 0, 0]
            gather(link, small["fc_dc"], low_dc, K0)
            link(nc.vector.tensor_copy(spec_dc, pair[:, 1, :]))
            link(nc.vector.tensor_copy(low_dc, small["added_dc"]))

        def after1(link):
            shift(link)
            link(ts(small["neg_inv"], small["inv"], -1.0, None, ALU.mult))

        norm_moments(nc, sem, "norm1", products, before1, after1, small)
        layer1_products(nc, sem, a, spec, small["inv"], small["neg_inv"], herm, change)

        def before2(link):
            gather(link, small["bias_dc"], spec_dc, KX)

        def after2(link):
            for b in range(B):
                link(tt(low_part(spec, b), low_part(spec, b), low[:, b], ALU.add))
            link(tt(small["sum"], small["sum"], small["mean"], ALU.add))
            link(tt(spec_dc, spec_dc, small["bias_dc"], ALU.add))
            link(stt(out=spec_dc, in0=small["sum"], scalar=-float(NPIX), in1=spec_dc, op0=ALU.mult, op1=ALU.add))
            link(ts(small["skip"], small["inv"], bias[:, 2:3], 1.0, ALU.mult, ALU.add))
            link(ts(small["inv"], small["inv"], NORM_SCALE, None, ALU.mult))
            link(ts(spec_dc, spec_dc, 0.5, None, ALU.mult))

        norm_moments(nc, sem, "norm2", products, before2, after2, small)


def split_kernels(nc, sem, rev, parts, gains):
    with ExitStack() as ctx:
        def sb(name, shape, dt=F32):
            return ctx.enter_context(nc.sbuf_tensor(name, shape, dt))

        kernels, size = sb("kernels", [P, 2, LAGS]), sb("kernel_size", [P, 2, LAGS])
        two = sb("kernel_halves", [P, 2, 2, LAGS], F16)
        top, total, inv_top = sb("kernel_top", [P, 2]), sb("kernel_total", [P, 2]), sb("kernel_inv_top", [P, 2])
        loaded, steps, sized, put = sem("kernels_in"), sem("kernel_steps"), sem("kernels_sized"), sem("kernel_parts_out")
        block = ctx.enter_context(nc.Block())

        @block.sync
        def _(sp):
            sp.dma_start(kernels[:], rev.rearrange("a h m -> h a m")).then_inc(loaded, 16)
            sp.wait_ge(steps, 13)
            sp.dma_start(parts.rearrange("h p m -> h (p m)"), two[:].rearrange("h a p m -> h (a p m)")).then_inc(put, 16)
            sp.wait_ge(put, 16)

        @block.scalar
        def _(sc):
            sc.wait_ge(loaded, 16)
            nc.scalar.activation(size[:], kernels[:], ACT.Abs).then_inc(sized, 1)

        @block.vector
        def _(ve):
            link = chained(ve, steps)
            ts, stt = nc.vector.tensor_scalar, nc.vector.scalar_tensor_tensor
            ve.wait_ge(sized, 1)
            link(nc.vector.tensor_reduce(top[:], size[:], AX.X, ALU.max))
            link(nc.vector.tensor_reduce(total[:], size[:], AX.X, ALU.add))
            link(ts(top[:], top[:], TINY, None, ALU.max))
            link(ts(total[:], total[:], TINY, None, ALU.max))
            link(nc.vector.reciprocal(inv_top[:], top[:]))
            for axis in range(2):
                r = kernels[:, axis, :]
                link(ts(r, r, inv_top[:, axis:axis + 1], KERNEL_SCALE, ALU.mult, ALU.mult))
                link(nc.vector.tensor_copy(two[:, axis, 0, :], r))
                link(nc.vector.tensor_tensor(two[:, axis, 1, :], r, two[:, axis, 0, :], ALU.subtract))
            link(nc.vector.memset(gains, 0.0))
            link(stt(out=gains[:, 1:2], in0=total[:, 0:1], scalar=1 / (NORM_SCALE * KERNEL_SCALE),
                     in1=top[:, 1:2], op0=ALU.mult, op1=ALU.mult))
            link(nc.vector.reciprocal(total[:, 0:1], total[:, 0:1]))
            link(stt(out=gains[:, 0:1], in0=total[:, 0:1], scalar=1 / KERNEL_SCALE, in1=top[:, 0:1], op0=ALU.mult, op1=ALU.mult))


def modes_to_rows(nc, sem, a, spec, lhs, undo):
    with ExitStack() as ctx:
        def sb(name, shape, dt=F32):
            return ctx.enter_context(nc.sbuf_tensor(name, shape, dt))

        _, where = constants()
        i0, i_n = where["ident"]
        ident, diag = sb("rows_ident", [P, P]), sb("mode_scales", [P, B, P])
        total = sb("mode_totals", [P, B])
        rows = [sb(f"mode_rows{j}", [P, C, 2, 2, KX], F16) for j in range(B // 2)]
        ps = [ctx.enter_context(nc.psum_tensor(f"rows_ps{j}", [P, 4, C], F32)) for j in range(8)]
        table, sized, scales, turned = sem("ident_loaded"), sem("modes_sized"), sem("mode_scales_made"), sem("rows_turned")
        steps, high, kept, stored = sem("scale_steps"), sem("rows_high"), sem("mode_rows_kept"), sem("rows_stored")
        block = ctx.enter_context(nc.Block())
        BANKS = KX // 4

        def part(t, b, n):
            return rows[b // 2][0:RI, :, t, b % 2, 4 * n:4 * n + 4].rearrange("r c k -> r k c")

        @block.sync
        def _(sp):
            sp.dma_start(ident[:], a["table"][:, i0:i0 + i_n]).then_inc(table, 16)
            for pair in range(B // 2):
                sp.wait_ge(kept, BANKS * 2 * (pair + 1))
                sp.dma_start(lhs[pair].rearrange("r c t b k -> r (c t b k)"),
                             rows[pair][0:RI].rearrange("r c t b k -> r (c t b k)")).then_inc(stored, 16)
            sp.wait_ge(stored, 16 * (B // 2))

        @block.tensor
        def _(pe):
            for b in range(B):
                pe.wait_ge(scales, b + 1)
                for n in range(BANKS):
                    m = BANKS * b + n
                    if m >= 8:
                        pe.wait_ge(kept, m - 7)
                    for k in range(4):
                        last = nc.tensor.matmul(ps[m % 8][0:RI, k, :], spec[:, b, 4 * n + k, :], diag[:, b, :],
                                                start=True, stop=True)
                    last.then_inc(turned, 1)

        @block.scalar
        def _(sc):
            for b in range(B):
                unused = rows[-1][:].rearrange("p c t b k -> p (c t b k)").bitcast(F32)[:, 0:KX * RI]
                if b:
                    sc.wait_ge(sized, b)
                nc.scalar.activation(unused, spec[:, b].rearrange("p k r -> p (k r)"), ACT.Abs,
                                     accum_out=total[:, b:b + 1]).then_inc(sized, 1)
            sc.wait_ge(sized, B)
            for b in range(B):
                for n in range(BANKS):
                    sc.wait_ge(turned, BANKS * b + n + 1)
                    nc.scalar.copy(part(0, b, n), ps[(BANKS * b + n) % 8][0:RI]).then_inc(high, 1)

        @block.vector
        def _(ve):
            link = chained(ve, steps)
            ve.wait_ge(table, 16)
            for b in range(B):
                t, s = total[:, b:b + 1], undo[:, b:b + 1]
                ve.wait_ge(sized, b + 1)
                link(nc.vector.tensor_scalar(t, t, TINY, 1 / FIELD_SCALE, ALU.max, ALU.mult))
                link(nc.vector.reciprocal(s, t))
                nc.vector.tensor_scalar(diag[:, b, :], ident[:], s, None, ALU.mult).then_inc(scales, 1)
                ve.wait_ge(scales, b + 1)
                link(nc.vector.tensor_scalar(s, t, 2.0 / (NPIX * TABLE_SCALE), None, ALU.mult))
            for b in range(B):
                for n in range(BANKS):
                    ve.wait_ge(high, BANKS * b + n + 1)
                    nc.vector.tensor_tensor(part(1, b, n), ps[(BANKS * b + n) % 8][0:RI], part(0, b, n), ALU.subtract)\
                        .then_inc(kept, 1)


def spread(nc, sem, a, sources, outs):
    with ExitStack() as ctx:
        _, where = constants()
        tables = ctx.enter_context(nc.sbuf_tensor("spread_tables", [P, 2, P], F32))
        n_all = B * len(sources)
        diag = ctx.enter_context(nc.sbuf_tensor("spread_diag", [P, n_all, P], F32))
        ps = [ctx.enter_context(nc.psum_tensor(f"spread_ps{k}", [P, B, C], F32)) for k in range(len(sources))]
        loaded, made, summed, kept = (sem(f"spread_{n}") for n in ("loaded", "made", "summed", "kept"))
        block = ctx.enter_context(nc.Block())

        @block.sync
        def _(sp):
            for j, n in enumerate(("ident", "ones")):
                at, w = where[n]
                sp.dma_start(tables[:, j, :], a["table"][:, at:at + w]).then_inc(loaded, 16)

        @block.vector
        def _(ve):
            ve.wait_ge(loaded, 32)
            for k, s in enumerate(sources):
                for b in range(B):
                    nc.vector.tensor_scalar(diag[:, B * k + b, :], tables[:, 0, :], s[:, b:b + 1], None, ALU.mult)\
                        .then_inc(made, 1)
            for k, out in enumerate(outs):
                ve.wait_ge(summed, k + 1)
                nc.vector.tensor_copy(out, ps[k][:]).then_inc(kept, 1)

        @block.tensor
        def _(pe):
            pe.wait_ge(made, n_all)
            for k in range(len(sources)):
                for b in range(B):
                    last = nc.tensor.matmul(ps[k][:, b, :], tables[:, 1, :], diag[:, B * k + b, :], start=True, stop=True)
                last.then_inc(summed, 1)


def toeplitz_layer(nc, sem, a, x, lhs, kernel_parts, x3, every, sums):
    with ExitStack() as ctx:
        def sb(name, shape, dt=F32):
            return ctx.enter_context(nc.sbuf_tensor(name, shape, dt))

        def banks(name):
            return [ctx.enter_context(nc.psum_tensor(f"{name}{j}", [P, 2, W], F32)) for j in range(2)]

        inverse = sb("inverse_parts", [P, 2, 2 * W + H], F16)
        inv_y, inv_x = inverse[:, :, 0:2 * W], inverse[:, :, 2 * W:]
        SETS, NIMG = 2, 2 * B
        TURNS = C // SETS
        xin = [sb(f"xin{j}", [P, B, HT, W]) for j in range(SETS)]
        xout = [sb(f"xout{j}", [P, B, HT, W]) for j in range(SETS)]
        toep = [sb(f"toeplitz{j}", [P, 4, LAGS - P], F16) for j in range(SETS)]
        modes = [sb(f"channel_modes{j}", [P, B // 2, 2, 2 * KX], F16) for j in range(SETS)]
        rows = [sb(f"rows{j}", [P, 2, W], F16) for j in range(2)]
        v = [sb(f"v{j}", [P, HT, W]) for j in range(4)]
        v_norm = [sb(f"v_norm{j}", [P, HT, W]) for j in range(2)]
        v_skip = [sb(f"v_skip{j}", [P, HT, W]) for j in range(2)]
        u = [sb(f"u{j}", [P, 2, HT, W], F16) for j in range(2)]
        mid = [sb(f"mid{j}", [P, 2, WT, H], F16) for j in range(2)]
        scalars = [sb(f"channel_scalars{j}", [P, 4 * B]) for j in range(SETS)]
        INV, SKIP, GAIN, UNDO = 0, B, 2 * B, 3 * B
        junk = [sb(f"conv_junk{j}", [P, HT * W]) for j in range(2)]
        acc = sb("conv_acc", [P, 2, NIMG])
        ps_r, ps_f, ps_m, ps_y = (banks(n) for n in ("rows_ps_", "field_ps", "mid_ps", "y_ps"))
        tables = sem("inv_tables")
        modes_in, x_in, toep_in, stored = (
            [sem(f"{n}{j}") for j in range(SETS)] for n in ("modes_in", "x_in", "toep_in", "x3_stored"))
        scalars_in, rows_high, normed, skipped, u_high, u_kept, mid_high = (
            sem(n) for n in ("channel_scalars", "rows_high_kept", "v_normed", "v_skipped", "u_high", "u_kept", "mid_high"))
        rows_made, rows_kept, field_made, v_kept, first, mid_kept, second, x3_kept, squared, sums_kept = (
            sem(n) for n in ("rows_made", "rows_kept", "field_made", "v_kept", "toeplitz1", "mid_kept",
                             "toeplitz2", "x3_kept", "x3_squared", "x3_sums_kept"))
        block = ctx.enter_context(nc.Block())
        hankel = bass.AP(kernel_parts.tensor, kernel_parts.offset, [[4 * LAGS, C], [1, P], [LAGS, 4], [1, LAGS - P]])
        def matrix_rows(j, axis, part, t):
            return toep[j][:, 2 * axis + part, P * t:P * t + H][:, ::-1]

        def image(i, k):
            return i * NIMG + k

        @block.sync
        def _(sp):
            sp.dma_start(inverse[:], a["inverse_tables"]).then_inc(tables, 16)

            def load_modes(i, j):
                src = lhs[:, :, bass.ds(i * SETS + j, 1)].rearrange("p r o t b k -> r p (o t b k)")
                sp.dma_start(modes[j][0:RI].rearrange("r p t k -> r p (t k)"), src).then_inc(modes_in[j], 16)

            def load_x(i, j):
                for b in range(B):
                    src = x[b, bass.ds(i * SETS + j, 1)].rearrange("o (t p) w -> p (o t) w", p=P)
                    sp.dma_start(xin[j][:, b], src).then_inc(x_in[j], 16)

            def load_kernels(i, j):
                sp.dma_start(toep[j][:], hankel[bass.ds(i * SETS + j, 1)].rearrange("o p k j -> p (o k) j"))\
                    .then_inc(toep_in[j], 16)

            def store(i, j):
                sp.wait_ge(x3_kept, done(image(i, B * j + B - 1)))
                for b in range(B):
                    dst = x3[b, bass.ds(i * SETS + j, 1)].rearrange("o (t p) w -> p (o t) w", p=P)
                    sp.dma_start(dst, xout[j][:, b]).then_inc(stored[j], 16)

            for j in range(SETS):
                sp.sem_inc(stored[j], 16 * B)
                load_modes(0, j)
                load_x(0, j)
                load_kernels(0, j)
            with sp.Fori(0, TURNS - 1) as i:
                for j in range(SETS):
                    last = image(i, B * j + B - 1)
                    sp.wait_ge(rows_made, done(last))
                    load_modes(i + 1, j)
                    sp.wait_ge(v_kept, done(last))
                    load_x(i + 1, j)
                    sp.wait_ge(second, done(last))
                    load_kernels(i + 1, j)
                    store(i, j)
            for j in range(SETS):
                store(TURNS - 1, j)
            for j in range(SETS):
                sp.wait_ge(stored[j], 16 * B * (TURNS + 1))

        @block.gpsimd
        def _(po):
            start(po, normed, u_kept, skipped)

            def scaled(i, k, out, which):
                by = scalars[k // B][:, which + k % B:which + k % B + 1].to_broadcast([P, HT * W])
                return nc.gpsimd.tensor_tensor(out[:].rearrange("p t w -> p (t w)"), v[k % 4][:].rearrange("p t w -> p (t w)"),
                                               by, ALU.mult)

            def norm(i, k):
                n = image(i, k)
                po.wait_ge(v_kept, done(n))
                po.wait_ge(u_kept, reusable(n, 2))
                scaled(i, k, v_norm[k % 2], INV).then_inc(normed, 1)

            def low_of_v(i, k):
                n = image(i, k)
                po.wait_ge(normed, done(n))
                po.wait_ge(u_high, done(n))
                nc.gpsimd.tensor_tensor(u[k % 2][:, 1], v_norm[k % 2][:], u[k % 2][:, 0], ALU.subtract).then_inc(u_kept, 1)

            def skip(i, k):
                n = image(i, k)
                po.wait_ge(u_kept, done(n))
                po.wait_ge(x3_kept, reusable(n, 2))
                scaled(i, k, v_skip[k % 2], SKIP).then_inc(skipped, 1)

            side_by_side(po, TURNS, NIMG, [(2, low_of_v), (1, skip), (3, norm)])

        @block.tensor
        def _(pe):
            start(pe, rows_made, field_made, first, second)
            pe.wait_ge(tables, 16)

            def modes_by_ky(i, k):
                if k % 2:
                    return
                j, b, n = k // B, k % B, image(i, k)
                if b == 0:
                    pe.wait_ge(modes_in[j], i * 16 + 16)
                pe.wait_ge(rows_kept, reusable(n, 3))
                for f, g in PRODUCTS:
                    last = nc.tensor.matmul(ps_r[k // 2 % 2][:].rearrange("p r w -> p (r w)"), modes[j][0:RI, b // 2, f, :],
                                            inv_y[0:RI, g, :], start=(f, g) == (0, 0), stop=f == 1)
                last.then_inc(rows_made, 2)

            def modes_by_kx(i, k):
                n = image(i, k)
                pe.wait_ge(rows_kept, done(n))
                pe.wait_ge(v_kept, reusable(n, 2))
                for t in range(HT):
                    for f, g in PRODUCTS:
                        last = nc.tensor.matmul(ps_f[k % 2][:, t, :], inv_x[:, f, P * t:P * (t + 1)], rows[k % 2][:, g, :],
                                                start=(f, g) == (0, 0), stop=f == 1)
                last.then_inc(field_made, 1)

            def along_h(i, k):
                j, n = k // B, image(i, k)
                if k % B == 0:
                    pe.wait_ge(toep_in[j], i * 16 + 16)
                pe.wait_ge(u_kept, done(n))
                pe.wait_ge(mid_kept, reusable(n, 2))
                for m in range(WT):
                    for t in range(HT):
                        for f, g in PRODUCTS:
                            last = nc.tensor.matmul(ps_m[k % 2][:, m, :], u[k % 2][:, f, t, P * m:P * (m + 1)],
                                                    matrix_rows(j, 0, g, t), start=t == 0 and (f, g) == (0, 0),
                                                    stop=t == HT - 1 and f == 1)
                last.then_inc(first, 1)

            def along_w(i, k):
                j, n = k // B, image(i, k)
                pe.wait_ge(mid_kept, done(n))
                pe.wait_ge(x3_kept, reusable(n, 2))
                for m in range(HT):
                    for t in range(WT):
                        for f, g in PRODUCTS:
                            last = nc.tensor.matmul(ps_y[k % 2][:, m, :], mid[k % 2][:, f, t, P * m:P * (m + 1)],
                                                    matrix_rows(j, 1, g, t), start=t == 0 and (f, g) == (0, 0),
                                                    stop=t == WT - 1 and f == 1)
                last.then_inc(second, 1)

            side_by_side(pe, TURNS, NIMG, [(4, modes_by_ky), (1, along_h), (3, modes_by_kx), (0, along_w)])

        @block.scalar
        def _(sc):
            start(sc, rows_high, u_high, mid_high, squared)

            def keep_rows(i, k):
                n = image(i, k)
                sc.wait_ge(rows_made, done(n))
                sc.wait_ge(field_made, reusable(n, 2))
                s = slice(KX * (k % 2), KX * (k % 2 + 1))
                for ri in range(2):
                    last = nc.scalar.activation(rows[k % 2][KX * ri:KX * (ri + 1), 0, :], ps_r[k // 2 % 2][s, ri, :],
                                                ACT.Copy, scale=1 / TABLE_SCALE)
                last.then_inc(rows_high, 1)

            def split_v(i, k):
                n = image(i, k)
                if k % B == 0:
                    sc.wait_ge(scalars_in, done(i * SETS + k // B))
                sc.wait_ge(v_kept, done(n))
                sc.wait_ge(first, reusable(n, 2))
                scale = scalars[k // B][:, INV + k % B:INV + k % B + 1]
                nc.scalar.activation(u[k % 2][:, 0], v[k % 4][:], ACT.Copy, scale=scale).then_inc(u_high, 1)

            def keep_mid(i, k):
                n = image(i, k)
                sc.wait_ge(first, done(n))
                sc.wait_ge(second, reusable(n, 2))
                scale = scalars[k // B][:, GAIN:GAIN + 1]
                nc.scalar.activation(mid[k % 2][:, 0], ps_m[k % 2][:], ACT.Copy, scale=scale).then_inc(mid_high, 1)

            def square(i, k):
                n = image(i, k)
                sc.wait_ge(x3_kept, done(n))
                sc.wait_ge(squared, reusable(n, 2))
                sc.wait_ge(sums_kept, reusable(i * SETS + k // B, SETS))
                nc.scalar.activation(junk[k % 2][:], xout[k // B][:, k % B].rearrange("p t w -> p (t w)"), ACT.Square,
                                     accum_out=acc[:, 1, k:k + 1]).then_inc(squared, 1)

            side_by_side(sc, TURNS, NIMG, [(4, keep_rows), (1, keep_mid), (3, split_v), (0, square)])

        @block.vector
        def _(ve):
            start(ve, rows_kept, scalars_in, v_kept, mid_kept, x3_kept, sums_kept)

            def low_of_rows(i, k):
                ve.wait_ge(rows_high, done(image(i, k)))
                s = slice(KX * (k % 2), KX * (k % 2 + 1))
                for ri in range(2):
                    out = rows[k % 2][KX * ri:KX * (ri + 1)]
                    last = nc.vector.scalar_tensor_tensor(out=out[:, 1, :], in0=ps_r[k // 2 % 2][s, ri, :],
                                                          scalar=1 / TABLE_SCALE, in1=out[:, 0, :], op0=ALU.mult,
                                                          op1=ALU.subtract)
                last.then_inc(rows_kept, 1)

            def add_field(i, k):
                j, b, n = k // B, k % B, image(i, k)
                if b == 0:
                    ve.wait_ge(x3_kept, reusable(n, NIMG - (B - 1)))
                    nc.vector.tensor_scalar(scalars[j][:], every[:, :, :, bass.ds(i * SETS + j, 1)]
                                            .rearrange("p s b o -> p (s b o)"), 1.0, None, ALU.mult)\
                        .then_inc(scalars_in, 1)
                    ve.wait_ge(x_in[j], i * (16 * B) + 16 * B)
                ve.wait_ge(field_made, done(n))
                ve.wait_ge(skipped, reusable(n, 4))
                ve.wait_ge(scalars_in, done(i * SETS + j))
                nc.vector.scalar_tensor_tensor(out=v[k % 4][:], in0=ps_f[k % 2][:], scalar=scalars[j][:, UNDO + b:UNDO + b + 1],
                                               in1=xin[j][:, b], op0=ALU.mult, op1=ALU.add).then_inc(v_kept, 1)

            def low_of_mid(i, k):
                n = image(i, k)
                ve.wait_ge(mid_high, done(n))
                scale = scalars[k // B][:, GAIN:GAIN + 1]
                nc.vector.scalar_tensor_tensor(out=mid[k % 2][:, 1], in0=ps_m[k % 2][:], scalar=scale,
                                               in1=mid[k % 2][:, 0], op0=ALU.mult, op1=ALU.subtract).then_inc(mid_kept, 1)

            def add_up(i, k):
                j, b, n = k // B, k % B, image(i, k)
                if b == 0:
                    ve.wait_ge(stored[j], i * (16 * B) + 16 * B)
                ve.wait_ge(second, done(n))
                ve.wait_ge(sums_kept, reusable(i * SETS + j, SETS))
                ve.wait_ge(skipped, done(n))
                nc.vector.scalar_tensor_tensor(out=xout[j][:, b], in0=ps_y[k % 2][:],
                                               scalar=scalars[j][:, GAIN + 1:GAIN + 2], in1=v_skip[k % 2][:],
                                               op0=ALU.mult, op1=ALU.add, accum_out=acc[:, 0, k:k + 1])\
                    .then_inc(x3_kept, 1)
                if b == B - 1:
                    ve.wait_ge(x3_kept, done(n))
                    ve.wait_ge(squared, done(n))
                    nc.vector.tensor_scalar(sums[:, :, :, bass.ds(i * SETS + j, 1)].rearrange("p s b o -> p s (b o)"),
                                            acc[:, :, B * j:B * (j + 1)], 1.0, None, ALU.mult).then_inc(sums_kept, 1)

            side_by_side(ve, TURNS, NIMG, [(3, add_field), (4, low_of_rows), (1, low_of_mid), (0, add_up)])


def attention_matrices(nc, sem, a, x3, sums, mean_sum, w_q, w_den, w_out, biases):
    with ExitStack() as ctx:
        def sb(name, shape):
            return ctx.enter_context(nc.sbuf_tensor(name, shape, F32))

        _, where = constants()
        masks = sb("att_tables", [P, 2, P])
        weights = sb("att_weights", [P, 4, C])
        vectors = sb("att_vectors", [P, 2])
        kv_row = sb("kv_b_row", [1, 2 * C])
        w_kv, kv_bias = sb("w_kv", [P, B, 2 * C]), sb("kv_bias", [P, B, 2 * C])
        beta_wide = sb("beta_wide", [P, B, P])
        by_group = sb("sums_by_group", [P, 2 * B, GROUPS])
        by_channel = sb("sums_by_channel", [P, 2 * B, GROUPS, PER_GROUP])
        names = ("q", "t", "u", "mean", "inv", "beta")
        rows = sb("att_small", [P, len(names), B])
        small = {n: rows[:, j, :] for j, n in enumerate(names)}
        loaded, summed, kept = (sem(f"att_{n}") for n in ("tables_in", "bias_summed", "bias_kept"))
        ts, tt = nc.vector.tensor_scalar, nc.vector.tensor_tensor
        same_head, ones = masks[:, 0, :], masks[:, 1, :]
        kv_w = weights[:, 1:3, :].rearrange("c t o -> c (t o)")

        with nc.Block() as block:
            @block.sync
            def _(sp):
                for j, n in enumerate(("same_head", "ones")):
                    at, w = where[n]
                    sp.dma_start(masks[:, j, :], a["table"][:, at:at + w]).then_inc(loaded, 16)
                sp.dma_start(weights[:, 0, :], a["q_wT"]).then_inc(loaded, 16)
                sp.dma_start(kv_w, a["kv_wT"]).then_inc(loaded, 16)
                sp.dma_start(weights[:, 3, :], a["proj_wT"]).then_inc(loaded, 16)
                sp.dma_start(vectors[:, 0:1], a["q_b"].rearrange("(c o) -> c o", o=1)).then_inc(loaded, 16)
                sp.dma_start(vectors[:, 1:2], a["proj_b"].rearrange("(c o) -> c o", o=1)).then_inc(loaded, 16)
                sp.dma_start(kv_row[:], a["kv_b"].rearrange("(p o) -> p o", p=1)).then_inc(loaded, 16)
                sp.wait_ge(loaded, 16 * 8)

        def products(ps):
            for s, row in ((1, 0), (0, 1)):
                for b in range(B):
                    last = nc.tensor.matmul(ps[:, row, b:b + 1],
                                            by_channel[:, B * s + b, :, :].rearrange("p g n -> p (g n)"), ones[:, 0:1],
                                            start=True, stop=True)
            return last

        def before(link):
            link(nc.vector.tensor_reduce(by_group[:], sums[:].rearrange("p s b (g n) -> p (s b) g n", n=PER_GROUP),
                                         AX.X, ALU.add))
            link(nc.vector.tensor_copy(by_channel[:], by_group[:].unsqueeze(3).broadcast_to([P, 2 * B, GROUPS, PER_GROUP])))
            link(nc.vector.memset(small["q"], 0.0))

        def after(link):
            link(nc.vector.scalar_tensor_tensor(out=small["beta"], in0=small["mean"], scalar=-1.0, in1=small["inv"],
                                                op0=ALU.mult, op1=ALU.mult))
            link(nc.vector.tensor_copy(beta_wide[:], small["beta"].unsqueeze(2).broadcast_to([P, B, P])))
            for b in range(B):
                link(ts(w_q[:, b, :], weights[:, 0, :], small["inv"][:, b:b + 1], None, ALU.mult))
                link(ts(w_kv[:, b, :], kv_w, small["inv"][:, b:b + 1], None, ALU.mult))
            link(ts(biases[:, 1, :], mean_sum, vectors[:, 1:2], None, ALU.add))

        norm_moments(nc, sem, "norm3", products, before, after, small, scale=1.0)

        with ExitStack() as scope:
            ps_q = scope.enter_context(nc.psum_tensor("q_bias_ps", [P, B], F32))
            ps_kv = [scope.enter_context(nc.psum_tensor(f"kv_bias_ps{j}", [P, 2 * C], F32)) for j in range(2)]
            block = scope.enter_context(nc.Block())

            @block.tensor
            def _(pe):
                nc.tensor.matmul(ps_q[:], weights[:, 0, :], small["beta"], start=True, stop=True).then_inc(summed, 1)
                for b in range(B):
                    if b >= 2:
                        pe.wait_ge(kept, b)
                    nc.tensor.matmul(ps_kv[b % 2][:], beta_wide[:, b, :], kv_w, start=True, stop=False)
                    nc.tensor.matmul(ps_kv[b % 2][:], ones[0:1, :], kv_row[:], start=False, stop=True).then_inc(summed, 1)

            @block.vector
            def _(ve):
                ve.wait_ge(summed, 1)
                ts(biases[:, 0, :], ps_q[:], vectors[:, 0:1], None, ALU.add).then_inc(kept, 1)
                for b in range(B):
                    ve.wait_ge(summed, b + 2)
                    nc.vector.tensor_copy(kv_bias[:, b, :], ps_kv[b % 2][:]).then_inc(kept, 1)

        SIDE = H // SUB
        ROWS, NBUF = 8, 4
        CHUNKS, TILES = SIDE // ROWS, ROWS * SIDE // P
        NT = CHUNKS * TILES
        raw = [sb(f"sample_rows{j}", [P, ROWS, W]) for j in range(NBUF)]
        xs = [sb(f"samples{j}", [P, ROWS * SIDE]) for j in range(NBUF)]
        kv = [sb(f"kv{j}", [P, 2 * C]) for j in range(4)]
        e, r, key = ([sb(f"{n}{j}", [P, C]) for j in range(4)] for n in ("key_exp", "key_relu", "key"))
        kv_masked = sb("kv_masked", [P, C])
        key_sum, zeros = sb("key_sum", [P, C]), sb("key_zeros", [P, C])
        ps_t = [ctx.enter_context(nc.psum_tensor(f"kv_ps{j}", [P, 2 * C], F32)) for j in range(4)]
        ps_kv, ps_k, ps_o = (ctx.enter_context(nc.psum_tensor(n, [P, C], F32)) for n in ("kv_sum_ps", "k_sum_ps", "w_out_ps"))
        rows_in = [sem(f"sample_rows_in{j}") for j in range(NBUF)]
        picked, made, biased, exped, keyed, added, matrices, folded, relued, pooled, zeroed = (
            sem(n) for n in ("samples_picked", "kv_made", "kv_biased", "key_exped", "keys_made", "kv_added",
                             "kv_matrices", "kv_folded", "key_relued", "keys_pooled", "key_zeroed"))
        block = ctx.enter_context(nc.Block())
        sampled = x3.rearrange("b c (r s) w -> b c r s w", s=SUB)

        def tile(i, k):
            return i * NT + k

        @block.sync
        def _(sp):
            with sp.Fori(0, B) as i:
                for n in range(CHUNKS):
                    sp.wait_ge(picked, reusable(i * CHUNKS + n, NBUF))
                    src = sampled[bass.ds(i, 1), :, ROWS * n:ROWS * (n + 1), SUB0, :].rearrange("o c r w -> c (o r) w")
                    sp.dma_start(raw[n % NBUF][:], src).then_inc(rows_in[n % NBUF], 16)

        @block.tensor
        def _(pe):
            start(pe, made, made, added, folded)

            def keys_values(i, k):
                n = tile(i, k)
                pe.wait_ge(picked, done(i * CHUNKS + k // TILES))
                pe.wait_ge(biased, reusable(n, 4))
                nc.tensor.matmul(ps_t[k % 4][:], xs[k // TILES % NBUF][:, P * (k % TILES):P * (k % TILES + 1)],
                                 w_kv[:, bass.ds(i, 1), :].rearrange("p o c -> p (o c)"), start=True, stop=True)\
                    .then_inc(made, 1)

            def sum_up(i, k):
                n = tile(i, k)
                pe.wait_ge(keyed, done(n))
                if k == 0:
                    pe.wait_ge(matrices, reusable(i, 1))
                first, last = k == 0, k == NT - 1
                product = nc.tensor.matmul(ps_kv[:], kv[k % 4][:, C:2 * C], key[k % 4][:], start=first, stop=last)
                if last:
                    pe.wait_ge(pooled, done(n))
                    product = nc.tensor.matmul(ps_k[:], key_sum[:], ones, start=True, stop=True)
                product.then_inc(added, 1)
                if last:
                    pe.wait_ge(matrices, done(i))
                    nc.tensor.matmul(ps_o[:], kv_masked[:], weights[:, 3, :], start=True, stop=True).then_inc(folded, 1)

            side_by_side(pe, B, NT, [(4, keys_values), (0, sum_up)])

        @block.scalar
        def _(sc):
            start(sc, exped, picked)

            def pick(i, k):
                n = k // TILES
                if k % TILES == 0:
                    sc.wait_ge(rows_in[n % NBUF], (i * (CHUNKS // NBUF) + n // NBUF) * 16 + 16)
                    sc.wait_ge(made, done(tile(i, TILES * n + TILES - 1)) + AHEAD - TILES * NBUF)
                    nc.scalar.copy(xs[n % NBUF][:].rearrange("p (r s) -> p r s", r=ROWS),
                                   raw[n % NBUF][:, :, SUB0::SUB]).then_inc(picked, 1)

            def exponentials(i, k):
                n = tile(i, k)
                sc.wait_ge(biased, done(n))
                sc.wait_ge(keyed, reusable(n, 4))
                nc.scalar.activation(e[k % 4][:], kv[k % 4][:, 0:C], ACT.Exp).then_inc(exped, 1)

            side_by_side(sc, B, NT, [(8, pick), (1, exponentials)])

        @block.gpsimd
        def _(po):
            start(po, pooled)
            nc.gpsimd.memset(zeros[:], 0.0).then_inc(zeroed, 1)
            po.wait_ge(zeroed, 1)

            def pool_keys(i, k):
                n = tile(i, k)
                po.wait_ge(keyed, done(n))
                if k == 0:
                    po.wait_ge(added, reusable(n, 1))
                else:
                    po.wait_ge(pooled, reusable(n, 1))
                nc.gpsimd.tensor_tensor(key_sum[:], key[k % 4][:], key_sum[:] if k else zeros[:], ALU.add)\
                    .then_inc(pooled, 1)

            side_by_side(po, B, NT, [(0, pool_keys)])

        @block.vector
        def _(ve):
            start(ve, biased, relued, keyed, matrices)

            def add_bias(i, k):
                n = tile(i, k)
                ve.wait_ge(made, done(n) + AHEAD)
                ve.wait_ge(added, reusable(n, 4))
                ve.wait_ge(pooled, reusable(n, 4))
                tt(kv[k % 4][:], ps_t[k % 4][:], kv_bias[:, bass.ds(i, 1), :].rearrange("p o c -> p (o c)"), ALU.add)\
                    .then_inc(biased, 1)

            def relu(i, k):
                n = tile(i, k)
                ve.wait_ge(biased, done(n))
                ve.wait_ge(keyed, reusable(n, 4))
                ts(r[k % 4][:], kv[k % 4][:, 0:C], 0.0, None, ALU.max).then_inc(relued, 1)

            def make_keys(i, k):
                n = tile(i, k)
                ve.wait_ge(exped, done(n))
                ve.wait_ge(relued, done(n))
                nc.vector.scalar_tensor_tensor(out=key[k % 4][:], in0=e[k % 4][:], scalar=1.0, in1=r[k % 4][:],
                                               op0=ALU.min, op1=ALU.add).then_inc(keyed, 1)
                if k == NT - 1:
                    ve.wait_ge(added, done(n))
                    ve.wait_ge(folded, reusable(i, 1))
                    tt(w_den[:, bass.ds(i, 1), :].rearrange("p o c -> p (o c)"), ps_k[:], same_head, ALU.mult)
                    tt(kv_masked[:], ps_kv[:], same_head, ALU.mult).then_inc(matrices, 1)
                    ve.wait_ge(folded, done(i))
                    ts(w_out[:, bass.ds(i, 1), :].rearrange("p o c -> p (o c)"), ps_o[:], 1.0, None, ALU.mult)

            side_by_side(ve, B, NT, [(2, add_bias), (1, relu), (0, make_keys)])


def attend(nc, sem, x3, out, w_q, w_den, w_out, biases):
    with ExitStack() as ctx:
        def sb(name, shape, n):
            return [ctx.enter_context(nc.sbuf_tensor(f"{name}{j}", shape, F32)) for j in range(n)]

        T, SETS, PER = 512, 4, 4
        NT = SETS * PER
        TURNS = NPIX // (T * NT)
        xin, xout = sb("att_in", [P, PER * T], SETS), sb("att_out", [P, PER * T], SETS)
        e, r, q = sb("q_exp", [P, T], 4), sb("q_relu", [P, T], 4), sb("q", [P, T], 4)
        log_den, inv_den, qz = sb("log_den", [P, T], 2), sb("inv_den", [P, T], 2), sb("qz", [P, T], 4)
        eps = sb("att_eps", [P, 1], 1)[0]
        ps_q, ps_d, ps_o = ([ctx.enter_context(nc.psum_tensor(f"{n}{j}", [P, T], F32)) for j in range(2)]
                            for n in ("q_ps", "den_ps", "out_ps"))
        x_in, stored = ([sem(f"{n}{j}") for j in range(SETS)] for n in ("att_x_in", "att_stored"))
        q_made, exped, relued, q_kept, den_made, logged, inverted, scaled, out_made, out_kept, eps_set = (
            sem(f"att_{n}") for n in ("q_made", "q_exped", "q_relued", "q_kept", "den_made", "logged", "inverted", "scaled",
                                      "out_made", "out_kept", "eps_set"))
        block = ctx.enter_context(nc.Block())
        px = PER * T

        def tile(b, i, k):
            return b * (TURNS * NT) + i * NT + k

        @block.sync
        def _(sp):
            for j in range(SETS):
                sp.sem_inc(stored[j], 16)

            def load(b, i, j):
                src = x3[b].rearrange("c h w -> c (h w)")[:, bass.ds(i * (SETS * px) + j * px, px)]
                sp.dma_start(xin[j][:], src).then_inc(x_in[j], 16)

            def store(b, i, j):
                sp.wait_ge(out_kept, done(tile(b, i, PER * j + PER - 1)))
                dst = out[b].rearrange("c h w -> c (h w)")[:, bass.ds(i * (SETS * px) + j * px, px)]
                sp.dma_start(dst, xout[j][:]).then_inc(stored[j], 16)

            for j in range(SETS):
                load(0, 0, j)
            for b in range(B):
                with sp.Fori(0, TURNS - 1) as i:
                    for j in range(SETS):
                        store(b, i, j)
                        load(b, i + 1, j)
                for j in range(SETS):
                    store(b, TURNS - 1, j)
                    if b + 1 < B:
                        load(b + 1, 0, j)
            for j in range(SETS):
                sp.wait_ge(stored[j], 16 + 16 * B * TURNS)

        @block.tensor
        def _(pe):
            start(pe, q_made, den_made, out_made)
            for b in range(B):
                def queries(i, k):
                    if k % PER == 0:
                        pe.wait_ge(x_in[k // PER], (i + b * TURNS) * 16 + 16)
                    pe.wait_ge(relued, reusable(tile(b, i, k), 2))
                    nc.tensor.matmul(ps_q[k % 2][:], w_q[:, b, :], xin[k // PER][:, T * (k % PER):T * (k % PER + 1)],
                                     start=True, stop=True).then_inc(q_made, 1)

                def denominators(i, k):
                    pe.wait_ge(q_kept, done(tile(b, i, k)))
                    pe.wait_ge(logged, reusable(tile(b, i, k), 2))
                    nc.tensor.matmul(ps_d[k % 2][:], w_den[:, b, :], q[k % 4][:], start=True, stop=True)\
                        .then_inc(den_made, 1)

                def outputs(i, k):
                    pe.wait_ge(scaled, done(tile(b, i, k)))
                    pe.wait_ge(out_kept, reusable(tile(b, i, k), 2))
                    nc.tensor.matmul(ps_o[k % 2][:], w_out[:, b, :], qz[k % 4][:], start=True, stop=True)\
                        .then_inc(out_made, 1)

                side_by_side(pe, TURNS, NT, [(6, queries), (4, denominators), (0, outputs)])

        @block.scalar
        def _(sc):
            sc.preload_act_table_set("natural_log_exp_and_others")
            start(sc, exped, logged, inverted)
            sc.wait_ge(eps_set, 1)
            for b in range(B):
                def exponential(i, k):
                    n = tile(b, i, k)
                    sc.wait_ge(q_made, done(n))
                    sc.wait_ge(q_kept, reusable(n, 4))
                    nc.scalar.activation(e[k % 4][:], ps_q[k % 2][:], ACT.Exp, bias=biases[:, 0, b:b + 1]).then_inc(exped, 1)

                def invert(i, k):
                    n = tile(b, i, k)
                    sc.wait_ge(den_made, done(n))
                    sc.wait_ge(inverted, reusable(n, 2))
                    nc.scalar.activation(log_den[k % 2][:], ps_d[k % 2][:], ACT.Ln, bias=eps[:]).then_inc(logged, 1)
                    sc.wait_ge(logged, done(n))
                    sc.wait_ge(scaled, reusable(n, 2))
                    nc.scalar.activation(inv_den[k % 2][:], log_den[k % 2][:], ACT.Exp, scale=-1.0).then_inc(inverted, 1)

                side_by_side(sc, TURNS, NT, [(6, exponential), (4, invert)])

        @block.gpsimd
        def _(po):
            start(po, scaled)
            nc.gpsimd.memset(eps[:], EPS_ATT).then_inc(eps_set, 1)
            for b in range(B):
                def scale(i, k):
                    n = tile(b, i, k)
                    po.wait_ge(inverted, done(n))
                    po.wait_ge(out_made, reusable(n, 4))
                    nc.gpsimd.tensor_tensor(qz[k % 4][:], q[k % 4][:], inv_den[k % 2][:], ALU.mult).then_inc(scaled, 1)

                side_by_side(po, TURNS, NT, [(2, scale)])

        @block.vector
        def _(ve):
            start(ve, relued, q_kept, out_kept)
            for b in range(B):
                def relu(i, k):
                    n = tile(b, i, k)
                    ve.wait_ge(exped, done(n))
                    ve.wait_ge(q_kept, reusable(n, 4))
                    nc.vector.tensor_scalar(r[k % 4][:], ps_q[k % 2][:], biases[:, 0, b:b + 1], 0.0, ALU.add, ALU.max)\
                        .then_inc(relued, 1)

                def finish_map(i, k):
                    n = tile(b, i, k)
                    ve.wait_ge(relued, done(n))
                    ve.wait_ge(scaled, reusable(n, 4))
                    ve.wait_ge(den_made, reusable(n, 4))
                    nc.vector.scalar_tensor_tensor(out=q[k % 4][:], in0=e[k % 4][:], scalar=1.0, in1=r[k % 4][:],
                                                   op0=ALU.min, op1=ALU.add).then_inc(q_kept, 1)

                def add_up(i, k):
                    n, s = tile(b, i, k), slice(T * (k % PER), T * (k % PER + 1))
                    if k % PER == 0:
                        ve.wait_ge(stored[k // PER], (i + b * TURNS) * 16 + 16)
                    ve.wait_ge(out_made, done(n))
                    nc.vector.scalar_tensor_tensor(out=xout[k // PER][:, s], in0=ps_o[k % 2][:],
                                                   scalar=biases[:, 1, b:b + 1], in1=xin[k // PER][:, s],
                                                   op0=ALU.add, op1=ALU.add).then_inc(out_kept, 1)

                side_by_side(ve, TURNS, NT, [(6, relu), (5, finish_map), (0, add_up)])


def conv_stack(nc, a, out):
    with ExitStack() as top:
        def sem(name):
            return top.enter_context(nc.semaphore(name))

        def sb(name, shape):
            return top.enter_context(nc.sbuf_tensor(name, shape, F32))

        def dram(name, shape):
            return nc.dram_tensor(name, shape, F32, kind="Internal").ap()

        x, x3 = a["x"], dram("x3", [B, C, H, W])
        rev, lhs = dram("reversed_kernels", [2, C, LAGS]), nc.dram_tensor("mode_rows_all", [B // 2, RI, C, 2, 2, KX], F16, kind="Internal").ap()
        kernel_parts = nc.dram_tensor("kernel_parts", [C, 4, LAGS], F16, kind="Internal").ap()
        gains, undo = sb("kernel_gains", [P, B]), sb("modes_undo", [P, B])
        rows = sb("norm2_rows", [P, 3, B])
        norm2 = {n: rows[:, j, :] for j, n in enumerate(("sum", "inv", "skip"))}
        sums = sb("x3_sums", [P, 2, B, C])

        ssm_kernels(nc, sem, a, rev)
        split_kernels(nc, sem, rev, kernel_parts, gains[:])
        with nc.sbuf_tensor("modes", [P, B, KX, RI], F32) as spec:
            with nc.sbuf_tensor("x_squares", [P, B, WT, GROUPS], F32) as squares:
                spectrum(nc, sem, x, spec, squares, a)
                modes_layers(nc, sem, a, spec, squares, norm2)
            modes_to_rows(nc, sem, a, spec, lhs, undo[:])
        with nc.sbuf_tensor("norm2_all", [P, 4, B, C], F32) as every:
            spread(nc, sem, a, [norm2["inv"], norm2["skip"], gains[:], undo[:]], [every[:, j] for j in range(4)])
            toeplitz_layer(nc, sem, a, x, lhs, kernel_parts, x3, every, sums)
        w_q, w_den, w_out = sb("w_q", [P, B, C]), sb("w_den", [P, B, C]), sb("w_out", [P, B, C])
        biases = sb("layer3_biases", [P, 2, B])
        attention_matrices(nc, sem, a, x3, sums, norm2["sum"], w_q, w_den, w_out, biases)
        attend(nc, sem, x3, out, w_q, w_den, w_out, biases)


def _laid_out(given):
    def t(name, *axes):
        return np.ascontiguousarray(np.transpose(given[name], axes or None))

    arrays = {
        "x": given["x"], "table": constants()[0], "inverse_tables": inverse_tables(),
        "w0": np.ascontiguousarray(np.transpose(given["L0_conv_weight"][0], (2, 0, 3, 1))),
        "fc_wT": t("L0_conv_fc_w"), "fc_b": given["L0_conv_fc_b"],
        "w1_re": t("L1_conv_weight_real", 3, 0, 1, 4, 2).reshape(KX, C, KY, C // 4),
        "w1_im": t("L1_conv_weight_imag", 3, 0, 1, 4, 2).reshape(KX, C, KY, C // 4),
        "bias1": given["L1_conv_bias"], "D": given["L2_conv_D"],
        "q_wT": t("L3_conv_q_w"), "kv_wT": t("L3_conv_kv_w"), "proj_wT": t("L3_conv_proj_w"),
        "q_b": given["L3_conv_q_b"], "kv_b": given["L3_conv_kv_b"], "proj_b": given["L3_conv_proj_b"],
    }
    for axis in range(2):
        arrays[f"log_dt{axis}"] = given[f"L2_conv_log_dt{axis}"]
        for n in ("A_re", "A_im"):
            arrays[f"{n}{axis}"] = t(f"L2_conv_{n}{axis}")
        for n in ("C_re", "C_im"):
            arrays[f"{n}{axis}"] = t(f"L2_conv_{n}{axis}", 2, 0, 1)
    return {n: np.ascontiguousarray(v) for n, v in arrays.items()}


def kernel(**inputs):
    import concourse.bacc as bacc
    from concourse.bass_utils import run_bass_kernel_spmd

    nc = bacc.Bacc("TRN2", target_bir_lowering=False, num_devices=1)
    arrays = _laid_out({n: np.asarray(v) for n, v in inputs.items()})
    a = {n: nc.dram_tensor(f"in_{n}", v.shape, mybir.dt.from_np(v.dtype), kind="ExternalInput").ap()
         for n, v in arrays.items()}
    out = nc.dram_tensor("out", (B, C, H, W), F32, kind="ExternalOutput").ap()
    conv_stack(nc, a, out)
    r = run_bass_kernel_spmd(nc, [{f"in_{n}": v for n, v in arrays.items()}], core_ids=[0])
    return r.results[0]["out"]
```
